# Optimizing a Trainium2 kernel written in Bass

```python
import numpy as np
import jax
import jax.numpy as jnp

def _softmax(x, axis=-1):
    return jax.nn.softmax(x, axis=axis)

def _gelu(x):
    return jax.nn.gelu(x, approximate=True)

def _silu(x):
    return jax.nn.silu(x)

def _sigmoid(x):
    return jax.nn.sigmoid(x)

def _layernorm(x, axis=-1, eps=1e-05):
    m = jnp.mean(x, axis=axis, keepdims=True)
    v = jnp.var(x, axis=axis, keepdims=True)
    return (x - m) / jnp.sqrt(v + eps)

def _scatter_add(tgt, idx, src, axis=0):
    return tgt.at[idx].add(src)

def _segment_sum(src, seg, n):
    return jax.ops.segment_sum(src, seg, n)
kernel_name = 'mk_prb_d2_jaxref_r8_5b6b00'

def setup_inputs(seed: int=0):
    np.random.seed(seed)
    _w = jnp.asarray

    def _L0_attn_setup():
        import jax, jax.numpy as jnp
        import numpy as np
        LN_EPS = 1e-05
        NEG_INF = -1e+38

        def _layer_norm(x, g, b):
            mu = x.mean(-1, keepdims=True)
            var = ((x - mu) ** 2).mean(-1, keepdims=True)
            return (x - mu) * jax.lax.rsqrt(var + LN_EPS) * g + b

        def _wkv(w, u, k, v):
            B, T, C = k.shape
            kt = jnp.swapaxes(k, 0, 1)
            vt = jnp.swapaxes(v, 0, 1)
            aa0 = jnp.zeros((B, C), k.dtype)
            bb0 = jnp.zeros((B, C), k.dtype)
            pp0 = jnp.full((B, C), NEG_INF, k.dtype)

            def step(carry, inp):
                aa, bb, pp = carry
                kk, vv = inp
                p = jnp.maximum(pp, u + kk)
                e1 = jnp.exp(pp - p)
                e2 = jnp.exp(u + kk - p)
                y = (e1 * aa + e2 * vv) / (e1 + e2)
                p2 = jnp.maximum(pp + w, w + kk)
                e1u = jnp.exp(pp + w - p2)
                e2u = jnp.exp(w + kk - p2)
                aa2 = e1u * aa + e2u * vv
                bb2 = e1u + e2u
                pp2 = p2 + jnp.log(bb2)
                return ((aa2, bb2, pp2), y)
            _, ys = jax.lax.scan(step, (aa0, bb0, pp0), (kt, vt))
            return jnp.swapaxes(ys, 0, 1)

        def _shift(h):
            return jnp.pad(h[:, :-1, :], ((0, 0), (1, 0), (0, 0)))
        key = jax.random.key(seed)
        B, T, C = (8, 256, 128)
        ks = jax.random.split(key, 12)
        s = 0.02
        return {'x': jax.random.normal(ks[0], (B, T, C), jnp.float32), 'time_decay': jax.random.normal(ks[1], (C,), jnp.float32) * 0.01, 'time_first': jax.random.normal(ks[2], (C,), jnp.float32) * 0.01, 'w_tk': jax.random.normal(ks[3], (C, C), jnp.float32) * s, 'w_tv': jax.random.normal(ks[4], (C, C), jnp.float32) * s, 'w_tr': jax.random.normal(ks[5], (C, C), jnp.float32) * s, 'w_ck': jax.random.normal(ks[6], (C, 4 * C), jnp.float32) * s, 'w_cv': jax.random.normal(ks[7], (4 * C, C), jnp.float32) * s, 'w_cr': jax.random.normal(ks[8], (C, C), jnp.float32) * s, 'ln1_g': jnp.ones((C,), jnp.float32), 'ln1_b': jnp.zeros((C,), jnp.float32), 'ln2_g': jnp.ones((C,), jnp.float32), 'ln2_b': jnp.zeros((C,), jnp.float32), 'mix_k': jnp.ones((1, 1, C), jnp.float32), 'mix_v': jnp.ones((1, 1, C), jnp.float32), 'mix_r': jnp.ones((1, 1, C), jnp.float32), 'cmix_k': jnp.ones((1, 1, C), jnp.float32), 'cmix_r': jnp.ones((1, 1, C), jnp.float32)}
    _L0_attn_in = _L0_attn_setup()

    def _L0_ffn_setup():
        import jax, jax.numpy as jnp
        import numpy as np
        DIM = 128
        DEPTH = 6
        HEADS = 16
        DIM_HEAD = 64
        WINDOW = 32
        INNER = HEADS * DIM_HEAD
        DIM_INNER = int(DIM * 4 * 2 / 3)
        QK_SCALE = 8.0

        def shift_tokens(t):
            a, s = jnp.split(t, 2, -1)
            s = jnp.pad(s, ((0, 0), (1, 0), (0, 0)))[:, :-1]
            return jnp.concatenate([a, s], -1)

        def l2norm(t):
            return t / jnp.maximum(jnp.linalg.norm(t, axis=-1, keepdims=True), 1e-12)

        def rotate_half(x):
            x1, x2 = jnp.split(x, 2, -1)
            return jnp.concatenate([-x2, x1], -1)

        def rotary_tables(n):
            half = jnp.arange(0, DIM_HEAD, 2, dtype=jnp.float32)
            inv_freq = 1.0 / 10000.0 ** (half / DIM_HEAD)
            t = jnp.arange(n, dtype=jnp.float32)
            freqs = t[:, None] * inv_freq[None, :]
            freqs = jnp.concatenate([freqs, freqs], -1)
            base_scale = (half + 0.4 * DIM_HEAD) / (1.4 * DIM_HEAD)
            power = (t - n // 2) / (WINDOW // 2)
            scale = base_scale[None, :] ** power[:, None]
            scale = jnp.concatenate([scale, scale], -1)
            return (freqs, scale)

        def local_attention(q, k, v):
            b, h, n, d = q.shape
            w = WINDOW
            nw = n // w
            bq = q.reshape(b, h, nw, w, d)
            bk = k.reshape(b, h, nw, w, d)
            bv = v.reshape(b, h, nw, w, d)

            def look(t):
                p = jnp.pad(t, ((0, 0), (0, 0), (1, 0), (0, 0), (0, 0)))
                return jnp.concatenate([p[:, :, :nw], p[:, :, 1:]], axis=3)
            bk2, bv2 = (look(bk), look(bv))
            seq = jnp.arange(n).reshape(nw, w)
            seq_p = jnp.pad(seq, ((1, 0), (0, 0)), constant_values=-1)
            jt = jnp.concatenate([seq_p[:nw], seq_p[1:]], axis=1)
            it = seq[:, :, None]
            jb = jt[:, None, :]
            mask = (it < jb) | (it > jb + w) | (jb == -1)
            sim = jnp.einsum('bhwie,bhwje->bhwij', bq, bk2) * QK_SCALE
            sim = jnp.where(mask, -jnp.finfo(sim.dtype).max, sim)
            attn = jax.nn.softmax(sim, -1)
            out = jnp.einsum('bhwij,bhwje->bhwie', attn, bv2)
            return out.reshape(b, h, n, d)

        def attn_layer(x, Wqkv, qs, ksc, Wo):
            b, n, _ = x.shape
            qkv = x @ Wqkv
            q, k, v = jnp.split(qkv, 3, -1)
            sh = lambda t: t.reshape(b, n, HEADS, DIM_HEAD).transpose(0, 2, 1, 3)
            q, k, v = (sh(q), sh(k), sh(v))
            q = l2norm(q) * qs
            k = l2norm(k) * ksc
            freqs, scale = rotary_tables(n)
            cos, sin = (jnp.cos(freqs), jnp.sin(freqs))
            q = q * cos * scale + rotate_half(q) * sin * scale
            inv = 1.0 / scale
            k = k * cos * inv + rotate_half(k) * sin * inv
            out = local_attention(q, k, v)
            out = out.transpose(0, 2, 1, 3).reshape(b, n, INNER)
            return out @ Wo

        def ffn_layer(x, g, bln, W1, b1, W2, b2):
            mu = x.mean(-1, keepdims=True)
            var = ((x - mu) ** 2).mean(-1, keepdims=True)
            xn = (x - mu) / jnp.sqrt(var + 1e-05) * g + bln
            hg = xn @ W1 + b1
            a, gate = jnp.split(hg, 2, -1)
            return a * jax.nn.gelu(gate, approximate=False) @ W2 + b2
        key = jax.random.key(seed)
        ks = jax.random.split(key, 8)
        B, N = (2, 256)
        init = lambda k, shape: jax.random.normal(k, shape, jnp.float32) * 0.02
        return {'x': jax.random.normal(ks[0], (B, N, DIM), jnp.float32), 'Wqkv': init(ks[1], (DEPTH, DIM, 3 * INNER)), 'q_scale': jnp.ones((DEPTH, DIM_HEAD), jnp.float32), 'k_scale': jnp.ones((DEPTH, DIM_HEAD), jnp.float32), 'Wo': init(ks[2], (DEPTH, INNER, DIM)), 'ln_g': jnp.ones((DEPTH, DIM), jnp.float32), 'ln_b': jnp.zeros((DEPTH, DIM), jnp.float32), 'W1': init(ks[3], (DEPTH, DIM, 2 * DIM_INNER)), 'b1': jnp.zeros((DEPTH, 2 * DIM_INNER), jnp.float32), 'W2': init(ks[4], (DEPTH, DIM_INNER, DIM)), 'b2': jnp.zeros((DEPTH, DIM), jnp.float32)}
    _L0_ffn_in = _L0_ffn_setup()

    def _L1_attn_setup():
        import jax, jax.numpy as jnp
        import numpy as np
        B, T, H = (2, 128, 128)
        NH = 4
        DK, DV = (64, 128)
        dk, dv = (DK // NH, DV // NH)
        LR = 16
        GATE_NORM = 16.0
        EPS = 1e-05
        key = jax.random.key(seed)
        ks = jax.random.split(key, 9)
        s = 0.02
        return {'x': jax.random.normal(ks[0], (B, T, H), jnp.float32), 'Wq': jax.random.normal(ks[1], (H, DK), jnp.float32) * s, 'Wk': jax.random.normal(ks[2], (H, DK), jnp.float32) * s, 'Wv': jax.random.normal(ks[3], (H, DV), jnp.float32) * s, 'Wgk1': jax.random.normal(ks[4], (H, LR), jnp.float32) * s, 'Wgk2': jax.random.normal(ks[5], (LR, DK), jnp.float32) * s, 'bgk2': jnp.zeros((DK,), jnp.float32), 'Wg': jax.random.normal(ks[6], (H, DV), jnp.float32) * s, 'Wo': jax.random.normal(ks[7], (DV, H), jnp.float32) * s, 'gw': jnp.ones((dv,), jnp.float32)}
    _L1_attn_in = _L1_attn_setup()

    def _L1_ffn_setup():
        import jax, jax.numpy as jnp
        import numpy as np
        B, S, H, E, K = (4, 256, 128, 8, 2)
        key = jax.random.key(seed)
        k0, k1, k2, k3 = jax.random.split(key, 4)
        x = jax.random.normal(k0, (B, S, H), dtype=jnp.float32)
        router_w = jax.random.normal(k1, (E, H), dtype=jnp.float32) * np.float32(1.0 / np.sqrt(H))
        xav1 = np.float32(np.sqrt(2.0 / (2 * H + H)))
        w1 = jax.random.normal(k2, (E, 2 * H, H), dtype=jnp.float32) * xav1
        w2 = jax.random.normal(k3, (E, H, 2 * H), dtype=jnp.float32) * xav1
        return {'x': x, 'router_w': router_w, 'w1': w1, 'w2': w2}
    _L1_ffn_in = _L1_ffn_setup()
    _d = {'L0_attn_x': _L0_attn_in['x'], 'L0_attn_time_decay': _L0_attn_in['time_decay'], 'L0_attn_time_first': _L0_attn_in['time_first'], 'L0_attn_w_tk': _L0_attn_in['w_tk'], 'L0_attn_w_tv': _L0_attn_in['w_tv'], 'L0_attn_w_tr': _L0_attn_in['w_tr'], 'L0_attn_w_ck': _L0_attn_in['w_ck'], 'L0_attn_w_cv': _L0_attn_in['w_cv'], 'L0_attn_w_cr': _L0_attn_in['w_cr'], 'L0_attn_ln1_g': _L0_attn_in['ln1_g'], 'L0_attn_ln1_b': _L0_attn_in['ln1_b'], 'L0_attn_ln2_g': _L0_attn_in['ln2_g'], 'L0_attn_ln2_b': _L0_attn_in['ln2_b'], 'L0_attn_mix_k': _L0_attn_in['mix_k'], 'L0_attn_mix_v': _L0_attn_in['mix_v'], 'L0_attn_mix_r': _L0_attn_in['mix_r'], 'L0_attn_cmix_k': _L0_attn_in['cmix_k'], 'L0_attn_cmix_r': _L0_attn_in['cmix_r'], 'L0_ffn_Wqkv': _L0_ffn_in['Wqkv'], 'L0_ffn_q_scale': _L0_ffn_in['q_scale'], 'L0_ffn_k_scale': _L0_ffn_in['k_scale'], 'L0_ffn_Wo': _L0_ffn_in['Wo'], 'L0_ffn_ln_g': _L0_ffn_in['ln_g'], 'L0_ffn_ln_b': _L0_ffn_in['ln_b'], 'L0_ffn_W1': _L0_ffn_in['W1'], 'L0_ffn_b1': _L0_ffn_in['b1'], 'L0_ffn_W2': _L0_ffn_in['W2'], 'L0_ffn_b2': _L0_ffn_in['b2'], 'L1_attn_Wq': _L1_attn_in['Wq'], 'L1_attn_Wk': _L1_attn_in['Wk'], 'L1_attn_Wv': _L1_attn_in['Wv'], 'L1_attn_Wgk1': _L1_attn_in['Wgk1'], 'L1_attn_Wgk2': _L1_attn_in['Wgk2'], 'L1_attn_bgk2': _L1_attn_in['bgk2'], 'L1_attn_Wg': _L1_attn_in['Wg'], 'L1_attn_Wo': _L1_attn_in['Wo'], 'L1_attn_gw': _L1_attn_in['gw'], 'L1_ffn_router_w': _L1_ffn_in['router_w'], 'L1_ffn_w1': _L1_ffn_in['w1'], 'L1_ffn_w2': _L1_ffn_in['w2']}
    _x0 = _d['L0_attn_x']
    _d['L0_attn_x'] = jax.random.normal(jax.random.fold_in(jax.random.key(seed), 1), (4, 512, 128), dtype=_x0.dtype)
    del _x0
    return _d

def reference(L0_attn_x, L0_attn_time_decay, L0_attn_time_first, L0_attn_w_tk, L0_attn_w_tv, L0_attn_w_tr, L0_attn_w_ck, L0_attn_w_cv, L0_attn_w_cr, L0_attn_ln1_g, L0_attn_ln1_b, L0_attn_ln2_g, L0_attn_ln2_b, L0_attn_mix_k, L0_attn_mix_v, L0_attn_mix_r, L0_attn_cmix_k, L0_attn_cmix_r, L0_ffn_Wqkv, L0_ffn_q_scale, L0_ffn_k_scale, L0_ffn_Wo, L0_ffn_ln_g, L0_ffn_ln_b, L0_ffn_W1, L0_ffn_b1, L0_ffn_W2, L0_ffn_b2, L1_attn_Wq, L1_attn_Wk, L1_attn_Wv, L1_attn_Wgk1, L1_attn_Wgk2, L1_attn_bgk2, L1_attn_Wg, L1_attn_Wo, L1_attn_gw, L1_ffn_router_w, L1_ffn_w1, L1_ffn_w2):

    def _L0_attn_ref(x, time_decay, time_first, w_tk, w_tv, w_tr, w_ck, w_cv, w_cr, ln1_g, ln1_b, ln2_g, ln2_b, mix_k, mix_v, mix_r, cmix_k, cmix_r):
        import jax, jax.numpy as jnp
        import numpy as np
        LN_EPS = 1e-05
        NEG_INF = -1e+38

        def _layer_norm(x, g, b):
            mu = x.mean(-1, keepdims=True)
            var = ((x - mu) ** 2).mean(-1, keepdims=True)
            return (x - mu) * jax.lax.rsqrt(var + LN_EPS) * g + b

        def _wkv(w, u, k, v):
            B, T, C = k.shape
            kt = jnp.swapaxes(k, 0, 1)
            vt = jnp.swapaxes(v, 0, 1)
            aa0 = jnp.zeros((B, C), k.dtype)
            bb0 = jnp.zeros((B, C), k.dtype)
            pp0 = jnp.full((B, C), NEG_INF, k.dtype)

            def step(carry, inp):
                aa, bb, pp = carry
                kk, vv = inp
                p = jnp.maximum(pp, u + kk)
                e1 = jnp.exp(pp - p)
                e2 = jnp.exp(u + kk - p)
                y = (e1 * aa + e2 * vv) / (e1 + e2)
                p2 = jnp.maximum(pp + w, w + kk)
                e1u = jnp.exp(pp + w - p2)
                e2u = jnp.exp(w + kk - p2)
                aa2 = e1u * aa + e2u * vv
                bb2 = e1u + e2u
                pp2 = p2 + jnp.log(bb2)
                return ((aa2, bb2, pp2), y)
            _, ys = jax.lax.scan(step, (aa0, bb0, pp0), (kt, vt))
            return jnp.swapaxes(ys, 0, 1)

        def _shift(h):
            return jnp.pad(h[:, :-1, :], ((0, 0), (1, 0), (0, 0)))
        h = _layer_norm(x, ln1_g, ln1_b)
        hp = _shift(h)
        xk = h * mix_k + hp * (1.0 - mix_k)
        xv = h * mix_v + hp * (1.0 - mix_v)
        xr = h * mix_r + hp * (1.0 - mix_r)
        k = xk @ w_tk
        v = xv @ w_tv
        r = jax.nn.sigmoid(xr @ w_tr)
        y = _wkv(time_decay, time_first, k, v)
        x = x + r * y
        h2 = _layer_norm(x, ln2_g, ln2_b)
        hp2 = _shift(h2)
        ck = h2 * cmix_k + hp2 * (1.0 - cmix_k)
        cr = h2 * cmix_r + hp2 * (1.0 - cmix_r)
        kk = jnp.square(jax.nn.relu(ck @ w_ck))
        x = x + jax.nn.sigmoid(cr @ w_cr) * (kk @ w_cv)
        return x

    def _L0_ffn_ref(x, Wqkv, q_scale, k_scale, Wo, ln_g, ln_b, W1, b1, W2, b2):
        import jax, jax.numpy as jnp
        import numpy as np
        DIM = 128
        DEPTH = 6
        HEADS = 16
        DIM_HEAD = 64
        WINDOW = 32
        INNER = HEADS * DIM_HEAD
        DIM_INNER = int(DIM * 4 * 2 / 3)
        QK_SCALE = 8.0

        def shift_tokens(t):
            a, s = jnp.split(t, 2, -1)
            s = jnp.pad(s, ((0, 0), (1, 0), (0, 0)))[:, :-1]
            return jnp.concatenate([a, s], -1)

        def l2norm(t):
            return t / jnp.maximum(jnp.linalg.norm(t, axis=-1, keepdims=True), 1e-12)

        def rotate_half(x):
            x1, x2 = jnp.split(x, 2, -1)
            return jnp.concatenate([-x2, x1], -1)

        def rotary_tables(n):
            half = jnp.arange(0, DIM_HEAD, 2, dtype=jnp.float32)
            inv_freq = 1.0 / 10000.0 ** (half / DIM_HEAD)
            t = jnp.arange(n, dtype=jnp.float32)
            freqs = t[:, None] * inv_freq[None, :]
            freqs = jnp.concatenate([freqs, freqs], -1)
            base_scale = (half + 0.4 * DIM_HEAD) / (1.4 * DIM_HEAD)
            power = (t - n // 2) / (WINDOW // 2)
            scale = base_scale[None, :] ** power[:, None]
            scale = jnp.concatenate([scale, scale], -1)
            return (freqs, scale)

        def local_attention(q, k, v):
            b, h, n, d = q.shape
            w = WINDOW
            nw = n // w
            bq = q.reshape(b, h, nw, w, d)
            bk = k.reshape(b, h, nw, w, d)
            bv = v.reshape(b, h, nw, w, d)

            def look(t):
                p = jnp.pad(t, ((0, 0), (0, 0), (1, 0), (0, 0), (0, 0)))
                return jnp.concatenate([p[:, :, :nw], p[:, :, 1:]], axis=3)
            bk2, bv2 = (look(bk), look(bv))
            seq = jnp.arange(n).reshape(nw, w)
            seq_p = jnp.pad(seq, ((1, 0), (0, 0)), constant_values=-1)
            jt = jnp.concatenate([seq_p[:nw], seq_p[1:]], axis=1)
            it = seq[:, :, None]
            jb = jt[:, None, :]
            mask = (it < jb) | (it > jb + w) | (jb == -1)
            sim = jnp.einsum('bhwie,bhwje->bhwij', bq, bk2) * QK_SCALE
            sim = jnp.where(mask, -jnp.finfo(sim.dtype).max, sim)
            attn = jax.nn.softmax(sim, -1)
            out = jnp.einsum('bhwij,bhwje->bhwie', attn, bv2)
            return out.reshape(b, h, n, d)

        def attn_layer(x, Wqkv, qs, ksc, Wo):
            b, n, _ = x.shape
            qkv = x @ Wqkv
            q, k, v = jnp.split(qkv, 3, -1)
            sh = lambda t: t.reshape(b, n, HEADS, DIM_HEAD).transpose(0, 2, 1, 3)
            q, k, v = (sh(q), sh(k), sh(v))
            q = l2norm(q) * qs
            k = l2norm(k) * ksc
            freqs, scale = rotary_tables(n)
            cos, sin = (jnp.cos(freqs), jnp.sin(freqs))
            q = q * cos * scale + rotate_half(q) * sin * scale
            inv = 1.0 / scale
            k = k * cos * inv + rotate_half(k) * sin * inv
            out = local_attention(q, k, v)
            out = out.transpose(0, 2, 1, 3).reshape(b, n, INNER)
            return out @ Wo

        def ffn_layer(x, g, bln, W1, b1, W2, b2):
            mu = x.mean(-1, keepdims=True)
            var = ((x - mu) ** 2).mean(-1, keepdims=True)
            xn = (x - mu) / jnp.sqrt(var + 1e-05) * g + bln
            hg = xn @ W1 + b1
            a, gate = jnp.split(hg, 2, -1)
            return a * jax.nn.gelu(gate, approximate=False) @ W2 + b2
        for i in range(DEPTH):
            x = attn_layer(shift_tokens(x), Wqkv[i], q_scale[i], k_scale[i], Wo[i]) + x
            x = ffn_layer(shift_tokens(x), ln_g[i], ln_b[i], W1[i], b1[i], W2[i], b2[i]) + x
        return x

    def _L1_attn_ref(x, Wq, Wk, Wv, Wgk1, Wgk2, bgk2, Wg, Wo, gw):
        import jax, jax.numpy as jnp
        import numpy as np
        B, T, H = (2, 128, 128)
        NH = 4
        DK, DV = (64, 128)
        dk, dv = (DK // NH, DV // NH)
        LR = 16
        GATE_NORM = 16.0
        EPS = 1e-05
        b, t, _ = x.shape
        q = (x @ Wq).reshape(b, t, NH, dk)
        k = (x @ Wk).reshape(b, t, NH, dk)
        v = (x @ Wv).reshape(b, t, NH, dv)
        gk = (jax.nn.log_sigmoid(x @ Wgk1 @ Wgk2 + bgk2) / GATE_NORM).reshape(b, t, NH, dk)
        scale = dk ** (-0.5)

        def step(S, inp):
            q_t, k_t, v_t, gk_t = inp
            S = jnp.exp(gk_t)[..., None] * S + k_t[..., None] * v_t[..., None, :]
            o_t = jnp.einsum('bhk,bhkv->bhv', q_t, S) * scale
            return (S, o_t)
        xs = tuple((jnp.moveaxis(a, 1, 0) for a in (q, k, v, gk)))
        S0 = jnp.zeros((b, NH, dk, dv), x.dtype)
        _, o = jax.lax.scan(step, S0, xs)
        o = jnp.moveaxis(o, 0, 1)
        g = (x @ Wg).reshape(b, t, NH, dv)
        o = o * jax.lax.rsqrt(jnp.mean(o * o, axis=-1, keepdims=True) + EPS) * gw
        o = o * (g * jax.nn.sigmoid(g))
        return o.reshape(b, t, DV) @ Wo

    def _L1_ffn_ref(x, router_w, w1, w2):
        import jax, jax.numpy as jnp
        import numpy as np
        B, S, H, E, K = (4, 256, 128, 8, 2)
        bsz, seq, hidden = x.shape
        n_experts = w1.shape[0]
        tokens = x.reshape(-1, hidden)
        T = tokens.shape[0]
        logits = tokens @ router_w.T
        topv, topi = jax.lax.top_k(logits, K)
        w = jax.nn.softmax(topv, axis=-1).astype(tokens.dtype)
        gate = jnp.zeros((T, n_experts), tokens.dtype).at[jnp.arange(T)[:, None], topi].add(w)
        out = jnp.zeros_like(tokens)
        for e in range(n_experts):
            h = jax.nn.gelu(tokens @ w1[e].T, approximate=False)
            y = h @ w2[e].T
            out = out + gate[:, e:e + 1] * y
        return out.reshape(bsz, seq, hidden)
    x = L0_attn_x
    xn = _layernorm(x, axis=-1)
    x = x + _L0_attn_ref(xn, L0_attn_time_decay, L0_attn_time_first, L0_attn_w_tk, L0_attn_w_tv, L0_attn_w_tr, L0_attn_w_ck, L0_attn_w_cv, L0_attn_w_cr, L0_attn_ln1_g, L0_attn_ln1_b, L0_attn_ln2_g, L0_attn_ln2_b, L0_attn_mix_k, L0_attn_mix_v, L0_attn_mix_r, L0_attn_cmix_k, L0_attn_cmix_r) + _L0_ffn_ref(xn, L0_ffn_Wqkv, L0_ffn_q_scale, L0_ffn_k_scale, L0_ffn_Wo, L0_ffn_ln_g, L0_ffn_ln_b, L0_ffn_W1, L0_ffn_b1, L0_ffn_W2, L0_ffn_b2)
    xn = _layernorm(x, axis=-1)
    x = x + _L1_attn_ref(xn, L1_attn_Wq, L1_attn_Wk, L1_attn_Wv, L1_attn_Wgk1, L1_attn_Wgk2, L1_attn_bgk2, L1_attn_Wg, L1_attn_Wo, L1_attn_gw) + _L1_ffn_ref(xn, L1_ffn_router_w, L1_ffn_w1, L1_ffn_w2)
    return x

_drawn_inputs = setup_inputs


def setup_inputs(seed=0):
    import zlib

    import numpy as np

    out = dict(_drawn_inputs(seed))
    spreads = {'L0_attn_ln1_g': (1.0, 0.6),
     'L0_attn_ln1_b': (0.0, 0.1),
     'L0_attn_ln2_g': (1.0, 0.6),
     'L0_attn_ln2_b': (0.0, 0.8),
     'L0_attn_mix_k': (1.0, 0.6),
     'L0_attn_mix_v': (1.0, 0.6),
     'L0_attn_mix_r': (1.0, 0.6),
     'L0_attn_cmix_k': (1.0, 0.6),
     'L0_attn_cmix_r': (1.0, 0.6),
     'L0_ffn_q_scale': (1.0, 0.6),
     'L0_ffn_k_scale': (1.0, 0.6),
     'L0_ffn_ln_g': (1.0, 0.6),
     'L0_ffn_ln_b': (0.0, 0.8),
     'L0_ffn_b1': (0.0, 0.8),
     'L0_ffn_b2': (0.0, 0.597),
     'L1_attn_bgk2': (0.0, 0.8),
     'L1_attn_gw': (1.0, 0.6)}
    factors = {'L0_attn_time_decay': 5.946,
     'L0_attn_time_first': 64.0,
     'L0_attn_w_tk': 2.897,
     'L0_attn_w_tr': 4.801,
     'L0_attn_w_ck': 6.446,
     'L0_attn_w_cv': 6.8,
     'L0_attn_w_cr': 8.0,
     'L0_ffn_W1': 4.136,
     'L0_ffn_W2': 4.034,
     'L1_attn_Wq': 6.546,
     'L1_attn_Wk': 6.475,
     'L1_attn_Wv': 6.507,
     'L1_attn_Wgk1': 8.0,
     'L1_attn_Wgk2': 8.0,
     'L1_attn_Wg': 6.534,
     'L1_attn_Wo': 6.516,
     'L1_ffn_router_w': 4.496,
     'L1_ffn_w1': 4.424,
     'L1_ffn_w2': 4.07}
    for name, (base, spread) in spreads.items():
        noise = np.random.default_rng([zlib.crc32(name.encode()), seed]).standard_normal(out[name].shape)
        drawn = base * np.exp(spread * noise) if base else spread * noise
        out[name] = jnp.asarray(drawn.astype(out[name].dtype))
    for name, factor in factors.items():
        out[name] = (out[name] * factor).astype(out[name].dtype)
    return out
```

```python
from contextlib import ExitStack

import concourse.bass as bass
from concourse import mybir

F32 = mybir.dt.float32
F32R = mybir.dt.float32r
BF16 = mybir.dt.bfloat16
ALU = mybir.AluOpType
ACT = mybir.ActivationFunctionType
AX = mybir.AxisListType.X

B, T, C = 4, 512, 128
NTOK = B * T
TILES = NTOK // 128
DEPTH, HEADS, DH, WIN = 6, 16, 64, 32
HALF = DH // 2
GH = 4
GROUPS = HEADS // GH
NW = T // WIN
UW = NW // 2
UNITS = 2 * GROUPS
INNER = HEADS * DH
GD = GH * DH
QK_SCALE = 8.0
FF = int(C * 4 * 2 / 3)
FT = [(0, 128), (128, 128), (256, FF - 256)]
NH, DK, DV, LR = 4, 16, 32, 16
GATE_NORM = 16.0
E, H2 = 8, 256
EPS = 1e-5
NEG_INF = -1e38
RN_MAX = 1e12
LN_SCALE = float(2 ** 20)

P_W, P_U, P_G1, P_B1, P_G2, P_B2, P_MK, P_MV, P_MR, P_CK, P_CR, P_GW, P_BGK = range(13)
NPAR = 13
L_QA, L_QB, L_KA, L_KB, L_G, L_B, L_B1A, L_B1G, L_B2 = 0, 1, 2, 3, 4, 5, 6, 9, 12
NLP = 13
PRE = 3


def after(k):
    return k + 1


def slot(w):
    return 4 * (w // 4) + 2 * (w % 2) + w % 4 // 2


def program(nc, x, params, lparams, w_tk, w_tv, w_tr, w_ck, w_cv, w_cr, wqkv, wo, w1, w2,
            gwq, gwk, gwv, gwg1, gwg2, gwg, gwo, router_t, ew1, ew2,
            rot, blocks, ident, mask, out):
    ctx = ExitStack()
    with ctx:
        def sem(name):
            return ctx.enter_context(nc.semaphore(name))

        def sbuf(name, cols, dt=F32):
            return ctx.enter_context(nc.sbuf_tensor(name, [128, cols], dt))

        bank = [ctx.enter_context(nc.psum_tensor(f"bank{i}", [128, 512], F32)) for i in range(8)]

        acc = sbuf("acc", NTOK)
        xres = sbuf("xres", NTOK)
        par = sbuf("par", NPAR)
        ident_s = sbuf("ident_s", 128)
        blocks_s = sbuf("blocks_s", 128)
        mean_s = sbuf("mean_s", 128)
        identb = sbuf("identb", 128, BF16)
        maskb = sbuf("maskb", 2 * 512, BF16)
        consts = sbuf("consts", 4)
        wq_hi = sbuf("wq_hi", 3 * INNER, F32R)
        wq_lo = sbuf("wq_lo", 3 * INNER, F32R)
        xs_hi = sbuf("xs_hi", WIN + T, F32R)
        xs_lo = sbuf("xs_lo", WIN + T, F32R)
        ARENA = 38300
        arena = sbuf("arena", ARENA)
        at = [0]

        def take(cols):
            a = arena[:, at[0]:at[0] + cols]
            at[0] += cols
            assert at[0] <= ARENA, at[0]
            return a

        accv = acc[:, :].rearrange("p (b t) -> p b t", b=B)
        xv = xres[:, :].rearrange("p (b t) -> p b t", b=B)

        xc = take(4 * T).rearrange("p (x t) -> p x t", x=4)
        lsq = take(2 * T).rearrange("p (x t) -> p x t", x=2)
        lln = take(2 * T).rearrange("p (x t) -> p x t", x=2)
        lrs = take(2 * T).rearrange("p (x t) -> p x t", x=2)
        wraw = take(3 * INNER)
        wo_s = take(8 * C).rearrange("p (k c) -> p k c", k=8)
        w1_s = take(2 * FF)
        w2_s = take(3 * C).rearrange("p (k c) -> p k c", k=3)
        lp = take(NLP)
        rot_s = take(4 * T).rearrange("p (k t) -> p k t", k=4)
        phase_at = at[0]
        t4, sqs, lnb, rnb = xc, lsq, lln, lrs
        qbd = take(2 * 2 * GH * T).rearrange("p (s a w h t) -> p s a w h t", s=2, a=2, w=NW, h=GH)
        kb = take(2 * 2 * (WIN + T)).rearrange("p (s a t) -> p s a t", s=2, a=2)
        sqb = take(4 * T).rearrange("p (x a t) -> p x a t", x=2, a=2)
        tab = take(2 * T).rearrange("p (x t) -> p x t", x=2)
        vflat = take(2 * 2 * 4 * GD)
        vb = vflat.rearrange("p (s o m d) -> p s o m d", s=2, o=2, m=4)
        hflat = take(3 * 1024)
        probs = hflat[:, 0:1024].rearrange("p (s w k) -> p s w k", s=2, w=UW)
        pts = hflat[:, 1024:1536]
        qst = hflat[:, 2048:3072].rearrange("p (a t) -> p a t", a=2)
        oflat = take(8 * T)
        ot = oflat.rearrange("p (k t) -> p k t", k=8)
        mx = take(2 * UW).rearrange("p (s w) -> p s w", s=2)
        sm = take(2 * UW).rearrange("p (s w) -> p s w", s=2)
        rc = take(2 * UW).rearrange("p (s w) -> p s w", s=2)
        xf = oflat[:, 0:NTOK].rearrange("p (b t) -> p b t", b=B)
        xh = oflat[:, NTOK:2 * NTOK].rearrange("p (b t) -> p b t", b=B)
        gg = vflat[:, 0:3072].rearrange("p (s j t) -> p s j t", s=2, j=3)
        hh = hflat.rearrange("p (s j t) -> p s j t", s=2, j=3)

        at[0] = phase_at
        xtok = take(NTOK).rearrange("p (m c) -> p m c", c=C)
        hb = take(B * (T + 1)).rearrange("p (b t) -> p b t", b=B)
        h2b = take(B * (T + 1)).rearrange("p (b t) -> p b t", b=B)
        traw = take(4 * C + 4 * C)
        tmix = take(2 * 8 * C).rearrange("p (x c) -> p x c", x=2)
        tcv = take(4 * C).rearrange("p (k c) -> p k c", k=4)
        om = take(5)
        wfull = take(T)
        rwx = take(NTOK).rearrange("p (b t) -> p b t", b=B)
        m_run = take(T + 1)
        s_run = take(T + 1)
        pp = take(T + 1)
        a_run = take(T + 1)
        args = take(2 * T).rearrange("p (x t) -> p x t", x=2)
        kw = take(T)
        kmx = take(T)
        bv = take(T)
        kkb = take(4 * T).rearrange("p (x t) -> p x t", x=4)
        rr = take(T)
        maskf = take(2 * 512)

        at[0] = phase_at
        xn2 = take(NTOK).rearrange("p (b t) -> p b t", b=B)
        graw = take(64 + 64 + 128 + LR + 64 + 128 + 128)
        gwk_s, gwq_s, gwv_s, gwg1_s, gwg2_s, gwg_s, gwo_s = (
            graw[:, a:a + n] for a, n in ((0, 64), (64, 64), (128, 128), (256, LR), (272, 64), (336, 128), (464, 128)))
        wkrep = take(DK * 128).rearrange("p (i h r) -> p i h r", i=DK, h=NH)
        wqrep = take(DK * 128).rearrange("p (i h r) -> p i h r", i=DK, h=NH)
        selrep = take(DK * 128).rearrange("p (i h r) -> p i h r", i=DK, h=NH)
        vt = take(NTOK).rearrange("p (b t) -> p b t", b=B)
        egk = take(NTOK).rearrange("p (b t) -> p b t", b=B)
        gs = take(NTOK).rearrange("p (b t) -> p b t", b=B)
        go = take(NTOK).rearrange("p (b t) -> p b t", b=B)
        kvb = take(2 * T).rearrange("p (x t) -> p x t", x=2)
        sst = take(2 * T).rearrange("p (x t) -> p x t", x=2)
        tmp = take(2 * T).rearrange("p (x t) -> p x t", x=2)
        zb = take(T)
        g1s = take(T)
        az = take(2 * T).rearrange("p (x t) -> p x t", x=2)
        rt_s = take(E)
        top8 = take(TILES * 8).rearrange("p (m e) -> p m e", m=TILES)
        lg = take(TILES * 8).rearrange("p (m e) -> p m e", m=TILES)
        topi = ctx.enter_context(nc.sbuf_tensor("topi", [128, TILES * 8], mybir.dt.uint32))
        topf = take(TILES * 8).rearrange("p (m e) -> p m e", m=TILES)
        gate = take(TILES * 8).rearrange("p (m e) -> p m e", m=TILES)
        gpart = take(TILES * 8).rearrange("p (m e) -> p m e", m=TILES)
        gw12 = take(3 * TILES).rearrange("p (x m) -> p x m", x=3)
        iot = take(E)
        at[0] = 5 * 1024
        ew1_s = take(E * 2 * C).rearrange("p (e h c) -> p e h c", e=E, h=2)
        ew2_s = take(E * H2).rearrange("p (e f) -> p e f", e=E)
        assert at[0] <= phase_at
        w1t = wkrep.rearrange("p i h r -> p (i h r)").rearrange("p (e f) -> p e f", e=E)
        w2t = wqrep.rearrange("p i h r -> p (i h r)").rearrange("p (e h c) -> p e h c", e=E, h=2)
        otok = selrep.rearrange("p i h r -> p (i h r)").rearrange("p (m c) -> p m c", c=C)
        ht = vt.rearrange("p b t -> p (b t)").rearrange("p (s h t) -> p s h t", s=2, h=2)

        def head_windows(u, h, k):
            g, hf = u // 2, u % 2
            rows = ot[64 * h:64 * h + 64, 2 * g:2 * g + 2, 256 * hf:256 * hf + 256]
            return rows.rearrange("p k (m x o q) -> p k m x o q", m=2, x=2, o=2)[:, :, :, k]

        def own_part(n, h):
            return bank[n][64 * h:64 * h + 64, :].rearrange("p (k m o h q) -> p k m o h q", k=2, m=2, o=2, h=2)[:, :, :, :, h]

        def group(names):
            return {n: sem(n) for n in names.split()}

        pe_s = group("mean_mm var_mm q_mm k_mm v_mm n2_mm s_mm t_mm pv_mm y_mm fg_mm fa_mm fy_mm")
        act_s = group("ln_sq ln_log ln_rstd sq_act log_act rn_act v_out exp_act pt_out o1_out xs_hi_act place_act xf_act gelu_act")
        dve_s = group("ln_xc ln_n ln_out max_dve sub_dve sum_dve rec_dve tab_dve mul_dve o0_out resid_dve xs_lo_dve xf0_dve hh_dve fres_dve")
        pool_s = group("split_hi split sqadd rotadd norm_pool")
        s = {**pe_s, **act_s, **dve_s, **pool_s}
        wqkv_in, wo_in, ff_in = sem("wqkv_in"), sem("wo_in"), sem("ff_in")
        z = group("const_in x_in tm_in rot_in fin_in out_done zeroed x_turned x_copied "
                  "kvr_mm ck_mm cr_mm cv_mm mixed dve_link decay_arg decay_exp sum_scan log_sum carry_arg carry_exp "
                  "out_arg out_exp gate_exp k_free cm_exp kk_dve cm_done b1_done "
                  "fin_sum rep_made g1_mm g1_copy z_mm z_copy abs_act gexp_act gln_act gk_dve egk_act "
                  "gv_mm gv_copy gg_mm gg_exp gg_dve gg_act abank "
                  "rk_mm rg_mm rq_mm kv_dve scan_dve qs_dve oadd gsq_act gms_mm gl_act gr_act gn_dve go_mm x1_dve "
                  "tok_mm tok_copy lg_mm lg_copy route ew_turned ew_copied eh_mm eh_act ey_mm ey_dve iota_pool")
        block = ctx.enter_context(nc.Block())

        @block.sync
        def _(sp):
            for dst, src in ((ident_s, ident), (blocks_s, blocks), (par, params)):
                sp.dma_start(dst[:, :], src).then_inc(z["const_in"], 16)
            sp.dma_start(maskf, mask).then_inc(z["const_in"], 16)
            xtiles = x.rearrange("b (m p) c -> p (b m) c", p=128)
            for i in range(4):
                sp.dma_start(xtok[:, 4 * i:4 * i + 4, :], xtiles[:, 4 * i:4 * i + 4, :]).then_inc(z["x_in"], 16)
            for n, src in enumerate((w_tk, w_tv, w_tr, w_cr)):
                sp.dma_start(traw[:, n * C:(n + 1) * C], src).then_inc(z["tm_in"], 16)
            sp.dma_start(tmix[:, 0, 4 * C:8 * C], w_ck).then_inc(z["tm_in"], 16)
            sp.dma_start(tcv, w_cv.rearrange("(k p) c -> p k c", p=128)).then_inc(z["tm_in"], 16)
            sp.dma_start(rot_s, rot).then_inc(z["rot_in"], 16)

            with sp.Fori(0, DEPTH) as layer:
                sp.wait_ge(s["split"], after(layer))
                sp.dma_start(wraw, wqkv[bass.ds(layer, 1), :, :].rearrange("l c n -> c (l n)")).then_inc(wqkv_in, 16)
                sp.wait_ge(s["y_mm"], after(layer * B))
                sp.dma_start(wo_s, wo[bass.ds(layer, 1), :, :].rearrange("l (k p) c -> p (l k) c", p=128)).then_inc(wo_in, 16)
                sp.dma_start(lp[:, 0:4], lparams[bass.ds(layer, 1), :, 0:4].rearrange("l p c -> p (l c)")).then_inc(wo_in, 16)
                sp.wait_ge(s["fres_dve"], after(layer * B))
                sp.dma_start(w1_s, w1[bass.ds(layer, 1), :, :].rearrange("l c n -> c (l n)")).then_inc(ff_in, 16)
                sp.dma_start(w2_s[:, 0:2, :], w2[bass.ds(layer, 1), 0:256, :].rearrange("l (k p) c -> p (l k) c", p=128)).then_inc(ff_in, 16)
                sp.dma_start(w2_s[0:FF - 256, 2, :], w2[bass.ds(layer, 1), 256:FF, :].rearrange("l p c -> p (l c)")).then_inc(ff_in, 16)
                sp.dma_start(lp[:, 4:NLP], lparams[bass.ds(layer, 1), :, 4:NLP].rearrange("l p c -> p (l c)")).then_inc(ff_in, 16)

            sp.wait_ge(s["fres_dve"], after(DEPTH * B))
            for dst, src in ((gwk_s, gwk), (gwq_s, gwq), (gwv_s, gwv), (gwg1_s, gwg1), (gwg2_s[0:LR, :], gwg2),
                             (gwg_s, gwg), (gwo_s, gwo), (rt_s, router_t),
                             (ew1_s, ew1.rearrange("e (h p) c -> p e h c", p=128)),
                             (ew2_s, ew2.rearrange("e p f -> p e f"))):
                sp.dma_start(dst, src).then_inc(z["fin_in"], 16)
            outv = out.rearrange("b (m p) c -> p (b m) c", p=128)
            for q in range(B):
                sp.wait_ge(z["ey_dve"], q * E + E)
                sp.dma_start(outv[:, 4 * q:4 * q + 4, :], otok[:, 4 * q:4 * q + 4, :]).then_inc(z["out_done"], 16)
            sp.wait_ge(z["out_done"], 16 * B)

        @block.tensor
        def _(pe):
            for n in pe_s.values():
                pe.sem_inc(n, 1)


            def layer_norm(i, src):
                for c in range(B):
                    if i:
                        pe.wait_ge(s["ln_xc"], after(i * B + c))
                    pe.matmul(bank[6][:, :], mean_s[:, :], src(c), start=True, stop=True).then_inc(s["mean_mm"], 1)
                    if c > 0:
                        variance(i, c - 1)
                variance(i, B - 1)

            def variance(i, c):
                pe.wait_ge(s["ln_sq"], after(i * B + c + 1))
                pe.wait_ge(s["ln_log"], after(i * B + c))
                pe.matmul(bank[7][:, :], mean_s[:, :], lsq[:, c % 2, :], start=True, stop=True).then_inc(s["var_mm"], 1)

            def layer_norm_static(i, src):
                for c in range(B):
                    pe.wait_ge(s["ln_xc"], after(i * B + c))
                    pe.matmul(bank[6][:, :], mean_s[:, :], src(c), start=True, stop=True).then_inc(s["mean_mm"], 1)
                    if c > 0:
                        variance(i, c - 1)
                variance(i, B - 1)

            pe.wait_ge(z["const_in"], 16 * 4)
            for m in range(TILES):
                if m % 4 == 0:
                    pe.wait_ge(z["x_in"], 16 * 4)
                mm = pe.transpose(bank[m // 4][:, 128 * (m % 4):128 * (m % 4) + 128], xtok[:, m, :], ident_s[:, :])
            mm.then_inc(z["x_turned"], 1)
            pe.wait_ge(z["x_copied"], B)
            pe.wait_ge(z["zeroed"], 1)
            layer_norm_static(0, lambda c: accv[:, c, :])
            pe.wait_ge(s["ln_out"], after(B))
            layer_norm_static(1, lambda c: xv[:, c, :])
            pe.wait_ge(z["mixed"], 1)
            for b in range(B):
                pe.wait_ge(s["ln_out"], after(B + b + 1))
                if b >= 2:
                    pe.wait_ge(z["k_free"], b - 1)
                for j in range(3):
                    o = bank[j + 3 * (b % 2)][:, :]
                    pe.matmul(o, tmix[:, 0, j * C:(j + 1) * C], hb[:, b, 1:T + 1], start=True, stop=False)
                    mm = pe.matmul(o, tmix[:, 1, j * C:(j + 1) * C], hb[:, b, 0:T], start=False, stop=True)
                mm.then_inc(z["kvr_mm"], 1)
            pe.wait_ge(z["b1_done"], B)
            layer_norm_static(2, lambda c: rwx[:, c, :])
            for b in range(B):
                pe.wait_ge(s["ln_out"], after(2 * B + b + 1))
                for j in range(4):
                    if b >= 1:
                        pe.wait_ge(z["kk_dve"], 4 * (b - 1) + j + 1)
                    o = bank[j][:, :]
                    w = slice((4 + j) * C, (5 + j) * C)
                    pe.matmul(o, tmix[:, 0, w], h2b[:, b, 1:T + 1], start=True, stop=False)
                    pe.matmul(o, tmix[:, 1, w], h2b[:, b, 0:T], start=False, stop=True).then_inc(z["ck_mm"], 1)
                if b >= 1:
                    pe.wait_ge(z["cm_exp"], b)
                w = slice(3 * C, 4 * C)
                pe.matmul(bank[4][:, :], tmix[:, 0, w], h2b[:, b, 1:T + 1], start=True, stop=False)
                pe.matmul(bank[4][:, :], tmix[:, 1, w], h2b[:, b, 0:T], start=False, stop=True).then_inc(z["cr_mm"], 1)
                if b >= 1:
                    pe.wait_ge(z["cm_done"], b)
                for j in range(4):
                    pe.wait_ge(z["kk_dve"], 4 * b + j + 1)
                    mm = pe.matmul(bank[5][:, :], tcv[:, j, :], kkb[:, j, :], start=(j == 0), stop=(j == 3))
                mm.then_inc(z["cv_mm"], 1)
            pe.wait_ge(z["cm_done"], B)

            def three(o, w_at, rhs, w_first):
                hi, lo = rhs
                if w_first:
                    pe.matmul(o, w_at(wq_hi), hi, start=True, stop=False)
                    pe.matmul(o, w_at(wq_lo), hi, start=False, stop=False)
                    return pe.matmul(o, w_at(wq_hi), lo, start=False, stop=True)
                pe.matmul(o, hi, w_at(wq_hi), start=True, stop=False)
                pe.matmul(o, hi, w_at(wq_lo), start=False, stop=False)
                return pe.matmul(o, lo, w_at(wq_hi), start=False, stop=True)

            def project(pi, g, x_kind):
                k = 0 if x_kind == "q" else 1
                pe.wait_ge(s["mul_dve"], after(pi * 2 + k))
                for a in range(2):
                    at_ = k * INNER + g * GD + a * 128
                    mm = three(bank[2 * k + a][:, :], lambda w: w[:, at_:at_ + 128],
                               (xs_hi[:, WIN:], xs_lo[:, WIN:]), True)
                mm.then_inc(s["q_mm" if k == 0 else "k_mm"], 1)

            def norms(pi, k):
                pe.wait_ge(s["sqadd"], after(pi * 2 + k + 1))
                if k == 0:
                    pe.wait_ge(s["v_out"], after(pi * 4))
                else:
                    pe.wait_ge(s["log_act"], after(pi * 2 + 1))
                pe.matmul(bank[4][:, :], blocks_s[:, :], sqs[:, k, :], start=True, stop=True).then_inc(s["n2_mm"], 1)

            def values(pi, g, c, n=None):
                if c == 0:
                    pe.wait_ge(s["log_act"], after(pi * 2 + 2))
                else:
                    pe.wait_ge(s["v_out"], after(pi * 4 + c))
                for j in range(2):
                    t0 = (WIN if c < 2 else 0) + 128 * (2 * (c % 2) + j)
                    mm = three(bank[4][:, j * GD:(j + 1) * GD],
                               lambda w: w[:, 2 * INNER + g * GD:2 * INNER + (g + 1) * GD],
                               (xs_hi[:, t0:t0 + 128], xs_lo[:, t0:t0 + 128]), False)
                mm.then_inc(s["v_mm"], 1)

            def scores(n, u):
                g, hf, un = u // 2, u % 2, n * UNITS + u
                pi = n * GROUPS + g
                pe.wait_ge(s["sub_dve"], after(un))
                if hf == 0:
                    pe.wait_ge(s["place_act"], after(pi + 1))
                    pe.wait_ge(s["rotadd"], after(pi * 2 + 2))
                for wl in range(UW):
                    t0 = (hf * UW + wl) * WIN
                    at_ = 64 * slot(wl)
                    for a in range(2):
                        pe.matmul(bank[5][:, at_:at_ + 64],
                                       qbd[:, g % 2, a, hf * UW + wl].rearrange("p h t -> p (h t)"),
                                       kb[:, g % 2, a, t0:t0 + 2 * WIN],
                                  start=(a == 0 and wl == 0), stop=False)
                pe.matmul(bank[5][:, :], identb[:, :], maskb[:, 512 * (hf > 0):512 * (hf > 0) + 512],
                          start=False, stop=True).then_inc(s["s_mm"], 1)

            def turn(n, u):
                un = n * UNITS + u
                pe.wait_ge(s["norm_pool"], after(un + 1))
                pe.wait_ge(s["o1_out"], after(un))
                for j in range(4):
                    mm = pe.transpose(bank[6][:, 128 * j:128 * j + 128],
                                      probs[:, u % 2, 2 * j:2 * j + 2, :].rearrange("p w k -> p (w k)"), ident_s[:, :])
                mm.then_inc(s["t_mm"], 1)

            def attend(n, u):
                g, hf, un = u // 2, u % 2, n * UNITS + u
                pe.wait_ge(s["pt_out"], after(un + 1))
                pe.wait_ge(s["o0_out"], after(un))
                pe.wait_ge(s["v_out"], after((n * GROUPS + g) * 4 + 4))
                for pair in range(2):
                    for j in range(4):
                        for r in (0, 64):
                            mm = pe.matmul(bank[7 - r // 64][:, 256 * pair + 64 * j:256 * pair + 64 * j + 64],
                                           vb[r:r + 64, g % 2, 1 - j % 2, 2 * hf + j // 2, 128 * pair:128 * pair + 128],
                                           pts[r:r + 64, 128 * j + 64 * pair:128 * j + 64 * pair + 64],
                                           start=True, stop=True)
                            if pair == 1 and j == 3:
                                mm.then_inc(s["pv_mm"], 1)

            def project_out(n, ahead, ks):
                if ks[0] == 0:
                    pe.wait_ge(s["v_out"], after((n * GROUPS + GROUPS + (1 if ahead else 0)) * 4))
                    pe.wait_ge(s["o0_out"], after(n * UNITS + UNITS - 2))
                    pe.wait_ge(s["o1_out"], after(n * UNITS + UNITS - 2))
                else:
                    pe.wait_ge(s["o0_out"], after(n * UNITS + UNITS))
                    pe.wait_ge(s["o1_out"], after(n * UNITS + UNITS))
                for k in ks:
                    mm = pe.matmul(bank[4][:, :], wo_s[:, k, :], ot[:, k, :], start=(k == 0), stop=(k == 7))
                if ks[-1] == 7:
                    mm.then_inc(s["y_mm"], 1)

            def attention(n, ahead):
                for u in range(UNITS):
                    g1 = u // 2 + 1
                    pi = n * GROUPS + g1
                    more = g1 < GROUPS or ahead
                    scores(n, u)
                    if u % 2 == 0:
                        if more:
                            if g1 == GROUPS:
                                pe.wait_ge(s["xs_lo_dve"], after(n + 2))
                            project(pi, g1 % GROUPS, "q")
                            project(pi, g1 % GROUPS, "k")
                        if u:
                            turn(n, u - 1)
                        if more:
                            if g1 == 1:
                                pe.wait_ge(s["resid_dve"], after(n))
                            norms(pi, 0)
                        if u:
                            attend(n, u - 1)
                        if more:
                            norms(pi, 1)
                            values(pi, g1 % GROUPS, 0)
                    else:
                        if more:
                            values(pi, g1 % GROUPS, 1)
                        turn(n, u - 1)
                        if more:
                            values(pi, g1 % GROUPS, 2)
                        attend(n, u - 1)
                        if more:
                            values(pi, g1 % GROUPS, 3)
                turn(n, UNITS - 1)
                project_out(n, ahead, range(0, 6))
                attend(n, UNITS - 1)
                project_out(n, ahead, range(6, 8))

            def feed_forward(n, b):
                pe.wait_ge(s["ln_out"], after(PRE * B + n + 1))
                for j, (f0, fn) in enumerate(FT):
                    pe.wait_ge(s["gelu_act"], after(n * 3 + j))
                    pe.matmul(bank[j][0:fn, :], w1_s[:, FF + f0:FF + f0 + fn], xh[:, b, :],
                              start=True, stop=True).then_inc(s["fg_mm"], 1)
                    pe.wait_ge(s["hh_dve"], after(n * 3 + j))
                    pe.matmul(bank[3 + j][0:fn, :], w1_s[:, f0:f0 + fn], xh[:, b, :],
                              start=True, stop=True).then_inc(s["fa_mm"], 1)

            def feed_forward_out(n, b):
                for j, (f0, fn) in enumerate(FT):
                    pe.wait_ge(s["hh_dve"], after(n * 3 + j + 1))
                    mm = pe.matmul(bank[6 + b % 2][:, :], w2_s[0:fn, j, :], hh[0:fn, b % 2, j, :],
                                   start=(j == 0), stop=(j == 2))
                mm.then_inc(s["fy_mm"], 1)

            with pe.Fori(0, DEPTH) as layer:
                pe.wait_ge(s["split"], after(layer + 1))
                pe.wait_ge(wo_in, layer * 32 + 32)
                n0 = layer * B
                pe.wait_ge(s["xs_lo_dve"], after(n0 + 1))
                project(n0 * GROUPS, 0, "q")
                project(n0 * GROUPS, 0, "k")
                norms(n0 * GROUPS, 0)
                norms(n0 * GROUPS, 1)
                for c in range(4):
                    values(n0 * GROUPS, 0, c)
                with pe.Fori(0, B - 1) as b:
                    attention(layer * B + b, True)
                attention(layer * B + (B - 1), False)
                pe.wait_ge(ff_in, layer * 64 + 64)
                pe.wait_ge(s["xf0_dve"], after(layer + 1))
                for c in range(B):
                    pe.wait_ge(s["xf_act"], after(layer * B + c + 1))
                    pe.wait_ge(s["ln_xc"], after((PRE + layer) * B + c))
                    if c == 0:
                        pe.wait_ge(s["o1_out"], after(layer * B * UNITS + B * UNITS))
                    pe.matmul(bank[6][:, :], mean_s[:, :], xf[:, c, :], start=True, stop=True).then_inc(s["mean_mm"], 1)
                    if c > 0:
                        variance(PRE + layer, c - 1)
                variance(PRE + layer, B - 1)
                for b in range(B):
                    feed_forward(layer * B + b, b)
                    if b:
                        feed_forward_out(layer * B + b - 1, b - 1)
                feed_forward_out(layer * B + B - 1, B - 1)

            LAST = PRE + DEPTH
            pe.wait_ge(z["fin_sum"], B)
            layer_norm_static(LAST, lambda c: accv[:, c, :])
            pe.wait_ge(z["fin_in"], 160)
            for b in range(B):
                pe.wait_ge(s["ln_out"], after(LAST * B + b + 1))
                if b:
                    pe.wait_ge(z["g1_copy"], b)
                pe.matmul(bank[6][0:LR, :], gwg1_s, xn2[:, b, :], start=True, stop=True).then_inc(z["g1_mm"], 1)
                pe.matmul(bank[b % 2][:, :], gwv_s, xn2[:, b, :], start=True, stop=True).then_inc(z["gv_mm"], 1) \
                    if b < 2 else None
                if b >= 2:
                    pe.wait_ge(z["gv_copy"], b - 1)
                    pe.matmul(bank[b % 2][:, :], gwv_s, xn2[:, b, :], start=True, stop=True).then_inc(z["gv_mm"], 1)
                if b >= 2:
                    pe.wait_ge(z["gg_dve"], b - 1)
                pe.matmul(bank[2 + b % 2][:, :], gwg_s, xn2[:, b, :], start=True, stop=True).then_inc(z["gg_mm"], 1)
                pe.wait_ge(z["g1_copy"], b + 1)
                if b:
                    pe.wait_ge(z["z_copy"], b)
                pe.matmul(bank[7][0:64, :], gwg2_s[0:LR, :], g1s[0:LR, :], start=True, stop=True).then_inc(z["z_mm"], 1)
            pe.wait_ge(z["rep_made"], 3)
            pe.wait_ge(z["gv_copy"], B)
            pe.wait_ge(z["gg_dve"], B)
            for b in range(B):
                pe.wait_ge(z["egk_act"], b + 1)
                for i in range(DK):
                    t = b * DK + i
                    if t >= 2:
                        pe.wait_ge(z["kv_dve"], t - 1)
                    pe.matmul(bank[t % 2][:, :], wkrep[:, i], xn2[:, b, :], start=True, stop=True).then_inc(z["rk_mm"], 1)
                    if t >= 2:
                        pe.wait_ge(z["scan_dve"], t - 1)
                    pe.matmul(bank[2 + t % 2][:, :], selrep[0:64, i], egk[0:64, b, :], start=True, stop=True).then_inc(z["rg_mm"], 1)
                    if t >= 2:
                        pe.wait_ge(z["qs_dve"], t - 1)
                    pe.matmul(bank[4 + t % 2][:, :], wqrep[:, i], xn2[:, b, :], start=True, stop=True).then_inc(z["rq_mm"], 1)
            for b in range(B):
                pe.wait_ge(z["gsq_act"], b + 1)
                if b:
                    pe.wait_ge(z["gl_act"], b)
                pe.matmul(bank[6][:, :], blocks_s[:, :], kvb[:, b % 2, :], start=True, stop=True).then_inc(z["gms_mm"], 1)
                pe.wait_ge(z["gn_dve"], b + 1)
                if b:
                    pe.wait_ge(z["x1_dve"], b)
                pe.matmul(bank[7][:, :], gwo_s, go[:, b, :], start=True, stop=True).then_inc(z["go_mm"], 1)
            for b in range(B):
                pe.wait_ge(z["x1_dve"], b + 1)
                if b == 0:
                    pe.wait_ge(z["kv_dve"], B * DK)
                    pe.wait_ge(z["scan_dve"], B * DK)
                    pe.wait_ge(z["qs_dve"], B * DK)
                for m in range(4):
                    mm = pe.transpose(bank[b][:, 128 * m:128 * m + 128], accv[:, b, 128 * m:128 * m + 128], ident_s[:, :])
                mm.then_inc(z["tok_mm"], 1)
            for m in range(TILES):
                mm = pe.matmul(bank[4][:, 8 * m:8 * m + 8], xn2[:, m // 4, 128 * (m % 4):128 * (m % 4) + 128], rt_s,
                               start=True, stop=True)
            mm.then_inc(z["lg_mm"], 1)
            for t in range(8):
                if t >= 2:
                    pe.wait_ge(z["ew_copied"], t - 1)
                for j in range(4):
                    e, h = (4 * (t % 4) + j) // 2, (4 * (t % 4) + j) % 2
                    src = ew1_s[:, e, h, :] if t < 4 else ew2_s[:, e, 128 * h:128 * h + 128]
                    mm = pe.transpose(bank[6 + t % 2][:, 128 * j:128 * j + 128], src, ident_s[:, :])
                mm.then_inc(z["ew_turned"], 1)
            pe.wait_ge(z["ew_copied"], 8)
            pe.wait_ge(z["tok_copy"], B)

            def expert_out(t):
                q, e = t // E, t % E
                pe.wait_ge(z["eh_act"], 2 * t + 2)
                if t >= 2:
                    pe.wait_ge(z["ey_dve"], t - 1)
                for m in range(4):
                    for h in range(2):
                        mm = pe.matmul(bank[6 + t % 2][:, 128 * m:128 * m + 128], ht[:, t % 2, h, 128 * m:128 * m + 128],
                                       w2t[:, e, h, :], start=(h == 0), stop=(h == 1))
                mm.then_inc(z["ey_mm"], 1)

            for t in range(B * E):
                q, e = t // E, t % E
                for h in range(2):
                    if t >= 2:
                        pe.wait_ge(z["eh_act"], 2 * (t - 2) + h + 1)
                    pe.matmul(bank[2 * (t % 2) + h][:, :], w1t[:, e, 128 * h:128 * h + 128], xn2[:, q, :],
                              start=True, stop=True).then_inc(z["eh_mm"], 1)
                if t:
                    expert_out(t - 1)
            expert_out(B * E - 1)

        @block.scalar
        def _(act):
            for n in act_s.values():
                act.sem_inc(n, 1)
            eps, one, floor = consts[:, 0:1], consts[:, 1:2], consts[:, 2:3]

            def layer_norm(i):
                for c in range(B):
                    act.wait_ge(s["ln_xc"], after(i * B + c + 1))
                    act.wait_ge(s["var_mm"], after(i * B + c - 1)) if c >= 2 else None
                    act.activation(lsq[:, c % 2, :], xc[:, c, :], ACT.Square).then_inc(s["ln_sq"], 1)
                    if c > 0:
                        rstd(i, c - 1)
                rstd(i, B - 1)

            def rstd(i, c):
                act.wait_ge(s["var_mm"], after(i * B + c + 1))
                act.activation(lln[:, c % 2, :], bank[7][:, :], ACT.Ln, bias=eps).then_inc(s["ln_log"], 1)
                act.wait_ge(s["ln_log"], after(i * B + c + 1))
                if c >= 2:
                    act.wait_ge(s["ln_n"], after(i * B + c - 1))
                act.activation(lrs[:, c % 2, :], lln[:, c % 2, :], ACT.Exp, scale=-0.5).then_inc(s["ln_rstd"], 1)

            act.preload_act_table_set("natural_log_exp_and_others")
            for b in range(B):
                act.wait_ge(z["x_turned"], 1)
                act.activation(accv[:, b, :], bank[b][:, :], ACT.Copy).then_inc(z["x_copied"], 1)
            act.wait_ge(z["zeroed"], 1)
            layer_norm(0)
            layer_norm(1)
            for b in range(B):
                act.wait_ge(z["decay_arg"], b + 1)
                act.activation(args[:, :, :], args[:, :, :], ACT.Exp).then_inc(z["decay_exp"], 1)
                act.wait_ge(z["sum_scan"], b + 1)
                act.activation(pp, s_run, ACT.Ln).then_inc(z["log_sum"], 1)
                act.wait_ge(z["carry_arg"], b + 1)
                act.activation(args[:, :, :], args[:, :, :], ACT.Exp).then_inc(z["carry_exp"], 1)
                act.wait_ge(z["out_arg"], b + 1)
                act.activation(args[:, :, :], args[:, :, :], ACT.Exp).then_inc(z["out_exp"], 1)
                act.activation(rr, bank[2 + 3 * (b % 2)][:, :], ACT.Exp, scale=-1.0).then_inc(z["gate_exp"], 1)
            layer_norm(2)
            for b in range(B):
                act.wait_ge(z["cr_mm"], b + 1)
                if b:
                    act.wait_ge(z["cm_done"], b)
                act.activation(rr, bank[4][:, :], ACT.Exp, scale=-1.0).then_inc(z["cm_exp"], 1)

            def shifted_hi(n, b):
                act.wait_ge(s["v_mm"], after(n * 16))
                act.activation(xs_hi[0:64, WIN:], xv[0:64, b, :], ACT.Copy)
                act.activation(xs_hi[64:128, WIN + 1:], xv[64:128, b, 0:T - 1], ACT.Copy).then_inc(s["xs_hi_act"], 1)

            def squares(pi, k):
                act.wait_ge(s["q_mm" if k == 0 else "k_mm"], after(pi + 1))
                act.wait_ge(s["sqadd"], after(pi * 2))
                act.activation(sqb[:, k, 0, :], bank[2 * k][:, :], ACT.Square)
                act.activation(sqb[:, k, 1, :], bank[2 * k + 1][:, :], ACT.Square).then_inc(s["sq_act"], 1)

            def rnorm(pi, k):
                act.wait_ge(s["n2_mm"], after(pi * 2 + k + 1))
                act.activation(lnb[:, k, :], bank[4][:, :], ACT.Ln, bias=floor, scale=LN_SCALE).then_inc(s["log_act"], 1)
                act.wait_ge(s["log_act"], after(pi * 2 + k + 1))
                act.wait_ge(s["tab_dve"], after(pi * 2 + k))
                act.activation(rnb[:, k, :], lnb[:, k, :], ACT.Exp, bias=consts[:, 3:4], scale=-0.5).then_inc(s["rn_act"], 1)

            def place(pi, g):
                act.wait_ge(s["rotadd"], after(pi * 2 + 1))
                for h in range(GH):
                    rows = slice(HALF * h, HALF * h + HALF)
                    ins = act.activation(qbd[rows, g % 2, :, :, h, :],
                                         qst[rows].rearrange("p a (w t) -> p a w t", w=NW), ACT.Copy)
                ins.then_inc(s["place_act"], 1)

            def values_out(pi, g, c):
                act.wait_ge(s["v_mm"], after(pi * 4 + c + 1))
                act.activation(vb[:, g % 2, c // 2, 2 * (c % 2):2 * (c % 2) + 2, :],
                               bank[4][:, :].rearrange("p (m d) -> p m d", m=2), ACT.Copy).then_inc(s["v_out"], 1)

            def exponent(n, u):
                un = n * UNITS + u
                act.wait_ge(s["sub_dve"], after(un + 1))
                act.activation(probs[:, u % 2], probs[:, u % 2], ACT.Exp, scale=QK_SCALE).then_inc(s["exp_act"], 1)

            def turned_out(n, u):
                act.wait_ge(s["t_mm"], after(n * UNITS + u + 1))
                act.activation(pts, bank[6][:, :], ACT.Copy).then_inc(s["pt_out"], 1)

            def heads_out(n, u):
                act.wait_ge(s["pv_mm"], after((n * UNITS + u) * 2 + 2))
                for h in range(2):
                    mm = act.activation(head_windows(u, h, 1), own_part(6, h), ACT.Copy)
                mm.then_inc(s["o1_out"], 1)

            def attention(n, b, ahead):
                for u in range(UNITS):
                    g1 = u // 2 + 1
                    pi = n * GROUPS + g1
                    more = g1 < GROUPS or ahead
                    if u % 2 == 0:
                        if more and g1 == GROUPS:
                            shifted_hi(n + 1, b + 1)
                        if more:
                            squares(pi, 0)
                        exponent(n, u)
                        if more:
                            squares(pi, 1)
                        if u:
                            turned_out(n, u - 1)
                        if more:
                            rnorm(pi, 0)
                        if u:
                            heads_out(n, u - 1)
                        if more:
                            rnorm(pi, 1)
                            values_out(pi, g1 % GROUPS, 0)
                    else:
                        exponent(n, u)
                        if more:
                            place(pi, g1 % GROUPS)
                            values_out(pi, g1 % GROUPS, 1)
                        turned_out(n, u - 1)
                        if more:
                            values_out(pi, g1 % GROUPS, 2)
                        heads_out(n, u - 1)
                        if more:
                            values_out(pi, g1 % GROUPS, 3)
                turned_out(n, UNITS - 1)
                heads_out(n, UNITS - 1)

            with act.Fori(0, DEPTH) as layer:
                n0 = layer * B
                act.preload_act_table_set("natural_log_exp_and_others")
                act.wait_ge(s["fres_dve"], after(n0))
                shifted_hi(n0, 0)
                squares(n0 * GROUPS, 0)
                squares(n0 * GROUPS, 1)
                rnorm(n0 * GROUPS, 0)
                rnorm(n0 * GROUPS, 1)
                place(n0 * GROUPS, 0)
                for c in range(4):
                    values_out(n0 * GROUPS, 0, c)
                with act.Fori(0, B - 1) as b:
                    attention(layer * B + b, b, True)
                attention(layer * B + (B - 1), B - 1, False)
                act.wait_ge(s["y_mm"], after(n0 + B))
                for c in range(B):
                    act.wait_ge(s["resid_dve"], after(layer * B + c + 1))
                    act.activation(xf[0:64, c, :], xv[0:64, c, :], ACT.Copy)
                    act.activation(xf[64:128, c, 1:T], xv[64:128, c, 0:T - 1], ACT.Copy).then_inc(s["xf_act"], 1)
                i = PRE + layer
                layer_norm(i)
                act.preload_act_table_set("gelu_and_others")
                for b in range(B):
                    for j, (f0, fn) in enumerate(FT):
                        act.wait_ge(s["fg_mm"], after((layer * B + b) * 3 + j + 1))
                        if b >= 2:
                            act.wait_ge(s["hh_dve"], after((layer * B + b - 2) * 3 + j + 1))
                        act.activation(gg[0:fn, b % 2, j, :], bank[j][0:fn, :], ACT.Gelu,
                                       bias=lp[0:fn, L_B1G + j:L_B1G + j + 1]).then_inc(s["gelu_act"], 1)

            act.preload_act_table_set("natural_log_exp_and_others")
            layer_norm(PRE + DEPTH)
            act.wait_ge(z["fin_in"], 160)
            for dst, src, sc in ((wkrep, gwk_s, 1.0), (wqrep, gwq_s, float(DK) ** -0.5)):
                act.activation(dst, src.rearrange("p (h i) -> p i h", h=NH)[:, :, :, None].to_broadcast([128, DK, NH, DV]),
                               ACT.Copy, scale=sc).then_inc(z["rep_made"], 1)
            act.activation(selrep[0:64], ident_s[0:64, 0:64].rearrange("p (h i) -> p i h", h=NH)[:, :, :, None]
                           .to_broadcast([64, DK, NH, DV]), ACT.Copy).then_inc(z["rep_made"], 1)
            for b in range(B):
                act.wait_ge(z["gv_mm"], b + 1)
                act.activation(vt[:, b, :], bank[b % 2][:, :], ACT.Copy).then_inc(z["gv_copy"], 1)
                act.wait_ge(z["gg_mm"], b + 1)
                act.activation(gs[:, b, :], bank[2 + b % 2][:, :], ACT.Exp, scale=-1.0).then_inc(z["gg_exp"], 1)
                act.wait_ge(z["z_copy"], b + 1)
                if b:
                    act.wait_ge(z["gk_dve"], b)
                act.activation(az[0:64, 0, :], zb[0:64, :], ACT.Abs).then_inc(z["abs_act"], 1)
                act.wait_ge(z["abs_act"], b + 1)
                act.activation(az[0:64, 1, :], az[0:64, 0, :], ACT.Exp, scale=-1.0).then_inc(z["gexp_act"], 1)
                act.wait_ge(z["gexp_act"], b + 1)
                act.activation(az[0:64, 0, :], az[0:64, 1, :], ACT.Ln, bias=one[0:64]).then_inc(z["gln_act"], 1)
                act.wait_ge(z["gk_dve"], b + 1)
                act.activation(egk[0:64, b, :], egk[0:64, b, :], ACT.Exp, scale=1.0 / GATE_NORM).then_inc(z["egk_act"], 1)
            for b in range(B):
                act.wait_ge(z["oadd"], DK * (b + 1))
                if b >= 2:
                    act.wait_ge(z["gms_mm"], b - 1)
                act.wait_ge(z["scan_dve"], B * DK)
                act.activation(kvb[:, b % 2, :], go[:, b, :], ACT.Square).then_inc(z["gsq_act"], 1)
                act.wait_ge(z["gms_mm"], b + 1)
                act.activation(az[:, 0, :], bank[6][:, :], ACT.Ln, bias=eps, scale=1.0 / DV).then_inc(z["gl_act"], 1)
                act.wait_ge(z["gl_act"], b + 1)
                if b:
                    act.wait_ge(z["gn_dve"], b)
                act.activation(az[:, 1, :], az[:, 0, :], ACT.Exp, scale=-0.5).then_inc(z["gr_act"], 1)
            for b in range(B):
                act.wait_ge(z["tok_mm"], b + 1)
                act.activation(otok[:, 4 * b:4 * b + 4, :], bank[b][:, :].rearrange("p (m c) -> p m c", c=C), ACT.Copy) \
                   .then_inc(z["tok_copy"], 1)
            act.wait_ge(z["lg_mm"], 1)
            act.activation(lg, bank[4][:, 0:128].rearrange("p (m e) -> p m e", e=8), ACT.Copy).then_inc(z["lg_copy"], 1)
            for t in range(8):
                act.wait_ge(z["ew_turned"], t + 1)
                dst = w1t[:, 2 * t:2 * t + 2, :] if t < 4 else w2t[:, 2 * (t - 4):2 * (t - 4) + 2, :, :]
                src = bank[6 + t % 2][:, :]
                src = src.rearrange("p (e f) -> p e f", e=2) if t < 4 else src.rearrange("p (e h c) -> p e h c", e=2, h=2)
                act.activation(dst, src, ACT.Copy).then_inc(z["ew_copied"], 1)
            act.wait_ge(z["route"], 1)
            act.activation(gw12[:, 0, :], gw12[:, 0, :], ACT.Exp).then_inc(z["route"], 1)
            act.preload_act_table_set("gelu_and_others")
            for t in range(B * E):
                for h in range(2):
                    act.wait_ge(z["eh_mm"], 2 * t + h + 1)
                    if t >= 2:
                        act.wait_ge(z["ey_mm"], t - 1)
                    act.activation(ht[:, t % 2, h, :], bank[2 * (t % 2) + h][:, :], ACT.Gelu).then_inc(z["eh_act"], 1)

        @block.vector
        def _(dve):
            for n in dve_s.values():
                dve.sem_inc(n, 1)
            dve.sem_inc(s["tab_dve"], 1)
            dve.sem_inc(s["mul_dve"], 1)
            count = [0]

            def link(ins):
                count[0] += 1
                ins.then_inc(z["dve_link"], 1)
                dve.wait_ge(z["dve_link"], count[0])

            def layer_norm(i, src, dst, gain=None, bias=None):
                for c in range(B):
                    dve.wait_ge(s["mean_mm"], after(i * B + c + 1))
                    dve.tensor_tensor(xc[:, c, :], src(c), bank[6][:, :], ALU.subtract).then_inc(s["ln_xc"], 1)
                    if c > 1:
                        normed(i, c - 2, dst, gain, bias)
                normed(i, B - 2, dst, gain, bias)
                normed(i, B - 1, dst, gain, bias)

            def normed(i, c, dst, gain, bias):
                dve.wait_ge(s["ln_rstd"], after(i * B + c + 1))
                if gain is None:
                    dve.tensor_tensor(dst(c), xc[:, c, :], lrs[:, c % 2, :], ALU.mult).then_inc(s["ln_out"], 1)

                    return
                dve.tensor_tensor(xc[:, c, :], xc[:, c, :], lrs[:, c % 2, :], ALU.mult).then_inc(s["ln_n"], 1)
                dve.wait_ge(s["ln_n"], after(i * B + c + 1))
                dve.tensor_scalar(dst(c), xc[:, c, :], gain, bias, ALU.mult, ALU.add).then_inc(s["ln_out"], 1)

            def col(k, rows=128):
                return par[0:rows, k:k + 1]

            dve.memset(mean_s[:, :], 1.0 / C)
            dve.memset(consts[:, 0:1], EPS)
            dve.memset(consts[:, 1:2], 1.0)
            dve.memset(consts[:, 2:3], 6e-20)
            dve.memset(consts[:, 3:4], 6.931471805599453)
            dve.memset(hb[:, :, 0:1], 0.0)
            dve.memset(h2b[:, :, 0:1], 0.0)
            dve.memset(m_run[:, 0:1], NEG_INF)
            dve.memset(s_run[:, 0:1], 1.0)
            dve.memset(a_run[:, 0:1], 0.0)
            dve.memset(wfull, 0.0).then_inc(z["zeroed"], 1)
            dve.wait_ge(z["zeroed"], 1)
            dve.wait_ge(z["x_copied"], B)
            dve.wait_ge(z["const_in"], 64)
            dve.tensor_copy(identb[:, :], ident_s[:, :])
            dve.tensor_copy(maskb[:, :], maskf)
            layer_norm(0, lambda c: accv[:, c, :], lambda c: xv[:, c, :], 1.0, 0.0)
            link(dve.tensor_scalar(wfull, wfull, col(P_W), None, ALU.add))
            dve.wait_ge(z["tm_in"], 96)
            link(dve.tensor_scalar(om[:, 0:5], par[:, P_MK:P_CR + 1], -1.0, 1.0, ALU.mult, ALU.add))
            for j, k in ((0, 0), (1, 1), (2, 2), (3, 4)):
                src = traw[:, j * C:(j + 1) * C]
                dve.tensor_scalar(tmix[:, 0, j * C:(j + 1) * C], src, col(P_MK + k), None, ALU.mult)
                dve.tensor_scalar(tmix[:, 1, j * C:(j + 1) * C], src, om[:, k:k + 1], None, ALU.mult)
            link(dve.tensor_scalar(tmix[:, 1, 4 * C:8 * C], tmix[:, 0, 4 * C:8 * C], om[:, 3:4], None, ALU.mult))
            dve.tensor_scalar(tmix[:, 0, 4 * C:8 * C], tmix[:, 0, 4 * C:8 * C], col(P_CK), None, ALU.mult).then_inc(z["mixed"], 1)
            dve.wait_ge(s["ln_out"], after(B))
            layer_norm(1, lambda c: xv[:, c, :], lambda c: hb[:, c, 1:T + 1], col(P_G1), col(P_B1))

            for b in range(B):
                k_ps, v_ps = bank[3 * (b % 2)][:, :], bank[3 * (b % 2) + 1][:, :]
                now = slice(1, T + 1)
                old = slice(0, T)
                dve.wait_ge(z["kvr_mm"], b + 1)
                link(dve.tensor_scalar(kw, k_ps, col(P_W), None, ALU.add))
                link(dve.tensor_tensor_scan(m_run[:, now], wfull, kw, m_run[:, 0:1], ALU.add, ALU.max))
                dve.scalar_tensor_tensor(args[:, 0, :], m_run[:, old], col(P_W), m_run[:, now], ALU.add, ALU.subtract)
                dve.tensor_tensor(args[:, 1, :], kw, m_run[:, now], ALU.subtract).then_inc(z["decay_arg"], 1)
                dve.wait_ge(z["decay_exp"], b + 1)
                dve.tensor_tensor_scan(s_run[:, now], args[:, 0, :], args[:, 1, :], 0.0, ALU.mult, ALU.add) \
                   .then_inc(z["sum_scan"], 1)
                dve.wait_ge(z["log_sum"], b + 1)
                link(dve.tensor_tensor(pp, pp, m_run, ALU.add))
                link(dve.tensor_tensor(kmx, k_ps, pp[:, old], ALU.max))
                dve.tensor_tensor(args[:, 0, :], pp[:, old], kmx, ALU.subtract)
                dve.tensor_tensor(args[:, 1, :], k_ps, kmx, ALU.subtract).then_inc(z["carry_arg"], 1)
                dve.wait_ge(z["carry_exp"], b + 1)
                link(dve.tensor_tensor(bv, v_ps, args[:, 1, :], ALU.mult))
                link(dve.tensor_tensor_scan(a_run[:, now], args[:, 0, :], bv, 0.0, ALU.mult, ALU.add))
                link(dve.scalar_tensor_tensor(kmx, k_ps, col(P_U), pp[:, old], ALU.add, ALU.max))
                dve.tensor_tensor(args[:, 0, :], pp[:, old], kmx, ALU.subtract)
                dve.scalar_tensor_tensor(args[:, 1, :], k_ps, col(P_U), kmx, ALU.add, ALU.subtract).then_inc(z["out_arg"], 1)
                dve.wait_ge(z["out_exp"], b + 1)
                dve.tensor_tensor(kw, args[:, 0, :], a_run[:, old], ALU.mult)
                dve.tensor_tensor(bv, v_ps, args[:, 1, :], ALU.mult)
                link(dve.tensor_tensor(kmx, args[:, 0, :], args[:, 1, :], ALU.add))
                link(dve.tensor_tensor(kw, kw, bv, ALU.add))
                dve.wait_ge(z["gate_exp"], b + 1)
                link(dve.scalar_tensor_tensor(bv, rr, 1.0, kmx, ALU.add, ALU.mult))
                link(dve.reciprocal(bv, bv))
                link(dve.tensor_tensor(kw, kw, bv, ALU.mult))
                link(dve.tensor_tensor(rwx[:, b, :], kw, xv[:, b, :], ALU.add))
                dve.sem_inc(z["k_free"], 1)
                dve.sem_inc(z["b1_done"], 1)
            layer_norm(2, lambda c: rwx[:, c, :], lambda c: h2b[:, c, 1:T + 1], col(P_G2), col(P_B2))
            for b in range(B):
                for j in range(4):
                    dve.wait_ge(z["ck_mm"], 4 * b + j + 1)
                    if b:
                        dve.wait_ge(z["cv_mm"], b)
                    link(dve.tensor_scalar(args[:, j % 2, :], bank[j][:, :], 0.0, None, ALU.max))
                    dve.tensor_tensor(kkb[:, j, :], args[:, j % 2, :], bank[j][:, :], ALU.mult).then_inc(z["kk_dve"], 1)
                dve.wait_ge(z["cm_exp"], b + 1)
                link(dve.tensor_scalar(bv, rr, 1.0, None, ALU.add))
                link(dve.reciprocal(bv, bv))
                dve.wait_ge(z["cv_mm"], b + 1)
                link(dve.tensor_tensor(bv, bank[5][:, :], bv, ALU.mult))
                link(dve.tensor_tensor(bv, bv, rwx[:, b, :], ALU.add))
                link(dve.tensor_tensor(accv[:, b, :], accv[:, b, :], bv, ALU.add))
                dve.sem_inc(z["cm_done"], 1)

            dve.memset(qbd[:, 0], 0.0)
            dve.memset(qbd[:, 1], 0.0)
            dve.memset(kb[:, :, :, 0:WIN], 0.0)
            for w in (xs_hi, xs_lo):
                dve.memset(w[:, 0:WIN].bitcast(F32), 0.0)
                ins = dve.memset(w[64:128, WIN:WIN + 1].bitcast(F32), 0.0)
            link(ins)
            dve.wait_ge(z["rot_in"], 16)

            def shifted_lo(n, b):
                dve.wait_ge(s["xs_hi_act"], after(n + 1))
                dve.tensor_tensor(xs_lo[0:64, WIN:], xv[0:64, b, :], xs_hi[0:64, WIN:].bitcast(F32), ALU.subtract)
                dve.tensor_tensor(xs_lo[64:128, WIN + 1:], xv[64:128, b, 0:T - 1], xs_hi[64:128, WIN + 1:].bitcast(F32),
                                  ALU.subtract).then_inc(s["xs_lo_dve"], 1)

            def rotation(pi, k):
                dve.wait_ge(s["rn_act"], after(pi * 2 + k + 1))
                dve.wait_ge(s["mul_dve"], after(pi * 2 + k + 1))
                dve.scalar_tensor_tensor(tab[:, 0, :], rnb[:, k, :], RN_MAX, rot_s[:, 2 * k, :], ALU.min, ALU.mult)
                dve.scalar_tensor_tensor(tab[:, 1, :], rnb[:, k, :], RN_MAX, rot_s[:, 2 * k + 1, :], ALU.min, ALU.mult) \
                   .then_inc(s["tab_dve"], 1)
                dve.wait_ge(s["tab_dve"], after(pi * 2 + k + 2))
                dve.wait_ge(s["rotadd"], after(pi * 2 + k))
                for o, a, t in ((0, 0, 0), (1, 1, 1), (2, 1, 0), (3, 0, 1)):
                    ins = dve.scalar_tensor_tensor(t4[:, o, :], bank[2 * k + a][:, :], lp[:, 2 * k + a:2 * k + a + 1],
                                                   tab[:, t, :], ALU.mult, ALU.mult)
                ins.then_inc(s["mul_dve"], 1)

            def maximum(n, u):
                un = n * UNITS + u
                sc = bank[5][:, :].rearrange("p (w k) -> p w k", w=UW)
                dve.wait_ge(s["s_mm"], after(un + 1))
                dve.tensor_reduce(mx[:, u % 2, :], sc, AX, ALU.max).then_inc(s["max_dve"], 1)
                dve.wait_ge(s["max_dve"], after(un + 1))
                dve.tensor_tensor(probs[:, u % 2], sc, mx[:, u % 2, :, None].to_broadcast([128, UW, 2 * WIN]),
                                  ALU.subtract).then_inc(s["sub_dve"], 1)

            def sums(n, u):
                un = n * UNITS + u
                dve.wait_ge(s["exp_act"], after(un + 1))
                dve.tensor_reduce(sm[:, u % 2, :], probs[:, u % 2], AX, ALU.add).then_inc(s["sum_dve"], 1)
                dve.wait_ge(s["sum_dve"], after(un + 1))
                dve.reciprocal(rc[:, u % 2, :], sm[:, u % 2, :]).then_inc(s["rec_dve"], 1)

            def heads_out(n, u):
                dve.wait_ge(s["pv_mm"], after((n * UNITS + u) * 2 + 1))
                for h in range(2):
                    ins = dve.tensor_copy(head_windows(u, h, 0), own_part(7, h))
                ins.then_inc(s["o0_out"], 1)

            def attention(n, b, ahead):
                for u in range(UNITS):
                    g1 = u // 2 + 1
                    pi = n * GROUPS + g1
                    more = g1 < GROUPS or ahead
                    if u % 2 == 0 and more and g1 == GROUPS:
                        shifted_lo(n + 1, b + 1)
                    maximum(n, u)
                    if u % 2 == 0:
                        sums(n, u)
                        if more:
                            rotation(pi, 0)
                        if u:
                            heads_out(n, u - 1)
                    else:
                        if more:
                            rotation(pi, 1)
                        sums(n, u)
                        heads_out(n, u - 1)
                heads_out(n, UNITS - 1)
                dve.wait_ge(s["y_mm"], after(n + 1))
                dve.tensor_tensor(xv[:, b, :], xv[:, b, :], bank[4][:, :], ALU.add).then_inc(s["resid_dve"], 1)

            with dve.Fori(0, DEPTH) as layer:
                n0 = layer * B
                dve.wait_ge(wo_in, layer * 32 + 32)
                shifted_lo(n0, 0)
                rotation(n0 * GROUPS, 0)
                rotation(n0 * GROUPS, 1)
                with dve.Fori(0, B - 1) as b:
                    attention(layer * B + b, b, True)
                attention(layer * B + (B - 1), B - 1, False)
                dve.wait_ge(ff_in, layer * 64 + 64)
                dve.memset(xf[64:128, :, 0:1], 0.0).then_inc(s["xf0_dve"], 1)
                dve.wait_ge(s["xf0_dve"], after(layer + 1))
                layer_norm(PRE + layer, lambda c: xf[:, c, :], lambda c: xh[:, c, :],
                           lp[:, L_G:L_G + 1], lp[:, L_B:L_B + 1])

                def result(b):
                    n = layer * B + b
                    dve.wait_ge(s["fy_mm"], after(n + 1))
                    dve.scalar_tensor_tensor(xv[:, b, :], bank[6 + b % 2][:, :], lp[:, L_B2:L_B2 + 1], xv[:, b, :],
                                             ALU.add, ALU.add).then_inc(s["fres_dve"], 1)

                for b in range(B):
                    for j, (f0, fn) in enumerate(FT):
                        f = (layer * B + b) * 3 + j
                        dve.wait_ge(s["gelu_act"], after(f + 1))
                        dve.wait_ge(s["fa_mm"], after(f + 1))
                        if b >= 2:
                            dve.wait_ge(s["fy_mm"], after(layer * B + b - 1))
                        dve.scalar_tensor_tensor(hh[0:fn, b % 2, j, :], bank[3 + j][0:fn, :],
                                                 lp[0:fn, L_B1A + j:L_B1A + j + 1], gg[0:fn, b % 2, j, :],
                                                 ALU.add, ALU.mult).then_inc(s["hh_dve"], 1)
                    if b:
                        result(b - 1)
                result(B - 1)

            dve.wait_ge(s["fres_dve"], after(DEPTH * B))
            for b in range(B):
                dve.tensor_tensor(accv[:, b, :], accv[:, b, :], xv[:, b, :], ALU.add).then_inc(z["fin_sum"], 1)
            dve.wait_ge(z["fin_sum"], B)
            layer_norm(PRE + DEPTH, lambda c: accv[:, c, :], lambda c: xn2[:, c, :], 1.0, 0.0)
            for b in range(B):
                dve.wait_ge(z["g1_mm"], b + 1)
                if b:
                    dve.wait_ge(z["z_mm"], b)
                dve.tensor_copy(g1s[0:LR, :], bank[6][0:LR, :]).then_inc(z["g1_copy"], 1)
                dve.wait_ge(z["gg_exp"], b + 1)
                link(dve.tensor_scalar(gs[:, b, :], gs[:, b, :], 1.0, None, ALU.add))
                link(dve.reciprocal(gs[:, b, :], gs[:, b, :]))
                dve.scalar_tensor_tensor(gs[:, b, :], bank[2 + b % 2][:, :], col(P_GW), gs[:, b, :], ALU.mult, ALU.mult) \
                   .then_inc(z["gg_dve"], 1)
                dve.wait_ge(z["z_mm"], b + 1)
                if b:
                    dve.wait_ge(z["abs_act"], b)
                dve.tensor_scalar(zb[0:64, :], bank[7][0:64, :], col(P_BGK, 64), None, ALU.add).then_inc(z["z_copy"], 1)
                dve.wait_ge(z["z_copy"], b + 1)
                dve.wait_ge(z["gln_act"], b + 1)
                dve.scalar_tensor_tensor(egk[0:64, b, :], zb[0:64, :], 0.0, az[0:64, 0, :], ALU.min, ALU.subtract) \
                   .then_inc(z["gk_dve"], 1)

            N = B * DK

            def kv(t):
                dve.wait_ge(z["rk_mm"], t + 1)
                if t >= 2:
                    dve.wait_ge(z["scan_dve"], t - 1)
                dve.tensor_tensor(kvb[:, t % 2, :], bank[t % 2][:, :], vt[:, t // DK, :], ALU.mult).then_inc(z["kv_dve"], 1)

            def scan(t):
                dve.wait_ge(z["rg_mm"], t + 1)
                dve.wait_ge(z["kv_dve"], t + 1)
                if t >= 2:
                    dve.wait_ge(z["qs_dve"], t - 1)
                dve.tensor_tensor_scan(sst[:, t % 2, :], bank[2 + t % 2][:, :], kvb[:, t % 2, :], 0.0, ALU.mult, ALU.add) \
                   .then_inc(z["scan_dve"], 1)

            def qs(t):
                dve.wait_ge(z["rq_mm"], t + 1)
                dve.wait_ge(z["scan_dve"], t + 1)
                if t >= 2:
                    dve.wait_ge(z["oadd"], t - 1)
                dve.tensor_tensor(tmp[:, t % 2, :], bank[4 + t % 2][:, :], sst[:, t % 2, :], ALU.mult).then_inc(z["qs_dve"], 1)

            for t in range(N + 2):
                if t < N:
                    kv(t)
                if 1 <= t <= N:
                    scan(t - 1)
                if t >= 2:
                    qs(t - 2)
            for b in range(B):
                dve.wait_ge(z["gr_act"], b + 1)
                link(dve.tensor_tensor(go[:, b, :], go[:, b, :], az[:, 1, :], ALU.mult))
                dve.tensor_tensor(go[:, b, :], go[:, b, :], gs[:, b, :], ALU.mult).then_inc(z["gn_dve"], 1)
                dve.wait_ge(z["go_mm"], b + 1)
                dve.tensor_tensor(accv[:, b, :], accv[:, b, :], bank[7][:, :], ALU.add).then_inc(z["x1_dve"], 1)
            dve.wait_ge(z["lg_copy"], 1)
            for m in range(TILES):
                ins = dve.max(top8[:, m, :], lg[:, m, :])
            link(ins)
            for m in range(TILES):
                ins = dve.max_index(topi[:, 8 * m:8 * m + 8], top8[:, m, :], lg[:, m, :])
            link(ins)
            dve.tensor_copy(topf, topi[:, :].rearrange("p (m e) -> p m e", e=8))
            dve.tensor_tensor(gw12[:, 0, :], top8[:, :, 1], top8[:, :, 0], ALU.subtract).then_inc(z["route"], 1)
            dve.wait_ge(z["route"], 2)
            link(dve.tensor_scalar(gw12[:, 1, :], gw12[:, 0, :], 1.0, None, ALU.add))
            link(dve.reciprocal(gw12[:, 1, :], gw12[:, 1, :]))
            link(dve.tensor_tensor(gw12[:, 2, :], gw12[:, 0, :], gw12[:, 1, :], ALU.mult))
            dve.wait_ge(z["iota_pool"], 8)

            def of_expert(x):
                return x[:, :, None].to_broadcast([128, TILES, 8])

            each = iot[:, None, :].to_broadcast([128, TILES, 8])
            dve.tensor_tensor(gate, each, topf[:, :, 0:1].to_broadcast([128, TILES, 8]), ALU.is_equal)
            link(dve.tensor_tensor(gpart, each, topf[:, :, 1:2].to_broadcast([128, TILES, 8]), ALU.is_equal))
            dve.tensor_tensor(gate, gate, of_expert(gw12[:, 1, :]), ALU.mult)
            link(dve.tensor_tensor(gpart, gpart, of_expert(gw12[:, 2, :]), ALU.mult))
            link(dve.tensor_tensor(gate, gate, gpart, ALU.add))
            dve.wait_ge(z["tok_copy"], B)
            for t in range(B * E):
                q, e = t // E, t % E
                dve.wait_ge(z["ey_mm"], t + 1)
                if e:
                    dve.wait_ge(z["ey_dve"], t)
                for m in range(4):
                    tile = 4 * q + m
                    ins = dve.scalar_tensor_tensor(otok[:, tile, :], bank[6 + t % 2][:, 128 * m:128 * m + 128],
                                                   gate[:, tile, e:e + 1], otok[:, tile, :], ALU.mult, ALU.add)
                ins.then_inc(z["ey_dve"], 1)

        @block.gpsimd
        def _(pool):
            for n in pool_s.values():
                pool.sem_inc(n, 1)

            def square_sum(pi, k):
                pool.wait_ge(s["sq_act"], after(pi * 2 + k + 1))
                pool.tensor_tensor(sqs[:, k, :], sqb[:, k, 0, :], sqb[:, k, 1, :], ALU.add).then_inc(s["sqadd"], 1)

            def rotate(pi, g, k):
                pool.wait_ge(s["mul_dve"], after(pi * 2 + k + 2))
                dst = qst if k == 0 else kb[:, g % 2, :, WIN:]
                pool.tensor_tensor(dst[:, 0, :], t4[:, 0, :], t4[:, 1, :], ALU.subtract)
                pool.tensor_tensor(dst[:, 1, :], t4[:, 2, :], t4[:, 3, :], ALU.add).then_inc(s["rotadd"], 1)

            def normalise(n, u):
                pool.wait_ge(s["rec_dve"], after(n * UNITS + u + 1))
                pool.tensor_tensor(probs[:, u % 2], probs[:, u % 2],
                                   rc[:, u % 2, :, None].to_broadcast([128, UW, 2 * WIN]), ALU.mult) \
                    .then_inc(s["norm_pool"], 1)

            def attention(n, ahead):
                for u in range(UNITS):
                    g1 = u // 2 + 1
                    pi = n * GROUPS + g1
                    more = g1 < GROUPS or ahead
                    if u % 2 == 0:
                        if more:
                            square_sum(pi, 0)
                            square_sum(pi, 1)
                        normalise(n, u)
                        if more:
                            rotate(pi, g1 % GROUPS, 0)
                    else:
                        if more:
                            rotate(pi, g1 % GROUPS, 1)
                        normalise(n, u)

            with pool.Fori(0, DEPTH) as layer:
                n0 = layer * B
                pool.wait_ge(z["zeroed"], 1)
                pool.wait_ge(wqkv_in, layer * 16 + 16)
                pool.wait_ge(s["v_mm"], after(n0 * 16))

                def halves(w, p, a):
                    return w[:, p * INNER:(p + 1) * INNER].rearrange("p (g a h d) -> p g a h d", g=GROUPS, a=2, h=GH)[:, :, a]

                def whole(w, p, a):
                    return w[:, p * INNER:(p + 1) * INNER].rearrange("p (g h a d) -> p g h a d", g=GROUPS, a=2, h=GH)[:, :, :, a]

                for p in range(2):
                    for a in range(2):
                        pool.tensor_tensor(halves(wq_hi[:, :], p, a), whole(wraw, p, a),
                                           consts[:, 1:2, None, None].to_broadcast([128, GROUPS, GH, HALF]), ALU.mult)
                pool.tensor_tensor(wq_hi[:, 2 * INNER:], wraw[:, 2 * INNER:], consts[:, 1:2].to_broadcast([128, INNER]), ALU.mult) \
                    .then_inc(s["split_hi"], 1)
                pool.wait_ge(s["split_hi"], after(layer + 1))
                for p in range(2):
                    for a in range(2):
                        pool.tensor_tensor(halves(wq_lo[:, :], p, a), whole(wraw, p, a),
                                           halves(wq_hi[:, :].bitcast(F32), p, a), ALU.subtract)
                pool.tensor_tensor(wq_lo[:, 2 * INNER:], wraw[:, 2 * INNER:], wq_hi[:, 2 * INNER:].bitcast(F32),
                                   ALU.subtract).then_inc(s["split"], 1)
                square_sum(n0 * GROUPS, 0)
                square_sum(n0 * GROUPS, 1)
                rotate(n0 * GROUPS, 0, 0)
                rotate(n0 * GROUPS, 0, 1)
                with pool.Fori(0, B - 1) as b:
                    attention(layer * B + b, True)
                attention(layer * B + (B - 1), False)

            pool.wait_ge(s["fres_dve"], after(DEPTH * B))
            for e in range(E):
                pool.memset(iot[:, e:e + 1], float(e)).then_inc(z["iota_pool"], 1)
            for t in range(B * DK):
                b = t // DK
                pool.wait_ge(z["qs_dve"], t + 1)
                if t % DK == 0:
                    pool.tensor_copy(go[:, b, :], tmp[:, t % 2, :]).then_inc(z["oadd"], 1)
                else:
                    pool.wait_ge(z["oadd"], t)
                    pool.tensor_tensor(go[:, b, :], go[:, b, :], tmp[:, t % 2, :], ALU.add).then_inc(z["oadd"], 1)


def rotary():
    import numpy as np
    f = np.float32
    half = np.arange(0, DH, 2, dtype=f)
    inv_freq = (1.0 / f(10000.0) ** (half / f(DH))).astype(f)
    t = np.arange(T, dtype=f)
    freqs = (t[:, None] * inv_freq[None, :]).astype(f)
    base = ((half + f(0.4 * DH)) / f(1.4 * DH)).astype(f)
    power = ((t - f(T // 2)) / f(WIN // 2)).astype(f)
    scale = (base[None, :] ** power[:, None]).astype(f)
    cos, sin = np.cos(freqs), np.sin(freqs)
    tabs = np.stack([cos * scale, sin * scale, cos * (1 / scale), sin * (1 / scale)]).astype(f)
    return np.ascontiguousarray(np.tile(tabs.transpose(2, 0, 1), (GH, 1, 1)))


def masks():
    import numpy as np
    q = np.arange(128)[:, None] % WIN
    k = np.arange(2 * WIN)[None, :]
    seen = np.where(k < WIN, q <= k, q >= k - WIN)
    m = np.where(seen, 0.0, -1e30)
    unit = np.tile(m, (1, UW))
    first = unit.copy()
    first[:, 0:WIN] = -1e30
    return np.concatenate([first, unit], axis=1).astype(np.float32)


def kernel(**inputs):
    import numpy as np
    import concourse.bacc as bacc
    from concourse.bass_utils import run_bass_kernel_spmd as run

    a = {k: np.ascontiguousarray(v) for k, v in inputs.items()}

    def column(v):
        v = v.reshape(-1)
        return np.concatenate([v, np.zeros(128 - v.size, v.dtype)])

    p0 = "L0_attn_"
    params = np.stack([column(v) for v in (
        a[p0 + "time_decay"], a[p0 + "time_first"], a[p0 + "ln1_g"], a[p0 + "ln1_b"], a[p0 + "ln2_g"], a[p0 + "ln2_b"],
        a[p0 + "mix_k"], a[p0 + "mix_v"], a[p0 + "mix_r"], a[p0 + "cmix_k"], a[p0 + "cmix_r"],
        np.tile(a["L1_attn_gw"], NH), a["L1_attn_bgk2"])], axis=1)
    f0 = "L0_ffn_"
    lparams = []
    for i in range(DEPTH):
        q, k, b1 = a[f0 + "q_scale"][i], a[f0 + "k_scale"][i], a[f0 + "b1"][i]
        cols = [np.tile(q[:HALF], GH), np.tile(q[HALF:], GH), np.tile(k[:HALF], GH), np.tile(k[HALF:], GH),
                a[f0 + "ln_g"][i], a[f0 + "ln_b"][i]]
        cols += [column(b1[s:s + n]) for s, n in FT] + [column(b1[FF + s:FF + s + n]) for s, n in FT]
        cols.append(a[f0 + "b2"][i])
        lparams.append(np.stack(cols, axis=1))
    arrays = {
        "x": a["L0_attn_x"], "params": params, "lparams": np.stack(lparams),
        "w_tk": a[p0 + "w_tk"], "w_tv": a[p0 + "w_tv"], "w_tr": a[p0 + "w_tr"], "w_ck": a[p0 + "w_ck"],
        "w_cv": a[p0 + "w_cv"], "w_cr": a[p0 + "w_cr"],
        "wqkv": a[f0 + "Wqkv"], "wo": a[f0 + "Wo"], "w1": a[f0 + "W1"], "w2": a[f0 + "W2"],
        "gwq": a["L1_attn_Wq"], "gwk": a["L1_attn_Wk"], "gwv": a["L1_attn_Wv"], "gwg1": a["L1_attn_Wgk1"],
        "gwg2": a["L1_attn_Wgk2"], "gwg": a["L1_attn_Wg"], "gwo": a["L1_attn_Wo"],
        "router_t": a["L1_ffn_router_w"].T, "ew1": a["L1_ffn_w1"], "ew2": a["L1_ffn_w2"],
        "rot": rotary(), "blocks": np.kron(np.eye(4), np.ones((32, 32))).astype(np.float32),
        "ident": np.eye(128, dtype=np.float32), "mask": masks(),
    }
    nc = bacc.Bacc("TRN2", target_bir_lowering=False, num_devices=1)
    data, args = {}, []
    for name, v in arrays.items():
        v = np.ascontiguousarray(v)
        data[f"in_{name}"] = v
        args.append(nc.dram_tensor(f"in_{name}", v.shape, mybir.dt.from_np(v.dtype), kind="ExternalInput").ap())
    out = nc.dram_tensor("out_0", (B, T, C), F32, kind="ExternalOutput").ap()
    program(nc, *args, out)
    r = run(nc, [data], core_ids=[0])
    return r.results[0]["out_0"]
```

```python
from contextlib import ExitStack

import concourse.bass as bass
from concourse import mybir

F32 = mybir.dt.float32
F32R = mybir.dt.float32r
BF16 = mybir.dt.bfloat16
ALU = mybir.AluOpType
ACT = mybir.ActivationFunctionType
AX = mybir.AxisListType.X

B, T, C = 4, 512, 128
NTOK = B * T
TILES = NTOK // 128
DEPTH, HEADS, DH, WIN = 6, 16, 64, 32
HALF = DH // 2
GH = 4
GROUPS = HEADS // GH
NW = T // WIN
UW = NW // 2
UNITS = 2 * GROUPS
INNER = HEADS * DH
GD = GH * DH
QK_SCALE = 8.0
FF = int(C * 4 * 2 / 3)
FT = [(0, 128), (128, 128), (256, FF - 256)]
NH, DK, DV, LR = 4, 16, 32, 16
GATE_NORM = 16.0
E, H2 = 8, 256
EPS = 1e-5
NEG_INF = -1e38
RN_MAX = 1e12
LN_SCALE = float(2 ** 20)

P_W, P_U, P_G1, P_B1, P_G2, P_B2, P_MK, P_MV, P_MR, P_CK, P_CR, P_GW, P_BGK = range(13)
NPAR = 13
L_QA, L_QB, L_KA, L_KB, L_G, L_B, L_B1A, L_B1G, L_B2 = 0, 1, 2, 3, 4, 5, 6, 9, 12
NLP = 13
K, Q = 0, 1
PRE = 3


def after(k):
    return k + 1


def slot(w):
    return 4 * (w // 4) + 2 * (w % 2) + w % 4 // 2


def program(nc, x, params, lparams, w_tk, w_tv, w_tr, w_ck, w_cv, w_cr, wqkv, wo, w1, w2,
            gwq, gwk, gwv, gwg1, gwg2, gwg, gwo, router_t, ew1, ew2,
            rot, blocks, ident, mask, out):
    ctx = ExitStack()
    with ctx:
        def sem(name):
            return ctx.enter_context(nc.semaphore(name))

        def sbuf(name, cols, dt=F32):
            return ctx.enter_context(nc.sbuf_tensor(name, [128, cols], dt))

        bank = [ctx.enter_context(nc.psum_tensor(f"bank{i}", [128, 512], F32)) for i in range(8)]

        acc = sbuf("acc", NTOK)
        xres = sbuf("xres", NTOK)
        par = sbuf("par", NPAR)
        ident_s = sbuf("ident_s", 128)
        blocks_s = sbuf("blocks_s", 128)
        mean_s = sbuf("mean_s", 128)
        identb = sbuf("identb", 128, BF16)
        maskb = sbuf("maskb", 2 * 512, BF16)
        consts = sbuf("consts", 4)
        wq_hi = sbuf("wq_hi", 3 * INNER, F32R)
        wq_lo = sbuf("wq_lo", 3 * INNER, F32R)
        xs_hi = sbuf("xs_hi", WIN + T, F32R)
        xs_lo = sbuf("xs_lo", WIN + T, F32R)
        xv_hi = sbuf("xv_hi", WIN + T, F32R)
        xv_lo = sbuf("xv_lo", WIN + T, F32R)
        ARENA = 38300
        arena = sbuf("arena", ARENA)
        at = [0]

        def take(cols):
            a = arena[:, at[0]:at[0] + cols]
            at[0] += cols
            assert at[0] <= ARENA, at[0]
            return a

        accv = acc[:, :].rearrange("p (b t) -> p b t", b=B)
        xv = xres[:, :].rearrange("p (b t) -> p b t", b=B)

        xc = take(4 * T).rearrange("p (x t) -> p x t", x=4)
        lsq = take(2 * T).rearrange("p (x t) -> p x t", x=2)
        lln = take(2 * T).rearrange("p (x t) -> p x t", x=2)
        lrs = take(2 * T).rearrange("p (x t) -> p x t", x=2)
        wraw = take(3 * INNER)
        wo_s = take(8 * C).rearrange("p (k c) -> p k c", k=8)
        w1_s = take(2 * FF)
        w2_s = take(3 * C).rearrange("p (k c) -> p k c", k=3)
        lp = take(NLP)
        rot_s = take(4 * T).rearrange("p (k t) -> p k t", k=4)
        phase_at = at[0]
        t4, sqs, lnb, rnb = xc, lsq, lln, lrs
        qbd = take(2 * 2 * GH * T).rearrange("p (s a w h t) -> p s a w h t", s=2, a=2, w=NW, h=GH)
        kb = take(2 * 2 * (WIN + T)).rearrange("p (s a t) -> p s a t", s=2, a=2)
        tab = take(2 * T).rearrange("p (x t) -> p x t", x=2)
        vflat = take(2 * 2 * 4 * GD)
        vb = vflat.rearrange("p (s o m d) -> p s o m d", s=2, o=2, m=4)
        hflat = take(4 * 1024)
        probs = hflat[:, 0:1024].rearrange("p (s w k) -> p s w k", s=2, w=UW)
        qst = hflat[:, 1024:2048].rearrange("p (a t) -> p a t", a=2)
        sqb = hflat[:, 2048:4096].rearrange("p (x a t) -> p x a t", x=2, a=2)
        pts = take(4 * 2 * 128).rearrange("p (j k c) -> p j k c", j=4, k=2)
        oflat = take(8 * T)
        ot = oflat.rearrange("p (k t) -> p k t", k=8)
        mx = take(2 * UW).rearrange("p (s w) -> p s w", s=2)
        sm = take(2 * UW).rearrange("p (s w) -> p s w", s=2)
        rc = take(2 * UW).rearrange("p (s w) -> p s w", s=2)
        xf = oflat[:, 0:NTOK].rearrange("p (b t) -> p b t", b=B)
        xh = oflat[:, NTOK:2 * NTOK].rearrange("p (b t) -> p b t", b=B)
        gg = vflat[:, 0:3072].rearrange("p (s j t) -> p s j t", s=2, j=3)
        hh = hflat[:, 0:3072].rearrange("p (s j t) -> p s j t", s=2, j=3)

        at[0] = phase_at
        xtok = take(NTOK).rearrange("p (m c) -> p m c", c=C)
        hb = take(B * (T + 1)).rearrange("p (b t) -> p b t", b=B)
        h2b = take(B * (T + 1)).rearrange("p (b t) -> p b t", b=B)
        traw = take(4 * C + 4 * C)
        tmix = take(2 * 8 * C).rearrange("p (x c) -> p x c", x=2)
        tcv = take(4 * C).rearrange("p (k c) -> p k c", k=4)
        om = take(5)
        wfull = take(T)
        rwx = take(NTOK).rearrange("p (b t) -> p b t", b=B)
        m_run = take(T + 1)
        s_run = take(T + 1)
        pp = take(T + 1)
        a_run = take(T + 1)
        args = take(2 * T).rearrange("p (x t) -> p x t", x=2)
        kw = take(T)
        kmx = take(T)
        bv = take(T)
        kkb = take(4 * T).rearrange("p (x t) -> p x t", x=4)
        rr = take(T)
        maskf = take(2 * 512)

        at[0] = phase_at
        xn2 = take(NTOK).rearrange("p (b t) -> p b t", b=B)
        graw = take(64 + 64 + 128 + LR + 64 + 128 + 128)
        gwk_s, gwq_s, gwv_s, gwg1_s, gwg2_s, gwg_s, gwo_s = (
            graw[:, a:a + n] for a, n in ((0, 64), (64, 64), (128, 128), (256, LR), (272, 64), (336, 128), (464, 128)))
        wkrep = take(DK * 128).rearrange("p (i h r) -> p i h r", i=DK, h=NH)
        wqrep = take(DK * 128).rearrange("p (i h r) -> p i h r", i=DK, h=NH)
        selrep = take(DK * 128).rearrange("p (i h r) -> p i h r", i=DK, h=NH)
        vt = take(NTOK).rearrange("p (b t) -> p b t", b=B)
        egk = take(NTOK).rearrange("p (b t) -> p b t", b=B)
        gs = take(NTOK).rearrange("p (b t) -> p b t", b=B)
        go = take(NTOK).rearrange("p (b t) -> p b t", b=B)
        kvb = take(2 * T).rearrange("p (x t) -> p x t", x=2)
        sst = take(2 * T).rearrange("p (x t) -> p x t", x=2)
        tmp = take(2 * T).rearrange("p (x t) -> p x t", x=2)
        zb = take(T)
        g1s = take(T)
        az = take(2 * T).rearrange("p (x t) -> p x t", x=2)
        rt_s = take(E)
        top8 = take(TILES * 8).rearrange("p (m e) -> p m e", m=TILES)
        lg = take(TILES * 8).rearrange("p (m e) -> p m e", m=TILES)
        topi = ctx.enter_context(nc.sbuf_tensor("topi", [128, TILES * 8], mybir.dt.uint32))
        topf = take(TILES * 8).rearrange("p (m e) -> p m e", m=TILES)
        gate = take(TILES * 8).rearrange("p (m e) -> p m e", m=TILES)
        gpart = take(TILES * 8).rearrange("p (m e) -> p m e", m=TILES)
        gw12 = take(3 * TILES).rearrange("p (x m) -> p x m", x=3)
        iot = take(E)
        at[0] = 5 * 1024
        ew1_s = take(E * 2 * C).rearrange("p (e h c) -> p e h c", e=E, h=2)
        ew2_s = take(E * H2).rearrange("p (e f) -> p e f", e=E)
        assert at[0] <= phase_at
        w1t = wkrep.rearrange("p i h r -> p (i h r)").rearrange("p (e f) -> p e f", e=E)
        w2t = wqrep.rearrange("p i h r -> p (i h r)").rearrange("p (e h c) -> p e h c", e=E, h=2)
        otok = selrep.rearrange("p i h r -> p (i h r)").rearrange("p (m c) -> p m c", c=C)
        ht = vt.rearrange("p b t -> p (b t)").rearrange("p (s h t) -> p s h t", s=2, h=2)

        def head_windows(u, h, pair):
            g, hf = u // 2, u % 2
            rows = ot[64 * h:64 * h + 64, 2 * g + pair, 256 * hf:256 * hf + 256]
            return rows.rearrange("p (w q) -> p w q", w=UW)

        def own_part(n, h):
            return bank[n][64 * h:64 * h + 64, :].rearrange("p (w h q) -> p w h q", w=UW, h=2)[:, :, h]

        def group(names):
            return {n: sem(n) for n in names.split()}

        pe_s = group("mean_mm var_mm q_mm k_mm v_mm n2_mm s_mm t_mm pv_mm y_mm fg_mm fa_mm fy_mm")
        act_s = group("ln_sq ln_log ln_rstd sq_act log_act rn_act v_out exp_act pt_out o1_out xs_hi_act xv_hi_act place_act xf_act gelu_act")
        dve_s = group("ln_xc ln_n ln_out max_dve sub_dve sum_dve rec_dve tab_dve mul_dve o0_out resid_dve xs_lo_dve xv_lo_dve xf0_dve hh_dve fres_dve")
        pool_s = group("split_hi split sqadd rotadd norm_pool")
        s = {**pe_s, **act_s, **dve_s, **pool_s}
        wqkv_in, wo_in, ff_in = sem("wqkv_in"), sem("wo_in"), sem("ff_in")
        z = group("const_in x_in tm_in rot_in fin_in out_done zeroed padded x_turned x_copied "
                  "kvr_mm ck_mm cr_mm cv_mm mixed dve_link decay_arg decay_exp sum_scan log_sum carry_arg carry_exp "
                  "out_arg out_exp gate_exp k_free cm_exp kk_dve cm_done b1_done "
                  "fin_sum rep_made g1_mm g1_copy z_mm z_copy abs_act gexp_act gln_act gk_dve egk_act "
                  "gv_mm gv_copy gg_mm gg_exp gg_dve gg_act abank "
                  "rk_mm rg_mm rq_mm kv_dve scan_dve qs_dve oadd gsq_act gms_mm gl_act gr_act gn_dve go_mm x1_dve "
                  "tok_mm tok_copy lg_mm lg_copy route ew_turned ew_copied eh_mm eh_act ey_mm ey_dve iota_pool")
        block = ctx.enter_context(nc.Block())

        @block.sync
        def _(sp):
            for dst, src in ((ident_s, ident), (blocks_s, blocks), (par, params)):
                sp.dma_start(dst[:, :], src).then_inc(z["const_in"], 16)
            sp.dma_start(maskf, mask).then_inc(z["const_in"], 16)
            xtiles = x.rearrange("b (m p) c -> p (b m) c", p=128)
            for i in range(4):
                sp.dma_start(xtok[:, 4 * i:4 * i + 4, :], xtiles[:, 4 * i:4 * i + 4, :]).then_inc(z["x_in"], 16)
            for n, src in enumerate((w_tk, w_tv, w_tr, w_cr)):
                sp.dma_start(traw[:, n * C:(n + 1) * C], src).then_inc(z["tm_in"], 16)
            sp.dma_start(tmix[:, 0, 4 * C:8 * C], w_ck).then_inc(z["tm_in"], 16)
            sp.dma_start(tcv, w_cv.rearrange("(k p) c -> p k c", p=128)).then_inc(z["tm_in"], 16)
            sp.dma_start(rot_s, rot).then_inc(z["rot_in"], 16)

            with sp.Fori(0, DEPTH) as layer:
                sp.wait_ge(s["split"], after(layer))
                sp.dma_start(wraw, wqkv[bass.ds(layer, 1), :, :].rearrange("l c n -> c (l n)")).then_inc(wqkv_in, 16)
                sp.wait_ge(s["y_mm"], after(layer * B))
                sp.dma_start(wo_s, wo[bass.ds(layer, 1), :, :].rearrange("l (k p) c -> p (l k) c", p=128)).then_inc(wo_in, 16)
                sp.dma_start(lp[:, 0:4], lparams[bass.ds(layer, 1), :, 0:4].rearrange("l p c -> p (l c)")).then_inc(wo_in, 16)
                sp.wait_ge(s["fres_dve"], after(layer * B))
                sp.dma_start(w1_s, w1[bass.ds(layer, 1), :, :].rearrange("l c n -> c (l n)")).then_inc(ff_in, 16)
                sp.dma_start(w2_s[:, 0:2, :], w2[bass.ds(layer, 1), 0:256, :].rearrange("l (k p) c -> p (l k) c", p=128)).then_inc(ff_in, 16)
                sp.dma_start(w2_s[0:FF - 256, 2, :], w2[bass.ds(layer, 1), 256:FF, :].rearrange("l p c -> p (l c)")).then_inc(ff_in, 16)
                sp.dma_start(lp[:, 4:NLP], lparams[bass.ds(layer, 1), :, 4:NLP].rearrange("l p c -> p (l c)")).then_inc(ff_in, 16)

            sp.wait_ge(s["fres_dve"], after(DEPTH * B))
            for dst, src in ((gwk_s, gwk), (gwq_s, gwq), (gwv_s, gwv), (gwg1_s, gwg1), (gwg2_s[0:LR, :], gwg2),
                             (gwg_s, gwg), (gwo_s, gwo), (rt_s, router_t),
                             (ew1_s, ew1.rearrange("e (h p) c -> p e h c", p=128)),
                             (ew2_s, ew2.rearrange("e p f -> p e f"))):
                sp.dma_start(dst, src).then_inc(z["fin_in"], 16)
            outv = out.rearrange("b (m p) c -> p (b m) c", p=128)
            for q in range(B):
                sp.wait_ge(z["ey_dve"], q * E + E)
                sp.dma_start(outv[:, 4 * q:4 * q + 4, :], otok[:, 4 * q:4 * q + 4, :]).then_inc(z["out_done"], 16)
            sp.wait_ge(z["out_done"], 16 * B)

        @block.tensor
        def _(pe):
            for n in pe_s.values():
                pe.sem_inc(n, 1)


            def layer_norm(i, src):
                for c in range(B):
                    pe.wait_ge(s["ln_xc"], after(i * B + c))
                    pe.matmul(bank[6][:, :], mean_s[:, :], src(c), start=True, stop=True).then_inc(s["mean_mm"], 1)
                    if c > 0:
                        variance(i, c - 1)
                variance(i, B - 1)

            def variance(i, c):
                pe.wait_ge(s["ln_sq"], after(i * B + c + 1))
                pe.wait_ge(s["ln_log"], after(i * B + c))
                pe.matmul(bank[7][:, :], mean_s[:, :], lsq[:, c % 2, :], start=True, stop=True).then_inc(s["var_mm"], 1)

            pe.wait_ge(z["const_in"], 16 * 4)
            for m in range(TILES):
                if m % 4 == 0:
                    pe.wait_ge(z["x_in"], 16 * 4)
                mm = pe.transpose(bank[m // 4][:, 128 * (m % 4):128 * (m % 4) + 128], xtok[:, m, :], ident_s[:, :])
            mm.then_inc(z["x_turned"], 1)
            pe.wait_ge(z["x_copied"], B)
            pe.wait_ge(z["zeroed"], 1)
            layer_norm(0, lambda c: accv[:, c, :])
            pe.wait_ge(s["ln_out"], after(B))
            layer_norm(1, lambda c: xv[:, c, :])
            pe.wait_ge(z["mixed"], 1)
            for b in range(B):
                pe.wait_ge(s["ln_out"], after(B + b + 1))
                if b >= 2:
                    pe.wait_ge(z["k_free"], b - 1)
                for j in range(3):
                    o = bank[j + 3 * (b % 2)][:, :]
                    pe.matmul(o, tmix[:, 0, j * C:(j + 1) * C], hb[:, b, 1:T + 1], start=True, stop=False)
                    mm = pe.matmul(o, tmix[:, 1, j * C:(j + 1) * C], hb[:, b, 0:T], start=False, stop=True)
                mm.then_inc(z["kvr_mm"], 1)
            pe.wait_ge(z["b1_done"], B)
            layer_norm(2, lambda c: rwx[:, c, :])
            for b in range(B):
                pe.wait_ge(s["ln_out"], after(2 * B + b + 1))
                for j in range(4):
                    if b >= 1:
                        pe.wait_ge(z["kk_dve"], 4 * (b - 1) + j + 1)
                    o = bank[j][:, :]
                    w = slice((4 + j) * C, (5 + j) * C)
                    pe.matmul(o, tmix[:, 0, w], h2b[:, b, 1:T + 1], start=True, stop=False)
                    pe.matmul(o, tmix[:, 1, w], h2b[:, b, 0:T], start=False, stop=True).then_inc(z["ck_mm"], 1)
                if b >= 1:
                    pe.wait_ge(z["cm_exp"], b)
                w = slice(3 * C, 4 * C)
                pe.matmul(bank[4][:, :], tmix[:, 0, w], h2b[:, b, 1:T + 1], start=True, stop=False)
                pe.matmul(bank[4][:, :], tmix[:, 1, w], h2b[:, b, 0:T], start=False, stop=True).then_inc(z["cr_mm"], 1)
                if b >= 1:
                    pe.wait_ge(z["cm_done"], b)
                for j in range(4):
                    pe.wait_ge(z["kk_dve"], 4 * b + j + 1)
                    mm = pe.matmul(bank[5][:, :], tcv[:, j, :], kkb[:, j, :], start=(j == 0), stop=(j == 3))
                mm.then_inc(z["cv_mm"], 1)
            pe.wait_ge(z["cm_done"], B)

            def three(o, w_at, rhs, w_first):
                hi, lo = rhs
                if w_first:
                    pe.matmul(o, w_at(wq_hi), hi, start=True, stop=False)
                    pe.matmul(o, w_at(wq_lo), hi, start=False, stop=False)
                    return pe.matmul(o, w_at(wq_hi), lo, start=False, stop=True)
                pe.matmul(o, hi, w_at(wq_hi), start=True, stop=False)
                pe.matmul(o, hi, w_at(wq_lo), start=False, stop=False)
                return pe.matmul(o, lo, w_at(wq_hi), start=False, stop=True)

            def project(pi, g, kind):
                pe.wait_ge(s["mul_dve"], after(pi * 2 + kind))
                for a in range(2):
                    at_ = (INNER if kind == K else 0) + g * GD + a * 128
                    mm = three(bank[2 * kind + a][:, :], lambda w: w[:, at_:at_ + 128],
                               (xs_hi[:, WIN:], xs_lo[:, WIN:]), True)
                mm.then_inc(s["k_mm" if kind == K else "q_mm"], 1)

            def norms(pi, kind):
                pe.wait_ge(s["sqadd"], after(pi * 2 + kind + 1))
                pe.matmul(bank[4][:, :], blocks_s[:, :], sqs[:, kind, :], start=True, stop=True).then_inc(s["n2_mm"], 1)

            def values(pi, g, c):
                for j in range(2):
                    t0 = (WIN if c < 2 else 0) + 128 * (2 * (c % 2) + j)
                    mm = three(bank[4][:, j * GD:(j + 1) * GD],
                               lambda w: w[:, 2 * INNER + g * GD:2 * INNER + (g + 1) * GD],
                               (xv_hi[:, t0:t0 + 128], xv_lo[:, t0:t0 + 128]), False)
                mm.then_inc(s["v_mm"], 1)

            def scores(n, u):
                g, hf, un = u // 2, u % 2, n * UNITS + u
                pi = n * GROUPS + g
                pe.wait_ge(s["sub_dve"], after(un))
                if hf == 0:
                    pe.wait_ge(s["place_act"], after(pi + 1))
                    pe.wait_ge(s["rotadd"], after(pi * 2 + 2))
                for wl in range(UW):
                    t0 = (hf * UW + wl) * WIN
                    at_ = 64 * slot(wl)
                    for a in range(2):
                        pe.matmul(bank[5][:, at_:at_ + 64],
                                       qbd[:, g % 2, a, hf * UW + wl].rearrange("p h t -> p (h t)"),
                                       kb[:, g % 2, a, t0:t0 + 2 * WIN],
                                  start=(a == 0 and wl == 0), stop=False)
                pe.matmul(bank[5][:, :], identb[:, :], maskb[:, 512 * (hf > 0):512 * (hf > 0) + 512],
                          start=False, stop=True).then_inc(s["s_mm"], 1)

            def turn(n, u):
                un = n * UNITS + u
                pe.wait_ge(s["norm_pool"], after(un + 1))
                pe.wait_ge(s["o1_out"], after(un))
                for j in range(4):
                    mm = pe.transpose(bank[6][:, 128 * j:128 * j + 128],
                                      probs[:, u % 2, 2 * j:2 * j + 2, :].rearrange("p w k -> p (w k)"), ident_s[:, :])
                mm.then_inc(s["t_mm"], 1)

            def attend(n, u):
                g, hf, un = u // 2, u % 2, n * UNITS + u
                pe.wait_ge(s["pt_out"], after(un + 1))
                pe.wait_ge(s["o0_out"], after(un))
                pe.wait_ge(s["v_out"], after((n * GROUPS + g) * 4 + 4))
                for pair in range(2):
                    o = bank[7 - pair][:, :].rearrange("p (m k o c) -> p m k o c", m=2, k=2, o=2)
                    for j in range(4):
                        mm = pe.matmul(o[:, j // 2, :, j % 2, :],
                                       vb[:, g % 2, 1 - j % 2, 2 * hf + j // 2, 128 * pair:128 * pair + 128],
                                       pts[:, j, :, 64 * pair:64 * pair + 64], start=True, stop=True)
                    mm.then_inc(s["pv_mm"], 1)

            def project_out(n, ahead, ks):
                if ks[0] == 0:
                    pe.wait_ge(s["v_out"], after((n * GROUPS + GROUPS + (1 if ahead else 0)) * 4))
                    pe.wait_ge(s["o0_out"], after(n * UNITS + UNITS - 2))
                    pe.wait_ge(s["o1_out"], after(n * UNITS + UNITS - 2))
                else:
                    pe.wait_ge(s["o0_out"], after(n * UNITS + UNITS))
                    pe.wait_ge(s["o1_out"], after(n * UNITS + UNITS))
                for k in ks:
                    mm = pe.matmul(bank[4][:, :], wo_s[:, k, :], ot[:, k, :], start=(k == 0), stop=(k == 7))
                if ks[-1] == 7:
                    mm.then_inc(s["y_mm"], 1)

            def attention(n, ahead):
                for u in range(UNITS):
                    g = u // 2
                    pi = n * GROUPS + g
                    v_too = g + 1 < GROUPS or ahead
                    qk_too = g + 2 < GROUPS or ahead
                    g1, g2 = (g + 1) % GROUPS, (g + 2) % GROUPS
                    if u % 2 == 0:
                        scores(n, u)
                        if u:
                            turn(n, u - 1)
                        if v_too:
                            if g == 0:
                                pe.wait_ge(s["resid_dve"], after(n))
                            if g1 == 0:
                                pe.wait_ge(s["xv_lo_dve"], after(n + 2))
                            pe.wait_ge(s["v_out"], after(pi * 4 + 4))
                            values(pi + 1, g1, 0)
                        if qk_too:
                            if g2 == 0:
                                pe.wait_ge(s["xs_lo_dve"], after(n + 2))
                            project(pi + 2, g2, K)
                        if u:
                            attend(n, u - 1)
                        if v_too:
                            pe.wait_ge(s["v_out"], after(pi * 4 + 5))
                            values(pi + 1, g1, 1)
                    else:
                        scores(n, u)
                        turn(n, u - 1)
                        if qk_too:
                            pe.wait_ge(s["v_out"], after(pi * 4 + 6))
                            norms(pi + 2, K)
                            project(pi + 2, g2, Q)
                        if v_too:
                            if qk_too:
                                pe.wait_ge(s["log_act"], after(pi * 2 + 5))
                            else:
                                pe.wait_ge(s["v_out"], after(pi * 4 + 6))
                            values(pi + 1, g1, 2)
                        attend(n, u - 1)
                        if qk_too:
                            pe.wait_ge(s["v_out"], after(pi * 4 + 7))
                            norms(pi + 2, Q)
                        if v_too:
                            if qk_too:
                                pe.wait_ge(s["log_act"], after(pi * 2 + 6))
                            else:
                                pe.wait_ge(s["v_out"], after(pi * 4 + 7))
                            values(pi + 1, g1, 3)
                turn(n, UNITS - 1)
                project_out(n, ahead, range(0, 6))
                attend(n, UNITS - 1)
                project_out(n, ahead, range(6, 8))

            def feed_forward(n, b):
                pe.wait_ge(s["ln_out"], after(PRE * B + n + 1))
                for j, (f0, fn) in enumerate(FT):
                    pe.wait_ge(s["gelu_act"], after(n * 3 + j))
                    pe.matmul(bank[j][0:fn, :], w1_s[:, FF + f0:FF + f0 + fn], xh[:, b, :],
                              start=True, stop=True).then_inc(s["fg_mm"], 1)
                    pe.wait_ge(s["hh_dve"], after(n * 3 + j))
                    pe.matmul(bank[3 + j][0:fn, :], w1_s[:, f0:f0 + fn], xh[:, b, :],
                              start=True, stop=True).then_inc(s["fa_mm"], 1)

            def feed_forward_out(n, b):
                for j, (f0, fn) in enumerate(FT):
                    pe.wait_ge(s["hh_dve"], after(n * 3 + j + 1))
                    mm = pe.matmul(bank[6 + b % 2][:, :], w2_s[0:fn, j, :], hh[0:fn, b % 2, j, :],
                                   start=(j == 0), stop=(j == 2))
                mm.then_inc(s["fy_mm"], 1)

            with pe.Fori(0, DEPTH) as layer:
                pe.wait_ge(s["split"], after(layer + 1))
                pe.wait_ge(wo_in, layer * 32 + 32)
                n0 = layer * B
                pe.wait_ge(s["xs_lo_dve"], after(n0 + 1))
                p0 = n0 * GROUPS
                project(p0, 0, K)
                project(p0, 0, Q)
                norms(p0, K)
                pe.wait_ge(s["log_act"], after(p0 * 2 + 1))
                norms(p0, Q)
                pe.wait_ge(s["xv_lo_dve"], after(n0 + 1))
                pe.wait_ge(s["log_act"], after(p0 * 2 + 2))
                values(p0, 0, 0)
                pe.wait_ge(s["v_out"], after(p0 * 4 + 1))
                values(p0, 0, 1)
                project(p0 + 1, 1, K)
                pe.wait_ge(s["v_out"], after(p0 * 4 + 2))
                norms(p0 + 1, K)
                pe.wait_ge(s["log_act"], after(p0 * 2 + 3))
                values(p0, 0, 2)
                project(p0 + 1, 1, Q)
                pe.wait_ge(s["v_out"], after(p0 * 4 + 3))
                norms(p0 + 1, Q)
                pe.wait_ge(s["log_act"], after(p0 * 2 + 4))
                values(p0, 0, 3)
                with pe.Fori(0, B - 1) as b:
                    attention(layer * B + b, True)
                attention(layer * B + (B - 1), False)
                pe.wait_ge(ff_in, layer * 64 + 64)
                pe.wait_ge(s["xf0_dve"], after(layer + 1))
                for c in range(B):
                    pe.wait_ge(s["xf_act"], after(layer * B + c + 1))
                    pe.wait_ge(s["ln_xc"], after((PRE + layer) * B + c))
                    if c == 0:
                        pe.wait_ge(s["o1_out"], after(layer * B * UNITS + B * UNITS))
                    pe.matmul(bank[6][:, :], mean_s[:, :], xf[:, c, :], start=True, stop=True).then_inc(s["mean_mm"], 1)
                    if c > 0:
                        variance(PRE + layer, c - 1)
                variance(PRE + layer, B - 1)
                for b in range(B):
                    feed_forward(layer * B + b, b)
                    if b:
                        feed_forward_out(layer * B + b - 1, b - 1)
                feed_forward_out(layer * B + B - 1, B - 1)

            LAST = PRE + DEPTH
            pe.wait_ge(z["fin_sum"], B)
            layer_norm(LAST, lambda c: accv[:, c, :])
            pe.wait_ge(z["fin_in"], 160)
            for b in range(B):
                pe.wait_ge(s["ln_out"], after(LAST * B + b + 1))
                if b:
                    pe.wait_ge(z["g1_copy"], b)
                pe.matmul(bank[6][0:LR, :], gwg1_s, xn2[:, b, :], start=True, stop=True).then_inc(z["g1_mm"], 1)
                if b >= 2:
                    pe.wait_ge(z["gv_copy"], b - 1)
                pe.matmul(bank[b % 2][:, :], gwv_s, xn2[:, b, :], start=True, stop=True).then_inc(z["gv_mm"], 1)
                if b >= 2:
                    pe.wait_ge(z["gg_dve"], b - 1)
                pe.matmul(bank[2 + b % 2][:, :], gwg_s, xn2[:, b, :], start=True, stop=True).then_inc(z["gg_mm"], 1)
                pe.wait_ge(z["g1_copy"], b + 1)
                if b:
                    pe.wait_ge(z["z_copy"], b)
                pe.matmul(bank[7][0:64, :], gwg2_s[0:LR, :], g1s[0:LR, :], start=True, stop=True).then_inc(z["z_mm"], 1)
            pe.wait_ge(z["rep_made"], 3)
            pe.wait_ge(z["gv_copy"], B)
            pe.wait_ge(z["gg_dve"], B)
            for b in range(B):
                pe.wait_ge(z["egk_act"], b + 1)
                for i in range(DK):
                    t = b * DK + i
                    if t >= 2:
                        pe.wait_ge(z["kv_dve"], t - 1)
                    pe.matmul(bank[t % 2][:, :], wkrep[:, i], xn2[:, b, :], start=True, stop=True).then_inc(z["rk_mm"], 1)
                    if t >= 2:
                        pe.wait_ge(z["scan_dve"], t - 1)
                    pe.matmul(bank[2 + t % 2][:, :], selrep[0:64, i], egk[0:64, b, :], start=True, stop=True).then_inc(z["rg_mm"], 1)
                    if t >= 2:
                        pe.wait_ge(z["qs_dve"], t - 1)
                    pe.matmul(bank[4 + t % 2][:, :], wqrep[:, i], xn2[:, b, :], start=True, stop=True).then_inc(z["rq_mm"], 1)
            for b in range(B):
                pe.wait_ge(z["gsq_act"], b + 1)
                if b:
                    pe.wait_ge(z["gl_act"], b)
                pe.matmul(bank[6][:, :], blocks_s[:, :], kvb[:, b % 2, :], start=True, stop=True).then_inc(z["gms_mm"], 1)
                pe.wait_ge(z["gn_dve"], b + 1)
                if b:
                    pe.wait_ge(z["x1_dve"], b)
                pe.matmul(bank[7][:, :], gwo_s, go[:, b, :], start=True, stop=True).then_inc(z["go_mm"], 1)
            for b in range(B):
                pe.wait_ge(z["x1_dve"], b + 1)
                if b == 0:
                    pe.wait_ge(z["kv_dve"], B * DK)
                    pe.wait_ge(z["scan_dve"], B * DK)
                    pe.wait_ge(z["qs_dve"], B * DK)
                for m in range(4):
                    mm = pe.transpose(bank[b][:, 128 * m:128 * m + 128], accv[:, b, 128 * m:128 * m + 128], ident_s[:, :])
                mm.then_inc(z["tok_mm"], 1)
            for m in range(TILES):
                mm = pe.matmul(bank[4][:, 8 * m:8 * m + 8], xn2[:, m // 4, 128 * (m % 4):128 * (m % 4) + 128], rt_s,
                               start=True, stop=True)
            mm.then_inc(z["lg_mm"], 1)
            for t in range(8):
                if t >= 2:
                    pe.wait_ge(z["ew_copied"], t - 1)
                for j in range(4):
                    e, h = (4 * (t % 4) + j) // 2, (4 * (t % 4) + j) % 2
                    src = ew1_s[:, e, h, :] if t < 4 else ew2_s[:, e, 128 * h:128 * h + 128]
                    mm = pe.transpose(bank[6 + t % 2][:, 128 * j:128 * j + 128], src, ident_s[:, :])
                mm.then_inc(z["ew_turned"], 1)
            pe.wait_ge(z["ew_copied"], 8)
            pe.wait_ge(z["tok_copy"], B)

            def expert_out(t):
                q, e = t // E, t % E
                pe.wait_ge(z["eh_act"], 2 * t + 2)
                if t >= 2:
                    pe.wait_ge(z["ey_dve"], t - 1)
                for m in range(4):
                    for h in range(2):
                        mm = pe.matmul(bank[6 + t % 2][:, 128 * m:128 * m + 128], ht[:, t % 2, h, 128 * m:128 * m + 128],
                                       w2t[:, e, h, :], start=(h == 0), stop=(h == 1))
                mm.then_inc(z["ey_mm"], 1)

            for t in range(B * E):
                q, e = t // E, t % E
                for h in range(2):
                    if t >= 2:
                        pe.wait_ge(z["eh_act"], 2 * (t - 2) + h + 1)
                    pe.matmul(bank[2 * (t % 2) + h][:, :], w1t[:, e, 128 * h:128 * h + 128], xn2[:, q, :],
                              start=True, stop=True).then_inc(z["eh_mm"], 1)
                if t:
                    expert_out(t - 1)
            expert_out(B * E - 1)

        @block.scalar
        def _(act):
            for n in act_s.values():
                act.sem_inc(n, 1)
            eps, one, floor = consts[:, 0:1], consts[:, 1:2], consts[:, 2:3]

            def layer_norm(i):
                for c in range(B):
                    act.wait_ge(s["ln_xc"], after(i * B + c + 1))
                    if c >= 2:
                        act.wait_ge(s["var_mm"], after(i * B + c - 1))
                    act.activation(lsq[:, c % 2, :], xc[:, c, :], ACT.Square).then_inc(s["ln_sq"], 1)
                    if c > 0:
                        rstd(i, c - 1)
                rstd(i, B - 1)

            def rstd(i, c):
                act.wait_ge(s["var_mm"], after(i * B + c + 1))
                act.activation(lln[:, c % 2, :], bank[7][:, :], ACT.Ln, bias=eps).then_inc(s["ln_log"], 1)
                act.wait_ge(s["ln_log"], after(i * B + c + 1))
                if c >= 2:
                    act.wait_ge(s["ln_n"], after(i * B + c - 1))
                act.activation(lrs[:, c % 2, :], lln[:, c % 2, :], ACT.Exp, scale=-0.5).then_inc(s["ln_rstd"], 1)

            act.preload_act_table_set("natural_log_exp_and_others")
            for b in range(B):
                act.wait_ge(z["x_turned"], 1)
                act.activation(accv[:, b, :], bank[b][:, :], ACT.Copy).then_inc(z["x_copied"], 1)
            act.wait_ge(z["zeroed"], 1)
            layer_norm(0)
            layer_norm(1)
            for b in range(B):
                act.wait_ge(z["decay_arg"], b + 1)
                act.activation(args[:, :, :], args[:, :, :], ACT.Exp).then_inc(z["decay_exp"], 1)
                act.wait_ge(z["sum_scan"], b + 1)
                act.activation(pp, s_run, ACT.Ln).then_inc(z["log_sum"], 1)
                act.wait_ge(z["carry_arg"], b + 1)
                act.activation(args[:, :, :], args[:, :, :], ACT.Exp).then_inc(z["carry_exp"], 1)
                act.wait_ge(z["out_arg"], b + 1)
                act.activation(args[:, :, :], args[:, :, :], ACT.Exp).then_inc(z["out_exp"], 1)
                act.activation(rr, bank[2 + 3 * (b % 2)][:, :], ACT.Exp, scale=-1.0).then_inc(z["gate_exp"], 1)
            layer_norm(2)
            for b in range(B):
                act.wait_ge(z["cr_mm"], b + 1)
                if b:
                    act.wait_ge(z["cm_done"], b)
                act.activation(rr, bank[4][:, :], ACT.Exp, scale=-1.0).then_inc(z["cm_exp"], 1)

            def tokens_for_qk(n, b):
                act.wait_ge(s["q_mm"], after(n * GROUPS))
                act.activation(xs_hi[0:64, WIN:], xv[0:64, b, :], ACT.Copy)
                act.activation(xs_hi[64:128, WIN + 1:], xv[64:128, b, 0:T - 1], ACT.Copy).then_inc(s["xs_hi_act"], 1)

            def tokens_for_v(n):
                act.wait_ge(s["xs_hi_act"], after(n + 1))
                act.wait_ge(s["v_mm"], after(n * GROUPS * 4))
                act.activation(xv_hi[:, WIN:], xs_hi[:, WIN:].bitcast(F32), ACT.Copy).then_inc(s["xv_hi_act"], 1)

            def squares(pi, kind):
                act.wait_ge(s["k_mm" if kind == K else "q_mm"], after(pi + 1))
                act.wait_ge(s["sqadd"], after(pi * 2))
                act.activation(sqb[:, kind, 0, :], bank[2 * kind][:, :], ACT.Square)
                act.activation(sqb[:, kind, 1, :], bank[2 * kind + 1][:, :], ACT.Square).then_inc(s["sq_act"], 1)

            def rnorm(pi, kind):
                act.wait_ge(s["n2_mm"], after(pi * 2 + kind + 1))
                act.activation(lnb[:, kind, :], bank[4][:, :], ACT.Ln, bias=floor, scale=LN_SCALE).then_inc(s["log_act"], 1)
                act.wait_ge(s["log_act"], after(pi * 2 + kind + 1))
                act.wait_ge(s["tab_dve"], after(pi * 2 + kind))
                act.activation(rnb[:, kind, :], lnb[:, kind, :], ACT.Exp, bias=consts[:, 3:4], scale=-0.5).then_inc(s["rn_act"], 1)

            def place(pi, g):
                act.wait_ge(s["rotadd"], after(pi * 2 + 2))
                for h in range(GH):
                    rows = slice(HALF * h, HALF * h + HALF)
                    ins = act.activation(qbd[rows, g % 2, :, :, h, :],
                                         qst[rows].rearrange("p a (w t) -> p a w t", w=NW), ACT.Copy)
                ins.then_inc(s["place_act"], 1)

            def values_out(pi, g, c):
                act.wait_ge(s["v_mm"], after(pi * 4 + c + 1))
                act.activation(vb[:, g % 2, c // 2, 2 * (c % 2):2 * (c % 2) + 2, :],
                               bank[4][:, :].rearrange("p (m d) -> p m d", m=2), ACT.Copy).then_inc(s["v_out"], 1)

            def exponent(n, u):
                un = n * UNITS + u
                act.wait_ge(s["sub_dve"], after(un + 1))
                act.activation(probs[:, u % 2], probs[:, u % 2], ACT.Exp, scale=QK_SCALE).then_inc(s["exp_act"], 1)

            def turned_out(n, u):
                act.wait_ge(s["t_mm"], after(n * UNITS + u + 1))
                for k in range(2):
                    rows = slice(64 * k, 64 * k + 64)
                    ins = act.activation(pts[rows, :, k, :], bank[6][rows, :].rearrange("p (j c) -> p j c", j=4), ACT.Copy)
                ins.then_inc(s["pt_out"], 1)

            def heads_out(n, u):
                act.wait_ge(s["pv_mm"], after((n * UNITS + u) * 2 + 2))
                for h in range(2):
                    mm = act.activation(head_windows(u, h, 1), own_part(6, h), ACT.Copy)
                mm.then_inc(s["o1_out"], 1)

            def attention(n, b, ahead):
                for u in range(UNITS):
                    g = u // 2
                    pi = n * GROUPS + g
                    v_too = g + 1 < GROUPS or ahead
                    qk_too = g + 2 < GROUPS or ahead
                    g1 = (g + 1) % GROUPS
                    if u % 2 == 0:
                        if ahead and g + 2 == GROUPS:
                            tokens_for_qk(n + 1, b + 1)
                        if ahead and g + 1 == GROUPS:
                            tokens_for_v(n + 1)
                        if u:
                            turned_out(n, u - 1)
                        exponent(n, u)
                        if v_too:
                            values_out(pi + 1, g1, 0)
                        if qk_too:
                            squares(pi + 2, K)
                        if u:
                            heads_out(n, u - 1)
                        if v_too:
                            values_out(pi + 1, g1, 1)
                    else:
                        if v_too:
                            place(pi + 1, g1)
                        turned_out(n, u - 1)
                        exponent(n, u)
                        if qk_too:
                            rnorm(pi + 2, K)
                            squares(pi + 2, Q)
                        if v_too:
                            values_out(pi + 1, g1, 2)
                        heads_out(n, u - 1)
                        if qk_too:
                            rnorm(pi + 2, Q)
                        if v_too:
                            values_out(pi + 1, g1, 3)
                turned_out(n, UNITS - 1)
                heads_out(n, UNITS - 1)

            act.wait_ge(z["padded"], 1)
            with act.Fori(0, DEPTH) as layer:
                n0 = layer * B
                act.preload_act_table_set("natural_log_exp_and_others")
                act.wait_ge(s["fres_dve"], after(n0))
                tokens_for_qk(n0, 0)
                tokens_for_v(n0)
                p0 = n0 * GROUPS
                squares(p0, K)
                squares(p0, Q)
                rnorm(p0, K)
                rnorm(p0, Q)
                values_out(p0, 0, 0)
                values_out(p0, 0, 1)
                squares(p0 + 1, K)
                rnorm(p0 + 1, K)
                values_out(p0, 0, 2)
                squares(p0 + 1, Q)
                rnorm(p0 + 1, Q)
                place(p0, 0)
                values_out(p0, 0, 3)
                with act.Fori(0, B - 1) as b:
                    attention(layer * B + b, b, True)
                attention(layer * B + (B - 1), B - 1, False)
                act.wait_ge(s["y_mm"], after(n0 + B))
                for c in range(B):
                    act.wait_ge(s["resid_dve"], after(layer * B + c + 1))
                    act.activation(xf[0:64, c, :], xv[0:64, c, :], ACT.Copy)
                    act.activation(xf[64:128, c, 1:T], xv[64:128, c, 0:T - 1], ACT.Copy).then_inc(s["xf_act"], 1)
                i = PRE + layer
                layer_norm(i)
                act.preload_act_table_set("gelu_and_others")
                for b in range(B):
                    for j, (f0, fn) in enumerate(FT):
                        act.wait_ge(s["fg_mm"], after((layer * B + b) * 3 + j + 1))
                        if b >= 2:
                            act.wait_ge(s["hh_dve"], after((layer * B + b - 2) * 3 + j + 1))
                        act.activation(gg[0:fn, b % 2, j, :], bank[j][0:fn, :], ACT.Gelu,
                                       bias=lp[0:fn, L_B1G + j:L_B1G + j + 1]).then_inc(s["gelu_act"], 1)

            act.preload_act_table_set("natural_log_exp_and_others")
            layer_norm(PRE + DEPTH)
            act.wait_ge(z["fin_in"], 160)
            for dst, src, sc in ((wkrep, gwk_s, 1.0), (wqrep, gwq_s, float(DK) ** -0.5)):
                act.activation(dst, src.rearrange("p (h i) -> p i h", h=NH)[:, :, :, None].to_broadcast([128, DK, NH, DV]),
                               ACT.Copy, scale=sc).then_inc(z["rep_made"], 1)
            act.activation(selrep[0:64], ident_s[0:64, 0:64].rearrange("p (h i) -> p i h", h=NH)[:, :, :, None]
                           .to_broadcast([64, DK, NH, DV]), ACT.Copy).then_inc(z["rep_made"], 1)
            for b in range(B):
                act.wait_ge(z["gv_mm"], b + 1)
                act.activation(vt[:, b, :], bank[b % 2][:, :], ACT.Copy).then_inc(z["gv_copy"], 1)
                act.wait_ge(z["gg_mm"], b + 1)
                act.activation(gs[:, b, :], bank[2 + b % 2][:, :], ACT.Exp, scale=-1.0).then_inc(z["gg_exp"], 1)
                act.wait_ge(z["z_copy"], b + 1)
                if b:
                    act.wait_ge(z["gk_dve"], b)
                act.activation(az[0:64, 0, :], zb[0:64, :], ACT.Abs).then_inc(z["abs_act"], 1)
                act.wait_ge(z["abs_act"], b + 1)
                act.activation(az[0:64, 1, :], az[0:64, 0, :], ACT.Exp, scale=-1.0).then_inc(z["gexp_act"], 1)
                act.wait_ge(z["gexp_act"], b + 1)
                act.activation(az[0:64, 0, :], az[0:64, 1, :], ACT.Ln, bias=one[0:64]).then_inc(z["gln_act"], 1)
                act.wait_ge(z["gk_dve"], b + 1)
                act.activation(egk[0:64, b, :], egk[0:64, b, :], ACT.Exp, scale=1.0 / GATE_NORM).then_inc(z["egk_act"], 1)
            for b in range(B):
                act.wait_ge(z["oadd"], DK * (b + 1))
                if b >= 2:
                    act.wait_ge(z["gms_mm"], b - 1)
                act.wait_ge(z["scan_dve"], B * DK)
                act.activation(kvb[:, b % 2, :], go[:, b, :], ACT.Square).then_inc(z["gsq_act"], 1)
                act.wait_ge(z["gms_mm"], b + 1)
                act.activation(az[:, 0, :], bank[6][:, :], ACT.Ln, bias=eps, scale=1.0 / DV).then_inc(z["gl_act"], 1)
                act.wait_ge(z["gl_act"], b + 1)
                if b:
                    act.wait_ge(z["gn_dve"], b)
                act.activation(az[:, 1, :], az[:, 0, :], ACT.Exp, scale=-0.5).then_inc(z["gr_act"], 1)
            for b in range(B):
                act.wait_ge(z["tok_mm"], b + 1)
                act.activation(otok[:, 4 * b:4 * b + 4, :], bank[b][:, :].rearrange("p (m c) -> p m c", c=C), ACT.Copy) \
                   .then_inc(z["tok_copy"], 1)
            act.wait_ge(z["lg_mm"], 1)
            act.activation(lg, bank[4][:, 0:128].rearrange("p (m e) -> p m e", e=8), ACT.Copy).then_inc(z["lg_copy"], 1)
            for t in range(8):
                act.wait_ge(z["ew_turned"], t + 1)
                dst = w1t[:, 2 * t:2 * t + 2, :] if t < 4 else w2t[:, 2 * (t - 4):2 * (t - 4) + 2, :, :]
                src = bank[6 + t % 2][:, :]
                src = src.rearrange("p (e f) -> p e f", e=2) if t < 4 else src.rearrange("p (e h c) -> p e h c", e=2, h=2)
                act.activation(dst, src, ACT.Copy).then_inc(z["ew_copied"], 1)
            act.wait_ge(z["route"], 1)
            act.activation(gw12[:, 0, :], gw12[:, 0, :], ACT.Exp).then_inc(z["route"], 1)
            act.preload_act_table_set("gelu_and_others")
            for t in range(B * E):
                for h in range(2):
                    act.wait_ge(z["eh_mm"], 2 * t + h + 1)
                    if t >= 2:
                        act.wait_ge(z["ey_mm"], t - 1)
                    act.activation(ht[:, t % 2, h, :], bank[2 * (t % 2) + h][:, :], ACT.Gelu).then_inc(z["eh_act"], 1)

        @block.vector
        def _(dve):
            for n in dve_s.values():
                dve.sem_inc(n, 1)
            dve.sem_inc(s["tab_dve"], 1)
            dve.sem_inc(s["mul_dve"], 1)
            count = [0]

            def link(ins):
                count[0] += 1
                ins.then_inc(z["dve_link"], 1)
                dve.wait_ge(z["dve_link"], count[0])

            def layer_norm(i, src, dst, gain=None, bias=None):
                for c in range(B):
                    dve.wait_ge(s["mean_mm"], after(i * B + c + 1))
                    dve.tensor_tensor(xc[:, c, :], src(c), bank[6][:, :], ALU.subtract).then_inc(s["ln_xc"], 1)
                    if c > 1:
                        normed(i, c - 2, dst, gain, bias)
                normed(i, B - 2, dst, gain, bias)
                normed(i, B - 1, dst, gain, bias)

            def normed(i, c, dst, gain, bias):
                dve.wait_ge(s["ln_rstd"], after(i * B + c + 1))
                if gain is None:
                    dve.tensor_tensor(dst(c), xc[:, c, :], lrs[:, c % 2, :], ALU.mult).then_inc(s["ln_out"], 1)

                    return
                dve.tensor_tensor(xc[:, c, :], xc[:, c, :], lrs[:, c % 2, :], ALU.mult).then_inc(s["ln_n"], 1)
                dve.wait_ge(s["ln_n"], after(i * B + c + 1))
                dve.tensor_scalar(dst(c), xc[:, c, :], gain, bias, ALU.mult, ALU.add).then_inc(s["ln_out"], 1)

            def col(k, rows=128):
                return par[0:rows, k:k + 1]

            dve.memset(mean_s[:, :], 1.0 / C)
            dve.memset(consts[:, 0:1], EPS)
            dve.memset(consts[:, 1:2], 1.0)
            dve.memset(consts[:, 2:3], 6e-20)
            dve.memset(consts[:, 3:4], 6.931471805599453)
            dve.memset(hb[:, :, 0:1], 0.0)
            dve.memset(h2b[:, :, 0:1], 0.0)
            dve.memset(m_run[:, 0:1], NEG_INF)
            dve.memset(s_run[:, 0:1], 1.0)
            dve.memset(a_run[:, 0:1], 0.0)
            dve.memset(wfull, 0.0).then_inc(z["zeroed"], 1)
            dve.wait_ge(z["zeroed"], 1)
            dve.wait_ge(z["x_copied"], B)
            dve.wait_ge(z["const_in"], 64)
            dve.tensor_copy(identb[:, :], ident_s[:, :])
            dve.tensor_copy(maskb[:, :], maskf)
            layer_norm(0, lambda c: accv[:, c, :], lambda c: xv[:, c, :], 1.0, 0.0)
            link(dve.tensor_scalar(wfull, wfull, col(P_W), None, ALU.add))
            dve.wait_ge(z["tm_in"], 96)
            link(dve.tensor_scalar(om[:, 0:5], par[:, P_MK:P_CR + 1], -1.0, 1.0, ALU.mult, ALU.add))
            for j, k in ((0, 0), (1, 1), (2, 2), (3, 4)):
                src = traw[:, j * C:(j + 1) * C]
                dve.tensor_scalar(tmix[:, 0, j * C:(j + 1) * C], src, col(P_MK + k), None, ALU.mult)
                dve.tensor_scalar(tmix[:, 1, j * C:(j + 1) * C], src, om[:, k:k + 1], None, ALU.mult)
            link(dve.tensor_scalar(tmix[:, 1, 4 * C:8 * C], tmix[:, 0, 4 * C:8 * C], om[:, 3:4], None, ALU.mult))
            dve.tensor_scalar(tmix[:, 0, 4 * C:8 * C], tmix[:, 0, 4 * C:8 * C], col(P_CK), None, ALU.mult).then_inc(z["mixed"], 1)
            dve.wait_ge(s["ln_out"], after(B))
            layer_norm(1, lambda c: xv[:, c, :], lambda c: hb[:, c, 1:T + 1], col(P_G1), col(P_B1))

            for b in range(B):
                k_ps, v_ps = bank[3 * (b % 2)][:, :], bank[3 * (b % 2) + 1][:, :]
                now = slice(1, T + 1)
                old = slice(0, T)
                dve.wait_ge(z["kvr_mm"], b + 1)
                link(dve.tensor_scalar(kw, k_ps, col(P_W), None, ALU.add))
                link(dve.tensor_tensor_scan(m_run[:, now], wfull, kw, m_run[:, 0:1], ALU.add, ALU.max))
                dve.scalar_tensor_tensor(args[:, 0, :], m_run[:, old], col(P_W), m_run[:, now], ALU.add, ALU.subtract)
                dve.tensor_tensor(args[:, 1, :], kw, m_run[:, now], ALU.subtract).then_inc(z["decay_arg"], 1)
                dve.wait_ge(z["decay_exp"], b + 1)
                dve.tensor_tensor_scan(s_run[:, now], args[:, 0, :], args[:, 1, :], 0.0, ALU.mult, ALU.add) \
                   .then_inc(z["sum_scan"], 1)
                dve.wait_ge(z["log_sum"], b + 1)
                link(dve.tensor_tensor(pp, pp, m_run, ALU.add))
                link(dve.tensor_tensor(kmx, k_ps, pp[:, old], ALU.max))
                dve.tensor_tensor(args[:, 0, :], pp[:, old], kmx, ALU.subtract)
                dve.tensor_tensor(args[:, 1, :], k_ps, kmx, ALU.subtract).then_inc(z["carry_arg"], 1)
                dve.wait_ge(z["carry_exp"], b + 1)
                link(dve.tensor_tensor(bv, v_ps, args[:, 1, :], ALU.mult))
                link(dve.tensor_tensor_scan(a_run[:, now], args[:, 0, :], bv, 0.0, ALU.mult, ALU.add))
                link(dve.scalar_tensor_tensor(kmx, k_ps, col(P_U), pp[:, old], ALU.add, ALU.max))
                dve.tensor_tensor(args[:, 0, :], pp[:, old], kmx, ALU.subtract)
                dve.scalar_tensor_tensor(args[:, 1, :], k_ps, col(P_U), kmx, ALU.add, ALU.subtract).then_inc(z["out_arg"], 1)
                dve.wait_ge(z["out_exp"], b + 1)
                dve.tensor_tensor(kw, args[:, 0, :], a_run[:, old], ALU.mult)
                dve.tensor_tensor(bv, v_ps, args[:, 1, :], ALU.mult)
                link(dve.tensor_tensor(kmx, args[:, 0, :], args[:, 1, :], ALU.add))
                link(dve.tensor_tensor(kw, kw, bv, ALU.add))
                dve.wait_ge(z["gate_exp"], b + 1)
                link(dve.scalar_tensor_tensor(bv, rr, 1.0, kmx, ALU.add, ALU.mult))
                link(dve.reciprocal(bv, bv))
                link(dve.tensor_tensor(kw, kw, bv, ALU.mult))
                link(dve.tensor_tensor(rwx[:, b, :], kw, xv[:, b, :], ALU.add))
                dve.sem_inc(z["k_free"], 1)
                dve.sem_inc(z["b1_done"], 1)
            layer_norm(2, lambda c: rwx[:, c, :], lambda c: h2b[:, c, 1:T + 1], col(P_G2), col(P_B2))
            for b in range(B):
                for j in range(4):
                    dve.wait_ge(z["ck_mm"], 4 * b + j + 1)
                    if b:
                        dve.wait_ge(z["cv_mm"], b)
                    link(dve.tensor_scalar(args[:, j % 2, :], bank[j][:, :], 0.0, None, ALU.max))
                    dve.tensor_tensor(kkb[:, j, :], args[:, j % 2, :], bank[j][:, :], ALU.mult).then_inc(z["kk_dve"], 1)
                dve.wait_ge(z["cm_exp"], b + 1)
                link(dve.tensor_scalar(bv, rr, 1.0, None, ALU.add))
                link(dve.reciprocal(bv, bv))
                dve.wait_ge(z["cv_mm"], b + 1)
                link(dve.tensor_tensor(bv, bank[5][:, :], bv, ALU.mult))
                link(dve.tensor_tensor(bv, bv, rwx[:, b, :], ALU.add))
                link(dve.tensor_tensor(accv[:, b, :], accv[:, b, :], bv, ALU.add))
                dve.sem_inc(z["cm_done"], 1)

            dve.memset(qbd[:, 0], 0.0)
            dve.memset(qbd[:, 1], 0.0)
            dve.memset(kb[:, :, :, 0:WIN], 0.0)
            dve.memset(pts, 0.0)
            for w in (xs_hi, xs_lo, xv_hi, xv_lo):
                dve.memset(w[:, 0:WIN].bitcast(F32), 0.0)
                ins = dve.memset(w[64:128, WIN:WIN + 1].bitcast(F32), 0.0)
            ins.then_inc(z["padded"], 1)
            dve.wait_ge(z["padded"], 1)
            dve.wait_ge(z["rot_in"], 16)

            def shifted_lo(n, b):
                dve.wait_ge(s["xs_hi_act"], after(n + 1))
                dve.tensor_tensor(xs_lo[0:64, WIN:], xv[0:64, b, :], xs_hi[0:64, WIN:].bitcast(F32), ALU.subtract)
                dve.tensor_tensor(xs_lo[64:128, WIN + 1:], xv[64:128, b, 0:T - 1], xs_hi[64:128, WIN + 1:].bitcast(F32),
                                  ALU.subtract).then_inc(s["xs_lo_dve"], 1)

            def shifted_lo_v(n):
                dve.wait_ge(s["xs_lo_dve"], after(n + 1))
                dve.wait_ge(s["xv_hi_act"], after(n + 1))
                dve.tensor_copy(xv_lo[:, WIN:], xs_lo[:, WIN:].bitcast(F32)).then_inc(s["xv_lo_dve"], 1)

            def tables(pi, kind):
                at_ = 2 if kind == K else 0
                dve.wait_ge(s["rn_act"], after(pi * 2 + kind + 1))
                dve.wait_ge(s["mul_dve"], after(pi * 2 + kind + 1))
                dve.scalar_tensor_tensor(tab[:, 0, :], rnb[:, kind, :], RN_MAX, rot_s[:, at_, :], ALU.min, ALU.mult)
                dve.scalar_tensor_tensor(tab[:, 1, :], rnb[:, kind, :], RN_MAX, rot_s[:, at_ + 1, :], ALU.min, ALU.mult) \
                   .then_inc(s["tab_dve"], 1)

            def rotation(pi, kind):
                dve.wait_ge(s["tab_dve"], after(pi * 2 + kind + 2))
                dve.wait_ge(s["rotadd"], after(pi * 2 + kind))
                for o, a, t in ((0, 0, 0), (1, 1, 1), (2, 1, 0), (3, 0, 1)):
                    gain = (L_KA if kind == K else L_QA) + a
                    ins = dve.scalar_tensor_tensor(t4[:, o, :], bank[2 * kind + a][:, :], lp[:, gain:gain + 1],
                                                   tab[:, t, :], ALU.mult, ALU.mult)
                ins.then_inc(s["mul_dve"], 1)

            def maximum(n, u):
                un = n * UNITS + u
                sc = bank[5][:, :].rearrange("p (w k) -> p w k", w=UW)
                dve.wait_ge(s["s_mm"], after(un + 1))
                dve.tensor_reduce(mx[:, u % 2, :], sc, AX, ALU.max).then_inc(s["max_dve"], 1)
                dve.wait_ge(s["max_dve"], after(un + 1))
                dve.tensor_tensor(probs[:, u % 2], sc, mx[:, u % 2, :, None].to_broadcast([128, UW, 2 * WIN]),
                                  ALU.subtract).then_inc(s["sub_dve"], 1)

            def sums(n, u):
                un = n * UNITS + u
                dve.wait_ge(s["exp_act"], after(un + 1))
                dve.tensor_reduce(sm[:, u % 2, :], probs[:, u % 2], AX, ALU.add).then_inc(s["sum_dve"], 1)
                dve.wait_ge(s["sum_dve"], after(un + 1))
                dve.reciprocal(rc[:, u % 2, :], sm[:, u % 2, :]).then_inc(s["rec_dve"], 1)

            def heads_out(n, u):
                dve.wait_ge(s["pv_mm"], after((n * UNITS + u) * 2 + 1))
                for h in range(2):
                    ins = dve.tensor_copy(head_windows(u, h, 0), own_part(7, h))
                ins.then_inc(s["o0_out"], 1)

            def attention(n, b, ahead):
                for u in range(UNITS):
                    g = u // 2
                    pi = n * GROUPS + g
                    v_too = g + 1 < GROUPS or ahead
                    qk_too = g + 2 < GROUPS or ahead
                    if u % 2 == 0:
                        if ahead and g + 1 == GROUPS:
                            shifted_lo_v(n + 1)
                        if v_too:
                            tables(pi + 1, Q)
                            rotation(pi + 1, Q)
                        maximum(n, u)
                        if ahead and g + 2 == GROUPS:
                            shifted_lo(n + 1, b + 1)
                        sums(n, u)
                    else:
                        maximum(n, u)
                        sums(n, u)
                        if qk_too:
                            tables(pi + 2, K)
                            rotation(pi + 2, K)
                    if u:
                        heads_out(n, u - 1)
                heads_out(n, UNITS - 1)
                dve.wait_ge(s["y_mm"], after(n + 1))
                dve.tensor_tensor(xv[:, b, :], xv[:, b, :], bank[4][:, :], ALU.add).then_inc(s["resid_dve"], 1)

            with dve.Fori(0, DEPTH) as layer:
                n0 = layer * B
                dve.wait_ge(wo_in, layer * 32 + 32)
                shifted_lo(n0, 0)
                shifted_lo_v(n0)
                for p, kind in ((n0 * GROUPS, K), (n0 * GROUPS, Q), (n0 * GROUPS + 1, K)):
                    tables(p, kind)
                    rotation(p, kind)
                with dve.Fori(0, B - 1) as b:
                    attention(layer * B + b, b, True)
                attention(layer * B + (B - 1), B - 1, False)
                dve.wait_ge(ff_in, layer * 64 + 64)
                dve.memset(xf[64:128, :, 0:1], 0.0).then_inc(s["xf0_dve"], 1)
                dve.wait_ge(s["xf0_dve"], after(layer + 1))
                layer_norm(PRE + layer, lambda c: xf[:, c, :], lambda c: xh[:, c, :],
                           lp[:, L_G:L_G + 1], lp[:, L_B:L_B + 1])

                def result(b):
                    n = layer * B + b
                    dve.wait_ge(s["fy_mm"], after(n + 1))
                    dve.scalar_tensor_tensor(xv[:, b, :], bank[6 + b % 2][:, :], lp[:, L_B2:L_B2 + 1], xv[:, b, :],
                                             ALU.add, ALU.add).then_inc(s["fres_dve"], 1)

                for b in range(B):
                    for j, (f0, fn) in enumerate(FT):
                        f = (layer * B + b) * 3 + j
                        dve.wait_ge(s["gelu_act"], after(f + 1))
                        dve.wait_ge(s["fa_mm"], after(f + 1))
                        if b >= 2:
                            dve.wait_ge(s["fy_mm"], after(layer * B + b - 1))
                        dve.scalar_tensor_tensor(hh[0:fn, b % 2, j, :], bank[3 + j][0:fn, :],
                                                 lp[0:fn, L_B1A + j:L_B1A + j + 1], gg[0:fn, b % 2, j, :],
                                                 ALU.add, ALU.mult).then_inc(s["hh_dve"], 1)
                    if b:
                        result(b - 1)
                result(B - 1)

            dve.wait_ge(s["fres_dve"], after(DEPTH * B))
            for b in range(B):
                dve.tensor_tensor(accv[:, b, :], accv[:, b, :], xv[:, b, :], ALU.add).then_inc(z["fin_sum"], 1)
            dve.wait_ge(z["fin_sum"], B)
            layer_norm(PRE + DEPTH, lambda c: accv[:, c, :], lambda c: xn2[:, c, :], 1.0, 0.0)
            for b in range(B):
                dve.wait_ge(z["g1_mm"], b + 1)
                if b:
                    dve.wait_ge(z["z_mm"], b)
                dve.tensor_copy(g1s[0:LR, :], bank[6][0:LR, :]).then_inc(z["g1_copy"], 1)
                dve.wait_ge(z["gg_exp"], b + 1)
                link(dve.tensor_scalar(gs[:, b, :], gs[:, b, :], 1.0, None, ALU.add))
                link(dve.reciprocal(gs[:, b, :], gs[:, b, :]))
                dve.scalar_tensor_tensor(gs[:, b, :], bank[2 + b % 2][:, :], col(P_GW), gs[:, b, :], ALU.mult, ALU.mult) \
                   .then_inc(z["gg_dve"], 1)
                dve.wait_ge(z["z_mm"], b + 1)
                if b:
                    dve.wait_ge(z["abs_act"], b)
                dve.tensor_scalar(zb[0:64, :], bank[7][0:64, :], col(P_BGK, 64), None, ALU.add).then_inc(z["z_copy"], 1)
                dve.wait_ge(z["z_copy"], b + 1)
                dve.wait_ge(z["gln_act"], b + 1)
                dve.scalar_tensor_tensor(egk[0:64, b, :], zb[0:64, :], 0.0, az[0:64, 0, :], ALU.min, ALU.subtract) \
                   .then_inc(z["gk_dve"], 1)

            N = B * DK

            def kv(t):
                dve.wait_ge(z["rk_mm"], t + 1)
                if t >= 2:
                    dve.wait_ge(z["scan_dve"], t - 1)
                dve.tensor_tensor(kvb[:, t % 2, :], bank[t % 2][:, :], vt[:, t // DK, :], ALU.mult).then_inc(z["kv_dve"], 1)

            def scan(t):
                dve.wait_ge(z["rg_mm"], t + 1)
                dve.wait_ge(z["kv_dve"], t + 1)
                if t >= 2:
                    dve.wait_ge(z["qs_dve"], t - 1)
                dve.tensor_tensor_scan(sst[:, t % 2, :], bank[2 + t % 2][:, :], kvb[:, t % 2, :], 0.0, ALU.mult, ALU.add) \
                   .then_inc(z["scan_dve"], 1)

            def qs(t):
                dve.wait_ge(z["rq_mm"], t + 1)
                dve.wait_ge(z["scan_dve"], t + 1)
                if t >= 2:
                    dve.wait_ge(z["oadd"], t - 1)
                dve.tensor_tensor(tmp[:, t % 2, :], bank[4 + t % 2][:, :], sst[:, t % 2, :], ALU.mult).then_inc(z["qs_dve"], 1)

            for t in range(N + 2):
                if t < N:
                    kv(t)
                if 1 <= t <= N:
                    scan(t - 1)
                if t >= 2:
                    qs(t - 2)
            for b in range(B):
                dve.wait_ge(z["gr_act"], b + 1)
                link(dve.tensor_tensor(go[:, b, :], go[:, b, :], az[:, 1, :], ALU.mult))
                dve.tensor_tensor(go[:, b, :], go[:, b, :], gs[:, b, :], ALU.mult).then_inc(z["gn_dve"], 1)
                dve.wait_ge(z["go_mm"], b + 1)
                dve.tensor_tensor(accv[:, b, :], accv[:, b, :], bank[7][:, :], ALU.add).then_inc(z["x1_dve"], 1)
            dve.wait_ge(z["lg_copy"], 1)
            for m in range(TILES):
                ins = dve.max(top8[:, m, :], lg[:, m, :])
            link(ins)
            for m in range(TILES):
                ins = dve.max_index(topi[:, 8 * m:8 * m + 8], top8[:, m, :], lg[:, m, :])
            link(ins)
            dve.tensor_copy(topf, topi[:, :].rearrange("p (m e) -> p m e", e=8))
            dve.tensor_tensor(gw12[:, 0, :], top8[:, :, 1], top8[:, :, 0], ALU.subtract).then_inc(z["route"], 1)
            dve.wait_ge(z["route"], 2)
            link(dve.tensor_scalar(gw12[:, 1, :], gw12[:, 0, :], 1.0, None, ALU.add))
            link(dve.reciprocal(gw12[:, 1, :], gw12[:, 1, :]))
            link(dve.tensor_tensor(gw12[:, 2, :], gw12[:, 0, :], gw12[:, 1, :], ALU.mult))
            dve.wait_ge(z["iota_pool"], 8)

            def of_expert(x):
                return x[:, :, None].to_broadcast([128, TILES, 8])

            each = iot[:, None, :].to_broadcast([128, TILES, 8])
            dve.tensor_tensor(gate, each, topf[:, :, 0:1].to_broadcast([128, TILES, 8]), ALU.is_equal)
            link(dve.tensor_tensor(gpart, each, topf[:, :, 1:2].to_broadcast([128, TILES, 8]), ALU.is_equal))
            dve.tensor_tensor(gate, gate, of_expert(gw12[:, 1, :]), ALU.mult)
            link(dve.tensor_tensor(gpart, gpart, of_expert(gw12[:, 2, :]), ALU.mult))
            link(dve.tensor_tensor(gate, gate, gpart, ALU.add))
            dve.wait_ge(z["tok_copy"], B)
            for t in range(B * E):
                q, e = t // E, t % E
                dve.wait_ge(z["ey_mm"], t + 1)
                if e:
                    dve.wait_ge(z["ey_dve"], t)
                for m in range(4):
                    tile = 4 * q + m
                    ins = dve.scalar_tensor_tensor(otok[:, tile, :], bank[6 + t % 2][:, 128 * m:128 * m + 128],
                                                   gate[:, tile, e:e + 1], otok[:, tile, :], ALU.mult, ALU.add)
                ins.then_inc(z["ey_dve"], 1)

        @block.gpsimd
        def _(pool):
            for n in pool_s.values():
                pool.sem_inc(n, 1)

            def square_sum(pi, kind):
                pool.wait_ge(s["sq_act"], after(pi * 2 + kind + 1))
                pool.tensor_tensor(sqs[:, kind, :], sqb[:, kind, 0, :], sqb[:, kind, 1, :], ALU.add).then_inc(s["sqadd"], 1)

            def rotate(pi, g, kind):
                pool.wait_ge(s["mul_dve"], after(pi * 2 + kind + 2))
                if kind == Q:
                    pool.wait_ge(s["place_act"], after(pi))
                dst = qst if kind == Q else kb[:, g % 2, :, WIN:]
                pool.tensor_tensor(dst[:, 0, :], t4[:, 0, :], t4[:, 1, :], ALU.subtract)
                pool.tensor_tensor(dst[:, 1, :], t4[:, 2, :], t4[:, 3, :], ALU.add).then_inc(s["rotadd"], 1)

            def normalise(n, u):
                pool.wait_ge(s["rec_dve"], after(n * UNITS + u + 1))
                pool.tensor_tensor(probs[:, u % 2], probs[:, u % 2],
                                   rc[:, u % 2, :, None].to_broadcast([128, UW, 2 * WIN]), ALU.mult) \
                    .then_inc(s["norm_pool"], 1)

            def attention(n, ahead):
                for u in range(UNITS):
                    g = u // 2
                    pi = n * GROUPS + g
                    v_too = g + 1 < GROUPS or ahead
                    qk_too = g + 2 < GROUPS or ahead
                    if u % 2 == 0:
                        if v_too:
                            rotate(pi + 1, (g + 1) % GROUPS, Q)
                        normalise(n, u)
                        if qk_too:
                            square_sum(pi + 2, K)
                    else:
                        normalise(n, u)
                        if qk_too:
                            square_sum(pi + 2, Q)
                            rotate(pi + 2, g % 2, K)

            with pool.Fori(0, DEPTH) as layer:
                n0 = layer * B
                pool.wait_ge(z["zeroed"], 1)
                pool.wait_ge(wqkv_in, layer * 16 + 16)
                pool.wait_ge(s["v_mm"], after(n0 * 16))

                def halves(w, p, a):
                    return w[:, p * INNER:(p + 1) * INNER].rearrange("p (g a h d) -> p g a h d", g=GROUPS, a=2, h=GH)[:, :, a]

                def whole(w, p, a):
                    return w[:, p * INNER:(p + 1) * INNER].rearrange("p (g h a d) -> p g h a d", g=GROUPS, a=2, h=GH)[:, :, :, a]

                for p in range(2):
                    for a in range(2):
                        pool.tensor_tensor(halves(wq_hi[:, :], p, a), whole(wraw, p, a),
                                           consts[:, 1:2, None, None].to_broadcast([128, GROUPS, GH, HALF]), ALU.mult)
                pool.tensor_tensor(wq_hi[:, 2 * INNER:], wraw[:, 2 * INNER:], consts[:, 1:2].to_broadcast([128, INNER]), ALU.mult) \
                    .then_inc(s["split_hi"], 1)
                pool.wait_ge(s["split_hi"], after(layer + 1))
                for p in range(2):
                    for a in range(2):
                        pool.tensor_tensor(halves(wq_lo[:, :], p, a), whole(wraw, p, a),
                                           halves(wq_hi[:, :].bitcast(F32), p, a), ALU.subtract)
                pool.tensor_tensor(wq_lo[:, 2 * INNER:], wraw[:, 2 * INNER:], wq_hi[:, 2 * INNER:].bitcast(F32),
                                   ALU.subtract).then_inc(s["split"], 1)
                p0 = n0 * GROUPS
                square_sum(p0, K)
                square_sum(p0, Q)
                rotate(p0, 0, K)
                rotate(p0, 0, Q)
                square_sum(p0 + 1, K)
                square_sum(p0 + 1, Q)
                rotate(p0 + 1, 1, K)
                with pool.Fori(0, B - 1) as b:
                    attention(layer * B + b, True)
                attention(layer * B + (B - 1), False)

            pool.wait_ge(s["fres_dve"], after(DEPTH * B))
            for e in range(E):
                pool.memset(iot[:, e:e + 1], float(e)).then_inc(z["iota_pool"], 1)
            for t in range(B * DK):
                b = t // DK
                pool.wait_ge(z["qs_dve"], t + 1)
                if t % DK == 0:
                    pool.tensor_copy(go[:, b, :], tmp[:, t % 2, :]).then_inc(z["oadd"], 1)
                else:
                    pool.wait_ge(z["oadd"], t)
                    pool.tensor_tensor(go[:, b, :], go[:, b, :], tmp[:, t % 2, :], ALU.add).then_inc(z["oadd"], 1)


def rotary():
    import numpy as np
    f = np.float32
    half = np.arange(0, DH, 2, dtype=f)
    inv_freq = (1.0 / f(10000.0) ** (half / f(DH))).astype(f)
    t = np.arange(T, dtype=f)
    freqs = (t[:, None] * inv_freq[None, :]).astype(f)
    base = ((half + f(0.4 * DH)) / f(1.4 * DH)).astype(f)
    power = ((t - f(T // 2)) / f(WIN // 2)).astype(f)
    scale = (base[None, :] ** power[:, None]).astype(f)
    cos, sin = np.cos(freqs), np.sin(freqs)
    tabs = np.stack([cos * scale, sin * scale, cos * (1 / scale), sin * (1 / scale)]).astype(f)
    return np.ascontiguousarray(np.tile(tabs.transpose(2, 0, 1), (GH, 1, 1)))


def masks():
    import numpy as np
    q = np.arange(128)[:, None] % WIN
    k = np.arange(2 * WIN)[None, :]
    seen = np.where(k < WIN, q <= k, q >= k - WIN)
    m = np.where(seen, 0.0, -1e30)
    unit = np.tile(m, (1, UW))
    first = unit.copy()
    first[:, 0:WIN] = -1e30
    return np.concatenate([first, unit], axis=1).astype(np.float32)


def kernel(**inputs):
    import numpy as np
    import concourse.bacc as bacc
    from concourse.bass_utils import run_bass_kernel_spmd as run

    a = {k: np.ascontiguousarray(v) for k, v in inputs.items()}

    def column(v):
        v = v.reshape(-1)
        return np.concatenate([v, np.zeros(128 - v.size, v.dtype)])

    p0 = "L0_attn_"
    params = np.stack([column(v) for v in (
        a[p0 + "time_decay"], a[p0 + "time_first"], a[p0 + "ln1_g"], a[p0 + "ln1_b"], a[p0 + "ln2_g"], a[p0 + "ln2_b"],
        a[p0 + "mix_k"], a[p0 + "mix_v"], a[p0 + "mix_r"], a[p0 + "cmix_k"], a[p0 + "cmix_r"],
        np.tile(a["L1_attn_gw"], NH), a["L1_attn_bgk2"])], axis=1)
    f0 = "L0_ffn_"
    lparams = []
    for i in range(DEPTH):
        q, k, b1 = a[f0 + "q_scale"][i], a[f0 + "k_scale"][i], a[f0 + "b1"][i]
        cols = [np.tile(q[:HALF], GH), np.tile(q[HALF:], GH), np.tile(k[:HALF], GH), np.tile(k[HALF:], GH),
                a[f0 + "ln_g"][i], a[f0 + "ln_b"][i]]
        cols += [column(b1[s:s + n]) for s, n in FT] + [column(b1[FF + s:FF + s + n]) for s, n in FT]
        cols.append(a[f0 + "b2"][i])
        lparams.append(np.stack(cols, axis=1))
    arrays = {
        "x": a["L0_attn_x"], "params": params, "lparams": np.stack(lparams),
        "w_tk": a[p0 + "w_tk"], "w_tv": a[p0 + "w_tv"], "w_tr": a[p0 + "w_tr"], "w_ck": a[p0 + "w_ck"],
        "w_cv": a[p0 + "w_cv"], "w_cr": a[p0 + "w_cr"],
        "wqkv": a[f0 + "Wqkv"], "wo": a[f0 + "Wo"], "w1": a[f0 + "W1"], "w2": a[f0 + "W2"],
        "gwq": a["L1_attn_Wq"], "gwk": a["L1_attn_Wk"], "gwv": a["L1_attn_Wv"], "gwg1": a["L1_attn_Wgk1"],
        "gwg2": a["L1_attn_Wgk2"], "gwg": a["L1_attn_Wg"], "gwo": a["L1_attn_Wo"],
        "router_t": a["L1_ffn_router_w"].T, "ew1": a["L1_ffn_w1"], "ew2": a["L1_ffn_w2"],
        "rot": rotary(), "blocks": np.kron(np.eye(4), np.ones((32, 32))).astype(np.float32),
        "ident": np.eye(128, dtype=np.float32), "mask": masks(),
    }
    nc = bacc.Bacc("TRN2", target_bir_lowering=False, num_devices=1)
    data, args = {}, []
    for name, v in arrays.items():
        v = np.ascontiguousarray(v)
        data[f"in_{name}"] = v
        args.append(nc.dram_tensor(f"in_{name}", v.shape, mybir.dt.from_np(v.dtype), kind="ExternalInput").ap())
    out = nc.dram_tensor("out_0", (B, T, C), F32, kind="ExternalOutput").ap()
    program(nc, *args, out)
    r = run(nc, [data], core_ids=[0])
    return r.results[0]["out_0"]
```

```python
from contextlib import ExitStack

import concourse.bass as bass
from concourse import mybir

F32 = mybir.dt.float32
F32R = mybir.dt.float32r
BF16 = mybir.dt.bfloat16
ALU = mybir.AluOpType
ACT = mybir.ActivationFunctionType
AX = mybir.AxisListType.X

B, T, C = 4, 512, 128
NTOK = B * T
TILES = NTOK // 128
DEPTH, HEADS, DH, WIN = 6, 16, 64, 32
HALF = DH // 2
GH = 4
GROUPS = HEADS // GH
NW = T // WIN
UW = NW // 2
UNITS = 2 * GROUPS
INNER = HEADS * DH
GD = GH * DH
QK_SCALE = 8.0
FF = int(C * 4 * 2 / 3)
FT = [(0, 128), (128, 128), (256, FF - 256)]
NH, DK, DV, LR = 4, 16, 32, 16
GATE_NORM = 16.0
Q_SCALE = float(DK) ** -0.5
E, H2 = 8, 256
EPS = 1e-5
NEG_INF = -1e38
RN_MAX = 1e12
LN_SCALE = float(2 ** 20)

P_W, P_U, P_G1, P_B1, P_G2, P_B2, P_MK, P_MV, P_MR, P_CK, P_CR, P_GW, P_BGK = range(13)
NPAR = 13
L_QA, L_QB, L_KA, L_KB, L_G, L_B, L_B1A, L_B1G, L_B2 = 0, 1, 2, 3, 4, 5, 6, 9, 12
NLP = 13
K, Q = 0, 1
PRE = 3


def after(k):
    return k + 1


def slot(w):
    return 4 * (w // 4) + 2 * (w % 2) + w % 4 // 2


def program(nc, x, params, lparams, w_tk, w_tv, w_tr, w_ck, w_cv, w_cr, wqkv, wo, w1, w2,
            gwq, gwk, gwv, gwg1, gwg2, gwg, gwo, router_t, ew1, ew2,
            rot, blocks, ident, mask, out):
    ctx = ExitStack()
    with ctx:
        def sem(name):
            return ctx.enter_context(nc.semaphore(name))

        def sbuf(name, cols, dt=F32):
            return ctx.enter_context(nc.sbuf_tensor(name, [128, cols], dt))

        bank = [ctx.enter_context(nc.psum_tensor(f"bank{i}", [128, 512], F32)) for i in range(8)]

        acc = sbuf("acc", NTOK)
        xres = sbuf("xres", NTOK)
        par = sbuf("par", NPAR)
        ident_s = sbuf("ident_s", 128)
        blocks_s = sbuf("blocks_s", 128)
        mean_s = sbuf("mean_s", 128)
        identb = sbuf("identb", 128, BF16)
        maskb = sbuf("maskb", 2 * 512, BF16)
        consts = sbuf("consts", 4)
        wq_hi = sbuf("wq_hi", 3 * INNER, F32R)
        wq_lo = sbuf("wq_lo", 3 * INNER, F32R)
        xs_hi = sbuf("xs_hi", WIN + T, F32R)
        xs_lo = sbuf("xs_lo", WIN + T, F32R)
        xv_hi = sbuf("xv_hi", WIN + T, F32R)
        xv_lo = sbuf("xv_lo", WIN + T, F32R)
        ARENA = 38300
        arena = sbuf("arena", ARENA)
        at = [0]

        def take(cols):
            a = arena[:, at[0]:at[0] + cols]
            at[0] += cols
            assert at[0] <= ARENA, at[0]
            return a

        accv = acc[:, :].rearrange("p (b t) -> p b t", b=B)
        xv = xres[:, :].rearrange("p (b t) -> p b t", b=B)

        xc = take(4 * T).rearrange("p (x t) -> p x t", x=4)
        lsq = take(2 * T).rearrange("p (x t) -> p x t", x=2)
        lln = take(2 * T).rearrange("p (x t) -> p x t", x=2)
        lrs = take(2 * T).rearrange("p (x t) -> p x t", x=2)
        wraw = take(3 * INNER)
        wo_s = take(8 * C).rearrange("p (k c) -> p k c", k=8)
        w1_s = take(2 * FF)
        w2_s = take(3 * C).rearrange("p (k c) -> p k c", k=3)
        lp = take(NLP)
        rot_s = take(4 * T).rearrange("p (k t) -> p k t", k=4)
        phase_at = at[0]
        t4, sqs, lnb, rnb = xc, lsq, lln, lrs
        qbd = take(2 * 2 * GH * T).rearrange("p (s a w h t) -> p s a w h t", s=2, a=2, w=NW, h=GH)
        kb = take(2 * 2 * (WIN + T)).rearrange("p (s a t) -> p s a t", s=2, a=2)
        tab = take(2 * T).rearrange("p (x t) -> p x t", x=2)
        vflat = take(2 * 2 * 4 * GD)
        vb = vflat.rearrange("p (s o m d) -> p s o m d", s=2, o=2, m=4)
        qst = take(2 * T).rearrange("p (a t) -> p a t", a=2)
        sqb = take(4 * T).rearrange("p (x a t) -> p x a t", x=2, a=2)
        pts = take(4 * 2 * 128).rearrange("p (j k c) -> p j k c", j=4, k=2)
        hflat = take(1024)
        probs = hflat.rearrange("p (s w k) -> p s w k", s=2, w=UW)
        oflat = take(8 * T)
        ot = oflat.rearrange("p (k t) -> p k t", k=8)
        mx = take(2 * UW).rearrange("p (s w) -> p s w", s=2)
        sm = take(2 * UW).rearrange("p (s w) -> p s w", s=2)
        rc = take(2 * UW).rearrange("p (s w) -> p s w", s=2)
        xf = oflat[:, 0:NTOK].rearrange("p (b t) -> p b t", b=B)
        xh = oflat[:, NTOK:2 * NTOK].rearrange("p (b t) -> p b t", b=B)
        gg = vflat[:, 0:3072].rearrange("p (s j t) -> p s j t", s=2, j=3)
        hh_at = at[0] - 3 * 2 * UW - 8 * T - 1024
        hh = arena[:, hh_at:hh_at + 3072].rearrange("p (s j t) -> p s j t", s=2, j=3)

        at[0] = phase_at
        xflat = take(NTOK)
        xtok = xflat.rearrange("p (m c) -> p m c", c=C)
        ckx = xflat.rearrange("p (b t) -> p b t", b=B)
        hb = take(B * (T + 1)).rearrange("p (b t) -> p b t", b=B)
        h2b = take(B * (T + 1)).rearrange("p (b t) -> p b t", b=B)
        traw = take(4 * C)
        tmix = take(2 * 8 * C).rearrange("p (x c) -> p x c", x=2)
        tcv = take(4 * C).rearrange("p (k c) -> p k c", k=4)
        om = take(5)
        wfull = take(T)
        rwx = take(NTOK).rearrange("p (b t) -> p b t", b=B)
        m_runs = [take(T + 1) for _ in range(2)]
        s_runs = [take(T + 1) for _ in range(2)]
        pps = [take(T + 1) for _ in range(2)]
        a_runs = [take(T + 1) for _ in range(2)]
        argss = [take(2 * T).rearrange("p (x t) -> p x t", x=2) for _ in range(2)]
        kws = [take(T) for _ in range(2)]
        kmxs = [take(T) for _ in range(2)]
        bvs = [take(T) for _ in range(2)]
        kkb = take(4 * T).rearrange("p (x t) -> p x t", x=4)
        rrs = [take(T) for _ in range(2)]
        maskf = take(2 * 512)

        at[0] = phase_at
        xn2 = take(NTOK).rearrange("p (b t) -> p b t", b=B)
        gwk_s, gwq_s, gwv_s, gwg2_s, gwg_s, gwo_s = (take(128) for _ in range(6))
        gwg1_s = take(LR)
        vt = take(NTOK).rearrange("p (b t) -> p b t", b=B)
        egk = take(NTOK).rearrange("p (b t) -> p b t", b=B)
        gs = take(NTOK).rearrange("p (b t) -> p b t", b=B)
        go = take(NTOK).rearrange("p (b t) -> p b t", b=B)
        kvb = take(2 * T).rearrange("p (x t) -> p x t", x=2)
        sst = take(2 * T).rearrange("p (x t) -> p x t", x=2)
        tmp = take(2 * T).rearrange("p (x t) -> p x t", x=2)
        zb = take(T)
        g1s = take(T)
        az = take(2 * T).rearrange("p (x t) -> p x t", x=2)
        rt_s = take(E)
        top8 = take(TILES * 8).rearrange("p (m e) -> p m e", m=TILES)
        lg = take(TILES * 8).rearrange("p (m e) -> p m e", m=TILES)
        topi = ctx.enter_context(nc.sbuf_tensor("topi", [128, TILES * 8], mybir.dt.uint32))
        topf = take(TILES * 8).rearrange("p (m e) -> p m e", m=TILES)
        gate = take(TILES * 8).rearrange("p (m e) -> p m e", m=TILES)
        gpart = take(TILES * 8).rearrange("p (m e) -> p m e", m=TILES)
        gw12 = take(3 * TILES).rearrange("p (x m) -> p x m", x=3)
        iot = take(E)
        end_at = at[0]
        at[0] = 5 * 1024
        ew1_s = take(E * 2 * C).rearrange("p (e h c) -> p e h c", e=E, h=2)
        ew2_s = take(E * H2).rearrange("p (e f) -> p e f", e=E)
        assert at[0] <= phase_at
        at[0] = end_at
        w1t = take(E * H2).rearrange("p (e f) -> p e f", e=E)
        w2t = take(E * 2 * C).rearrange("p (e h c) -> p e h c", e=E, h=2)
        otok = take(NTOK).rearrange("p (m c) -> p m c", c=C)
        ht = take(2 * 2 * T).rearrange("p (s h t) -> p s h t", s=2, h=2)
        sel = wq_hi[:, 0:DK * 128].rearrange("p (i h r) -> p i h r", i=DK, h=NH)
        parts = [wq_lo[:, T * i:T * i + T] for i in range(6)] + [wq_hi[:, DK * 128 + T * i:DK * 128 + T * i + T] for i in range(2)] \
            + [w[:, 0:T] for w in (xs_hi, xs_lo, xv_hi, xv_lo)]
        k_parts, q_parts, g_parts = parts[0:4], parts[4:8], parts[8:12]

        def head_windows(u, h, pair):
            g, hf = u // 2, u % 2
            rows = ot[64 * h:64 * h + 64, 2 * g + pair, 256 * hf:256 * hf + 256]
            return rows.rearrange("p (w q) -> p w q", w=UW)

        def own_part(n, h):
            return bank[n][64 * h:64 * h + 64, :].rearrange("p (w h q) -> p w h q", w=UW, h=2)[:, :, h]

        def group(names):
            return {n: sem(n) for n in names.split()}

        pe_s = group("mean_mm var_mm q_mm k_mm v_mm n2_mm s_mm t_mm pv_mm y_mm fg_mm fa_mm fy_mm")
        act_s = group("ln_sq ln_log ln_rstd sq_act log_act rn_act v_out exp_act pt_out o1_out xs_hi_act xv_hi_act placed_act xf_act gelu_act")
        dve_s = group("ln_xc ln_n ln_out placed_dve max_dve sub_dve sum_dve rec_dve tab_dve mul_dve o0_out resid_dve xv_lo_dve xf0_dve hh_dve fres_dve")
        pool_s = group("split_hi split sqadd rotadd norm_pool xs_lo_pool")
        s = {**pe_s, **act_s, **dve_s, **pool_s}
        wqkv_in, wo_in, ff_in = sem("wqkv_in"), sem("wo_in"), sem("ff_in")
        v_shifted = [sem("v_shifted_even"), sem("v_shifted_odd")]
        z = group("const_in x_in tm_in rot_in fin_in out_done zeroed padded x_turned x_copied "
                  "kvr_mm ck_mm cr_mm cv_mm mixed dve_link decay_arg decay_exp sum_scan log_sum carry_arg carry_exp "
                  "out_arg out_exp gate_exp rwkv_even rwkv_odd ck_in cm_gate relu_dve kk_act cm_done "
                  "fin_sum sel_made kp_mm kp_hi kp_lo qp_mm qp_hi qp_lo eg_hi eg_lo g1_mm g1_copy z_mm z_copy abs_act gexp_act gln_act gk_dve egk_act "
                  "gv_mm gv_copy gg_mm gg_dve gg_act "
                  "rk_mm rg_mm rq_mm kv_dve scan_dve qs_dve oadd gsq_act gms_mm gl_act gr_act gn_dve go_mm x1_dve "
                  "tok_mm lg_mm lg_copy route ew_turned ew_copied eh_mm eh_act ey_mm ey_dve out_dve iota_pool")
        RW_STEPS = 13
        rwkv = (z["rwkv_even"], z["rwkv_odd"])
        block = ctx.enter_context(nc.Block())

        @block.sync
        def _(sp):
            for dst, src in ((ident_s, ident), (blocks_s, blocks), (par, params)):
                sp.dma_start(dst[:, :], src).then_inc(z["const_in"], 16)
            sp.dma_start(maskf, mask).then_inc(z["const_in"], 16)
            xtiles = x.rearrange("b (m p) c -> p (b m) c", p=128)
            for i in range(4):
                sp.dma_start(xtok[:, 4 * i:4 * i + 4, :], xtiles[:, 4 * i:4 * i + 4, :]).then_inc(z["x_in"], 16)
            for n, src in enumerate((w_tk, w_tv, w_tr, w_cr)):
                sp.dma_start(traw[:, n * C:(n + 1) * C], src).then_inc(z["tm_in"], 16)
            sp.dma_start(tmix[:, 0, 4 * C:8 * C], w_ck).then_inc(z["tm_in"], 16)
            sp.dma_start(tcv, w_cv.rearrange("(k p) c -> p k c", p=128)).then_inc(z["tm_in"], 16)
            sp.dma_start(rot_s, rot).then_inc(z["rot_in"], 16)

            with sp.Fori(0, DEPTH) as layer:
                sp.wait_ge(s["split"], after(layer))
                sp.dma_start(wraw, wqkv[bass.ds(layer, 1), :, :].rearrange("l c n -> c (l n)")).then_inc(wqkv_in, 16)
                sp.wait_ge(s["y_mm"], after(layer * B))
                sp.dma_start(wo_s, wo[bass.ds(layer, 1), :, :].rearrange("l (k p) c -> p (l k) c", p=128)).then_inc(wo_in, 16)
                sp.dma_start(lp[:, 0:4], lparams[bass.ds(layer, 1), :, 0:4].rearrange("l p c -> p (l c)")).then_inc(wo_in, 16)
                sp.wait_ge(s["fres_dve"], after(layer * B))
                sp.dma_start(w1_s, w1[bass.ds(layer, 1), :, :].rearrange("l c n -> c (l n)")).then_inc(ff_in, 16)
                sp.dma_start(w2_s[:, 0:2, :], w2[bass.ds(layer, 1), 0:256, :].rearrange("l (k p) c -> p (l k) c", p=128)).then_inc(ff_in, 16)
                sp.dma_start(w2_s[0:FF - 256, 2, :], w2[bass.ds(layer, 1), 256:FF, :].rearrange("l p c -> p (l c)")).then_inc(ff_in, 16)
                sp.dma_start(lp[:, 4:NLP], lparams[bass.ds(layer, 1), :, 4:NLP].rearrange("l p c -> p (l c)")).then_inc(ff_in, 16)

            sp.wait_ge(s["fres_dve"], after(DEPTH * B))
            for dst, src in ((gwk_s[:, 0:64], gwk), (gwk_s[:, 64:128], gwk), (gwq_s[:, 0:64], gwq), (gwq_s[:, 64:128], gwq),
                             (gwg2_s[0:LR, 0:64], gwg2), (gwg2_s[0:LR, 64:128], gwg2), (gwv_s, gwv), (gwg1_s, gwg1),
                             (gwg_s, gwg), (gwo_s, gwo), (rt_s, router_t),
                             (ew1_s, ew1.rearrange("e (h p) c -> p e h c", p=128)),
                             (ew2_s, ew2.rearrange("e p f -> p e f"))):
                sp.dma_start(dst, src).then_inc(z["fin_in"], 16)
            outv = out.rearrange("b (m p) c -> p (b m) c", p=128)
            for q in range(B):
                sp.wait_ge(z["out_dve"], q + 1)
                sp.dma_start(outv[:, 4 * q:4 * q + 4, :], otok[:, 4 * q:4 * q + 4, :]).then_inc(z["out_done"], 16)
            sp.wait_ge(z["out_done"], 16 * B)

        @block.tensor
        def _(pe):
            for n in pe_s.values():
                pe.sem_inc(n, 1)

            def layer_norm(i, src):
                for c in range(B):
                    pe.wait_ge(s["ln_xc"], after(i * B + c))
                    pe.matmul(bank[6][:, :], mean_s[:, :], src(c), start=True, stop=True).then_inc(s["mean_mm"], 1)
                    if c > 0:
                        variance(i, c - 1)
                variance(i, B - 1)

            def variance(i, c):
                pe.wait_ge(s["ln_sq"], after(i * B + c + 1))
                pe.wait_ge(s["ln_log"], after(i * B + c))
                pe.matmul(bank[7][:, :], mean_s[:, :], lsq[:, c % 2, :], start=True, stop=True).then_inc(s["var_mm"], 1)

            pe.wait_ge(z["const_in"], 16 * 4)
            for m in range(TILES):
                if m % 4 == 0:
                    pe.wait_ge(z["x_in"], 16 * 4)
                mm = pe.transpose(bank[m // 4][:, 128 * (m % 4):128 * (m % 4) + 128], xtok[:, m, :], ident_s[:, :])
            mm.then_inc(z["x_turned"], 1)
            pe.wait_ge(z["x_copied"], B)
            pe.wait_ge(z["zeroed"], 1)
            layer_norm(0, lambda c: accv[:, c, :])
            pe.wait_ge(s["ln_out"], after(B))
            layer_norm(1, lambda c: xv[:, c, :])
            pe.wait_ge(z["mixed"], 1)
            for b in range(B):
                pe.wait_ge(s["ln_out"], after(B + b + 1))
                if b >= 2:
                    pe.wait_ge(rwkv[b % 2], RW_STEPS * (b // 2))
                for j in range(3):
                    o = bank[j + 3 * (b % 2)][:, :]
                    pe.matmul(o, tmix[:, 0, j * C:(j + 1) * C], hb[:, b, 1:T + 1], start=True, stop=False)
                    mm = pe.matmul(o, tmix[:, 1, j * C:(j + 1) * C], hb[:, b, 0:T], start=False, stop=True)
                mm.then_inc(z["kvr_mm"], 1)
            for done in rwkv:
                pe.wait_ge(done, RW_STEPS * (B // 2))
            layer_norm(2, lambda c: rwx[:, c, :])
            for b in range(B):
                pe.wait_ge(z["ck_in"], b + 1)
                for j in range(4):
                    if b >= 1:
                        pe.wait_ge(z["kk_act"], 4 * (b - 1) + j + 1)
                    o = bank[j][:, :]
                    w = slice((4 + j) * C, (5 + j) * C)
                    pe.matmul(o, tmix[:, 0, w], ckx[:, b, :], start=True, stop=True).then_inc(z["ck_mm"], 1)
                if b >= 1:
                    pe.wait_ge(z["cm_gate"], b)
                w = slice(3 * C, 4 * C)
                pe.matmul(bank[4][:, :], tmix[:, 0, w], h2b[:, b, 1:T + 1], start=True, stop=False)
                pe.matmul(bank[4][:, :], tmix[:, 1, w], h2b[:, b, 0:T], start=False, stop=True).then_inc(z["cr_mm"], 1)
                if b >= 1:
                    pe.wait_ge(z["cm_done"], b)
                for j in range(4):
                    pe.wait_ge(z["kk_act"], 4 * b + j + 1)
                    mm = pe.matmul(bank[5][:, :], tcv[:, j, :], kkb[:, j, :], start=(j == 0), stop=(j == 3))
                mm.then_inc(z["cv_mm"], 1)
            pe.wait_ge(z["cm_done"], B)

            def three(o, w_at, rhs, w_first):
                hi, lo = rhs
                if w_first:
                    pe.matmul(o, w_at(wq_hi), hi, start=True, stop=False)
                    pe.matmul(o, w_at(wq_lo), hi, start=False, stop=False)
                    return pe.matmul(o, w_at(wq_hi), lo, start=False, stop=True)
                pe.matmul(o, hi, w_at(wq_hi), start=True, stop=False)
                pe.matmul(o, hi, w_at(wq_lo), start=False, stop=False)
                return pe.matmul(o, lo, w_at(wq_hi), start=False, stop=True)

            def project(pi, g, kind):
                pe.wait_ge(s["mul_dve"], after(pi * 2 + kind))
                for a in range(2):
                    at_ = (INNER if kind == K else 0) + g * GD + a * 128
                    mm = three(bank[2 * kind + a][:, :], lambda w: w[:, at_:at_ + 128],
                               (xs_hi[:, WIN:], xs_lo[:, WIN:]), True)
                mm.then_inc(s["k_mm" if kind == K else "q_mm"], 1)

            def norms(pi, kind, n_bank=4):
                pe.wait_ge(s["sqadd"], after(pi * 2 + kind + 1))
                pe.matmul(bank[n_bank][:, :], blocks_s[:, :], sqs[:, kind, :], start=True, stop=True).then_inc(s["n2_mm"], 1)

            def values(pi, g, c):
                for j in range(2):
                    t0 = WIN + 128 * (2 * c + j)
                    mm = three(bank[4][:, j * GD:(j + 1) * GD],
                               lambda w: w[:, 2 * INNER + g * GD:2 * INNER + (g + 1) * GD],
                               (xv_hi[:, t0:t0 + 128], xv_lo[:, t0:t0 + 128]), False)
                mm.then_inc(s["v_mm"], 1)

            def scores(n, u):
                g, hf, un = u // 2, u % 2, n * UNITS + u
                pi = n * GROUPS + g
                pe.wait_ge(s["sub_dve"], after(un))
                if u == 0:
                    pe.wait_ge(s["log_act"], after(pi * 2 + 4))
                if hf == 0:
                    pe.wait_ge(s["placed_act"], after(pi + 1))
                    pe.wait_ge(s["placed_dve"], after(pi + 1))
                    pe.wait_ge(s["rotadd"], after(pi * 2 + 2))
                for wl in range(UW):
                    t0 = (hf * UW + wl) * WIN
                    at_ = 64 * slot(wl)
                    for a in range(2):
                        pe.matmul(bank[5][:, at_:at_ + 64],
                                       qbd[:, g % 2, a, hf * UW + wl].rearrange("p h t -> p (h t)"),
                                       kb[:, g % 2, a, t0:t0 + 2 * WIN],
                                  start=(a == 0 and wl == 0), stop=False)
                pe.matmul(bank[5][:, :], identb[:, :], maskb[:, 512 * (hf > 0):512 * (hf > 0) + 512],
                          start=False, stop=True).then_inc(s["s_mm"], 1)

            def turn(n, u):
                un = n * UNITS + u
                pe.wait_ge(s["norm_pool"], after(un + 1))
                pe.wait_ge(s["o1_out"], after(un))
                for j in range(4):
                    mm = pe.transpose(bank[6][:, 128 * j:128 * j + 128],
                                      probs[:, u % 2, 2 * j:2 * j + 2, :].rearrange("p w k -> p (w k)"), ident_s[:, :])
                mm.then_inc(s["t_mm"], 1)

            def attend(n, u):
                g, hf, un = u // 2, u % 2, n * UNITS + u
                pe.wait_ge(s["pt_out"], after(un + 1))
                pe.wait_ge(s["o0_out"], after(un))
                pe.wait_ge(s["v_out"], after((n * GROUPS + g) * 2 + 2))
                pe.wait_ge(v_shifted[g % 2], (n * (GROUPS // 2) + g // 2) * 32 + 32)
                for pair in range(2):
                    o = bank[7 - pair][:, :].rearrange("p (m k o c) -> p m k o c", m=2, k=2, o=2)
                    for j in range(4):
                        mm = pe.matmul(o[:, j // 2, :, j % 2, :],
                                       vb[:, g % 2, 1 - j % 2, 2 * hf + j // 2, 128 * pair:128 * pair + 128],
                                       pts[:, j, :, 64 * pair:64 * pair + 64], start=True, stop=True)
                    mm.then_inc(s["pv_mm"], 1)

            def project_out(n, ahead, ks):
                if ks[0] == 0:
                    if ahead:
                        pe.wait_ge(s["log_act"], after((n * GROUPS + GROUPS + 1) * 2 + 2))
                    else:
                        pe.wait_ge(s["v_out"], after((n * GROUPS + GROUPS) * 2))
                    pe.wait_ge(s["o0_out"], after(n * UNITS + UNITS - 2))
                    pe.wait_ge(s["o1_out"], after(n * UNITS + UNITS - 2))
                if ks[-1] == 7:
                    pe.wait_ge(s["o0_out"], after(n * UNITS + UNITS))
                    pe.wait_ge(s["o1_out"], after(n * UNITS + UNITS))
                for k in ks:
                    mm = pe.matmul(bank[4][:, :], wo_s[:, k, :], ot[:, k, :], start=(k == 0), stop=(k == 7))
                if ks[-1] == 7:
                    mm.then_inc(s["y_mm"], 1)

            def attention(layer, n, ahead):
                for u in range(UNITS):
                    g = u // 2
                    pi = n * GROUPS + g
                    v_too = g + 1 < GROUPS or ahead
                    qk_too = g + 2 < GROUPS or ahead
                    g1, g2 = (g + 1) % GROUPS, (g + 2) % GROUPS
                    if u % 2 == 0:
                        scores(n, u)
                        if u:
                            turn(n, u - 1)
                        if v_too:
                            if g == 0:
                                pe.wait_ge(s["resid_dve"], after(n))
                            if g1 == 0:
                                pe.wait_ge(s["xv_lo_dve"], after(n + 2))
                            pe.wait_ge(s["log_act"], after(pi * 2 + 4))
                            values(pi + 1, g1, 0)
                        if qk_too:
                            if g2 == 0:
                                pe.wait_ge(s["xs_lo_pool"], after(2 * n + 4))
                            project(pi + 2, g2, K)
                        if u:
                            attend(n, u - 1)
                        if v_too:
                            pe.wait_ge(s["v_out"], after(pi * 2 + 3))
                            values(pi + 1, g1, 1)
                    else:
                        scores(n, u)
                        if qk_too:
                            project(pi + 2, g2, Q)
                        turn(n, u - 1)
                        if qk_too:
                            pe.wait_ge(s["v_out"], after(pi * 2 + 4))
                            norms(pi + 2, K)
                        attend(n, u - 1)
                        if qk_too:
                            pe.wait_ge(s["log_act"], after(pi * 2 + 5))
                            norms(pi + 2, Q)
                turn(n, UNITS - 1)
                pe.wait_ge(wo_in, layer * 32 + 32)
                project_out(n, ahead, range(0, 2))
                attend(n, UNITS - 1)
                project_out(n, ahead, range(2, 6))
                project_out(n, ahead, range(6, 8))

            def feed_forward(n, b, bank_free=None):
                pe.wait_ge(s["ln_out"], after(PRE * B + n + 1))
                for j, (f0, fn) in enumerate(FT):
                    if j == 0 and bank_free is not None:
                        pe.wait_ge(s["log_act"], bank_free)
                    if b or j == 2:
                        pe.wait_ge(s["gelu_act"], after(n * 3 + j - 1))
                    pe.matmul(bank[4 + (b * 3 + j) % 2][0:fn, :], w1_s[:, FF + f0:FF + f0 + fn], xh[:, b, :],
                              start=True, stop=True).then_inc(s["fg_mm"], 1)
                    pe.wait_ge(s["hh_dve"], after(n * 3 + j))
                    pe.matmul(bank[6][0:fn, :], w1_s[:, f0:f0 + fn], xh[:, b, :],
                              start=True, stop=True).then_inc(s["fa_mm"], 1)

            def feed_forward_out(n, b):
                pe.wait_ge(s["fres_dve"], after(n))
                for j, (f0, fn) in enumerate(FT):
                    pe.wait_ge(s["hh_dve"], after(n * 3 + j + 1))
                    mm = pe.matmul(bank[7][:, :], w2_s[0:fn, j, :], hh[0:fn, b % 2, j, :],
                                   start=(j == 0), stop=(j == 2))
                mm.then_inc(s["fy_mm"], 1)

            def first_projections(layer):
                pe.wait_ge(s["split"], after(layer + 1))
                pe.wait_ge(s["xs_lo_pool"], after(2 * layer * B + 2))
                project(layer * B * GROUPS, 0, K)
                project(layer * B * GROUPS, 0, Q)

            def first_norms(layer):
                norms(layer * B * GROUPS, K)
                norms(layer * B * GROUPS, Q, 5)

            def first_values(layer):
                p0 = layer * B * GROUPS
                pe.wait_ge(s["xv_lo_dve"], after(layer * B + 1))
                pe.wait_ge(s["log_act"], after(p0 * 2 + 1))
                values(p0, 0, 0)
                project(p0 + 1, 1, K)
                pe.wait_ge(s["v_out"], after(p0 * 2 + 1))
                values(p0, 0, 1)
                project(p0 + 1, 1, Q)
                pe.wait_ge(s["v_out"], after(p0 * 2 + 2))
                norms(p0 + 1, K)
                pe.wait_ge(s["log_act"], after(p0 * 2 + 2))
                norms(p0 + 1, Q, 5)

            def whole_layer(layer, another):
                n0 = layer * B
                with pe.Fori(0, B - 1) as b:
                    attention(layer, layer * B + b, True)
                attention(layer, layer * B + (B - 1), False)
                pe.wait_ge(ff_in, layer * 64 + 64)
                pe.wait_ge(s["xf0_dve"], after(layer + 1))
                for c in range(B):
                    pe.wait_ge(s["xf_act"], after(layer * B + c + 1))
                    pe.wait_ge(s["ln_xc"], after((PRE + layer) * B + c))
                    if c == 0:
                        pe.wait_ge(s["o1_out"], after(layer * B * UNITS + B * UNITS))
                    pe.matmul(bank[6][:, :], mean_s[:, :], xf[:, c, :], start=True, stop=True).then_inc(s["mean_mm"], 1)
                    if c > 0:
                        variance(PRE + layer, c - 1)
                variance(PRE + layer, B - 1)
                pe.wait_ge(s["ln_xc"], after((PRE + layer) * B + B))
                feed_forward(n0, 0)
                feed_forward(n0 + 1, 1)
                pe.wait_ge(s["ln_log"], after((PRE + layer) * B + B))
                feed_forward_out(n0, 0)
                feed_forward(n0 + 2, 2)
                feed_forward_out(n0 + 1, 1)
                if another:
                    first_projections(layer + 1)
                feed_forward_out(n0 + 2, 2)
                if another:
                    pe.wait_ge(s["gelu_act"], after(layer * B * 3 + 9))
                    first_norms(layer + 1)
                feed_forward(n0 + 3, 3, after((layer + 1) * B * GROUPS * 2 + 2) if another else None)
                feed_forward_out(n0 + 3, 3)
                if another:
                    pe.wait_ge(s["gelu_act"], after(layer * B * 3 + 12))
                    first_values(layer + 1)

            first_projections(0)
            first_norms(0)
            first_values(0)
            with pe.Fori(0, DEPTH - 1) as layer:
                whole_layer(layer, True)
            whole_layer(DEPTH - 1, False)

            LAST = PRE + DEPTH
            pe.wait_ge(z["fin_sum"], B)
            layer_norm(LAST, lambda c: accv[:, c, :])
            pe.wait_ge(z["fin_in"], 16 * 13)
            for b in range(B):
                pe.wait_ge(s["ln_out"], after(LAST * B + b + 1))
                pe.matmul(bank[b][:, :], gwg_s, xn2[:, b, :], start=True, stop=True).then_inc(z["gg_mm"], 1)
            for b in range(B):
                if b:
                    pe.wait_ge(z["g1_copy"], b)
                pe.matmul(bank[6][0:LR, :], gwg1_s, xn2[:, b, :], start=True, stop=True).then_inc(z["g1_mm"], 1)
                if b:
                    pe.wait_ge(z["kp_lo"], b)
                pe.matmul(bank[4][:, :], gwk_s, xn2[:, b, :], start=True, stop=True).then_inc(z["kp_mm"], 1)
                pe.wait_ge(z["g1_copy"], b + 1)
                if b:
                    pe.wait_ge(z["z_copy"], b)
                pe.matmul(bank[7][:, :], gwg2_s[0:LR, :], g1s[0:LR, :], start=True, stop=True).then_inc(z["z_mm"], 1)
                if b:
                    pe.wait_ge(z["qp_lo"], b)
                pe.matmul(bank[5][:, :], gwq_s, xn2[:, b, :], start=True, stop=True).then_inc(z["qp_mm"], 1)
                pe.wait_ge(z["gg_dve"], b + 1)
                pe.matmul(bank[b][:, :], gwv_s, xn2[:, b, :], start=True, stop=True).then_inc(z["gv_mm"], 1)
            for m in range(TILES):
                mm = pe.matmul(bank[6][:, 8 * m:8 * m + 8], xn2[:, m // 4, 128 * (m % 4):128 * (m % 4) + 128], rt_s,
                               start=True, stop=True)
            mm.then_inc(z["lg_mm"], 1)
            pe.wait_ge(z["z_copy"], B)
            for t in range(8):
                if t == 1:
                    pe.wait_ge(z["lg_copy"], 1)
                if t >= 2:
                    pe.wait_ge(z["ew_copied"], t - 1)
                for j in range(4):
                    e, h = (4 * (t % 4) + j) // 2, (4 * (t % 4) + j) % 2
                    src = ew1_s[:, e, h, :] if t < 4 else ew2_s[:, e, 128 * h:128 * h + 128]
                    mm = pe.transpose(bank[7 - t % 2][:, 128 * j:128 * j + 128], src, ident_s[:, :])
                mm.then_inc(z["ew_turned"], 1)

            def repeat_k(t):
                b, i = t // DK, t % DK
                pe.wait_ge(z["kp_lo"], b + 1)
                if t:
                    pe.wait_ge(z["kv_dve"], t)
                pe.matmul(bank[0][:, :], sel[:, i], k_parts[b], start=True, stop=True).then_inc(z["rk_mm"], 1)

            def repeat_decay(t):
                b, i = t // DK, t % DK
                pe.wait_ge(z["eg_lo"], b + 1)
                if t:
                    pe.wait_ge(z["scan_dve"], t)
                pe.matmul(bank[1][:, :], sel[:, i], g_parts[b], start=True, stop=True).then_inc(z["rg_mm"], 1)

            def repeat_q(t):
                b, i = t // DK, t % DK
                pe.wait_ge(z["qp_lo"], b + 1)
                if t:
                    pe.wait_ge(z["qs_dve"], t)
                pe.matmul(bank[2][:, :], sel[:, i], q_parts[b], start=True, stop=True).then_inc(z["rq_mm"], 1)

            def expert_in(m):
                q, e = m // E, m % E
                for h in range(2):
                    if m >= 2:
                        pe.wait_ge(z["eh_act"], 2 * (m - 2) + h + 1)
                    pe.matmul(bank[3 + 2 * (m % 2) + h][:, :], w1t[:, e, 128 * h:128 * h + 128], xn2[:, q, :],
                              start=True, stop=True).then_inc(z["eh_mm"], 1)

            def expert_out(m):
                q, e = m // E, m % E
                pe.wait_ge(z["eh_act"], 2 * m + 2)
                if m:
                    pe.wait_ge(z["ey_dve"], m)
                for j in range(4):
                    for h in range(2):
                        mm = pe.matmul(bank[7][:, 128 * j:128 * j + 128], ht[:, m % 2, h, 128 * j:128 * j + 128],
                                       w2t[:, e, h, :], start=(h == 0), stop=(h == 1))
                mm.then_inc(z["ey_mm"], 1)

            pe.wait_ge(z["sel_made"], 1)
            pe.wait_ge(z["gv_copy"], B)
            pe.wait_ge(z["gg_dve"], B)
            pe.wait_ge(z["ew_copied"], 8)
            for t in range(B * DK + 2):
                if t < B * DK:
                    repeat_k(t)
                if 1 <= t <= B * DK:
                    repeat_decay(t - 1)
                if t >= 2:
                    repeat_q(t - 2)
                if t % 2 == 0 and t < 2 * B * E:
                    expert_in(t // 2)
                elif t >= 3 and t % 2:
                    expert_out(t // 2 - 1)
            def mean_square(b):
                pe.wait_ge(z["gsq_act"], b + 1)
                if b == 1:
                    pe.wait_ge(z["ey_dve"], B * E)
                if b >= 2:
                    pe.wait_ge(z["gl_act"], b - 1)
                pe.matmul(bank[6 + b % 2][:, :], blocks_s[:, :], xc[:, b, :], start=True, stop=True).then_inc(z["gms_mm"], 1)

            def gla_out(b):
                pe.wait_ge(z["gn_dve"], b + 1)
                if b >= 2:
                    pe.wait_ge(z["x1_dve"], b - 1)
                pe.matmul(bank[4 + b % 2][:, :], gwo_s, go[:, b, :], start=True, stop=True).then_inc(z["go_mm"], 1)

            pe.wait_ge(z["eh_act"], 2 * B * E)
            mean_square(0)
            mean_square(1)
            gla_out(0)
            mean_square(2)
            gla_out(1)
            mean_square(3)
            gla_out(2)
            gla_out(3)
            for b in range(B):
                pe.wait_ge(z["x1_dve"], b + 1)
                for m in range(4):
                    mm = pe.transpose(bank[b][:, 128 * m:128 * m + 128], accv[:, b, 128 * m:128 * m + 128], ident_s[:, :])
                mm.then_inc(z["tok_mm"], 1)

        @block.scalar
        def _(act):
            for n in act_s.values():
                act.sem_inc(n, 1)
            eps, one, floor = consts[:, 0:1], consts[:, 1:2], consts[:, 2:3]

            def layer_norm(i):
                for c in range(B):
                    act.wait_ge(s["ln_xc"], after(i * B + c + 1))
                    if c >= 2:
                        act.wait_ge(s["var_mm"], after(i * B + c - 1))
                    act.activation(lsq[:, c % 2, :], xc[:, c, :], ACT.Square).then_inc(s["ln_sq"], 1)
                    if c > 0:
                        rstd(i, c - 1)
                rstd(i, B - 1)

            def rstd(i, c):
                act.wait_ge(s["var_mm"], after(i * B + c + 1))
                act.activation(lln[:, c % 2, :], bank[7][:, :], ACT.Ln, bias=eps).then_inc(s["ln_log"], 1)
                act.wait_ge(s["ln_log"], after(i * B + c + 1))
                if c >= 2:
                    act.wait_ge(s["ln_n"], after(i * B + c - 1))
                act.activation(lrs[:, c % 2, :], lln[:, c % 2, :], ACT.Exp, scale=-0.5).then_inc(s["ln_rstd"], 1)

            act.preload_act_table_set("natural_log_exp_and_others")
            for b in range(B):
                act.wait_ge(z["x_turned"], 1)
                act.activation(accv[:, b, :], bank[b][:, :], ACT.Copy).then_inc(z["x_copied"], 1)
            def tokens_for_qk(n, b):
                act.wait_ge(s["q_mm"], after(n * GROUPS))
                act.activation(xs_hi[0:64, WIN:], xv[0:64, b, :], ACT.Copy)
                act.activation(xs_hi[64:128, WIN + 1:], xv[64:128, b, 0:T - 1], ACT.Copy).then_inc(s["xs_hi_act"], 1)

            def tokens_for_v(n):
                act.wait_ge(s["xs_hi_act"], after(n + 1))
                act.wait_ge(s["v_mm"], after(n * GROUPS * 2))
                act.activation(xv_hi[:, WIN:], xs_hi[:, WIN:].bitcast(F32), ACT.Copy).then_inc(s["xv_hi_act"], 1)

            def first_tokens(layer):
                tokens_for_qk(layer * B, 0)
                tokens_for_v(layer * B)

            act.wait_ge(z["zeroed"], 1)
            layer_norm(0)
            act.wait_ge(s["ln_out"], after(1))
            act.wait_ge(z["padded"], 1)
            first_tokens(0)
            layer_norm(1)
            for b0 in range(0, B, 2):
                pair = (b0, b0 + 1)
                for b in pair:
                    act.wait_ge(z["decay_arg"], b + 1)
                    act.activation(argss[b % 2], argss[b % 2], ACT.Exp).then_inc(z["decay_exp"], 1)
                for b in pair:
                    act.wait_ge(z["sum_scan"], b + 1)
                    act.activation(pps[b % 2], s_runs[b % 2], ACT.Ln).then_inc(z["log_sum"], 1)
                for b in pair:
                    act.wait_ge(z["carry_arg"], b + 1)
                    act.activation(argss[b % 2], argss[b % 2], ACT.Exp).then_inc(z["carry_exp"], 1)
                for b in pair:
                    act.wait_ge(z["out_arg"], b + 1)
                    act.activation(argss[b % 2], argss[b % 2], ACT.Exp).then_inc(z["out_exp"], 1)
                    act.activation(rrs[b % 2], bank[2 + 3 * (b % 2)][:, :], ACT.Exp, scale=-1.0).then_inc(z["gate_exp"], 1)
            layer_norm(2)
            act.preload_act_table_set("sigmoid_and_others")
            for b in range(B):
                for j in range(4):
                    act.wait_ge(z["relu_dve"], 4 * b + j + 1)
                    if b:
                        act.wait_ge(z["cv_mm"], b)
                    act.activation(kkb[:, j, :], argss[0][:, j % 2, :], ACT.Square).then_inc(z["kk_act"], 1)
                act.wait_ge(z["cr_mm"], b + 1)
                if b >= 2:
                    act.wait_ge(z["cm_done"], b - 1)
                act.activation(rrs[b % 2], bank[4][:, :], ACT.Sigmoid).then_inc(z["cm_gate"], 1)
            act.preload_act_table_set("natural_log_exp_and_others")

            def squares(pi, kind):
                act.wait_ge(s["k_mm" if kind == K else "q_mm"], after(pi + 1))
                act.wait_ge(s["sqadd"], after(pi * 2))
                act.activation(sqb[:, kind, 0, :], bank[2 * kind][:, :], ACT.Square)
                act.activation(sqb[:, kind, 1, :], bank[2 * kind + 1][:, :], ACT.Square).then_inc(s["sq_act"], 1)

            def rnorm(pi, kind, n_bank=4):
                act.wait_ge(s["n2_mm"], after(pi * 2 + kind + 1))
                act.activation(lnb[:, kind, :], bank[n_bank][:, :], ACT.Ln, bias=floor, scale=LN_SCALE).then_inc(s["log_act"], 1)
                act.wait_ge(s["log_act"], after(pi * 2 + kind + 1))
                act.wait_ge(s["tab_dve"], after(pi * 2 + kind))
                act.activation(rnb[:, kind, :], lnb[:, kind, :], ACT.Exp, bias=consts[:, 3:4], scale=-0.5).then_inc(s["rn_act"], 1)

            def place(pi, g):
                act.wait_ge(s["rotadd"], after(pi * 2 + 2))
                for h in range(2):
                    rows = slice(HALF * h, HALF * h + HALF)
                    ins = act.activation(qbd[rows, g % 2, :, :, h, :],
                                         qst[rows].rearrange("p a (w t) -> p a w t", w=NW), ACT.Copy)
                ins.then_inc(s["placed_act"], 1)

            def values_out(pi, g, c):
                act.wait_ge(s["v_mm"], after(pi * 2 + c + 1))
                act.activation(vb[:, g % 2, 0, 2 * c:2 * c + 2, :],
                               bank[4][:, :].rearrange("p (m d) -> p m d", m=2), ACT.Copy).then_inc(s["v_out"], 1)
                if c == 1:
                    act.wait_ge(s["v_out"], after(pi * 2 + 2))
                    act.dma_start(vb[WIN:128, g % 2, 1], vb[0:128 - WIN, g % 2, 0]).then_inc(v_shifted[g % 2], 16)
                    act.dma_start(vb[0:WIN, g % 2, 1, 1:4, :], vb[128 - WIN:128, g % 2, 0, 0:3, :]).then_inc(v_shifted[g % 2], 16)

            def exponent(n, u):
                un = n * UNITS + u
                act.wait_ge(s["sub_dve"], after(un + 1))
                act.activation(probs[:, u % 2], probs[:, u % 2], ACT.Exp, scale=QK_SCALE).then_inc(s["exp_act"], 1)

            def turned_out(n, u):
                act.wait_ge(s["t_mm"], after(n * UNITS + u + 1))
                for k in range(2):
                    rows = slice(64 * k, 64 * k + 64)
                    ins = act.activation(pts[rows, :, k, :], bank[6][rows, :].rearrange("p (j c) -> p j c", j=4), ACT.Copy)
                ins.then_inc(s["pt_out"], 1)

            def heads_out(n, u):
                act.wait_ge(s["pv_mm"], after((n * UNITS + u) * 2 + 2))
                for h in range(2):
                    mm = act.activation(head_windows(u, h, 1), own_part(6, h), ACT.Copy)
                mm.then_inc(s["o1_out"], 1)

            def attention(n, b, ahead):
                for u in range(UNITS):
                    g = u // 2
                    pi = n * GROUPS + g
                    v_too = g + 1 < GROUPS or ahead
                    qk_too = g + 2 < GROUPS or ahead
                    g1 = (g + 1) % GROUPS
                    if u % 2 == 0:
                        if u:
                            turned_out(n, u - 1)
                        if v_too:
                            values_out(pi + 1, g1, 0)
                        exponent(n, u)
                        if qk_too:
                            squares(pi + 2, K)
                        if u:
                            heads_out(n, u - 1)
                        if v_too:
                            values_out(pi + 1, g1, 1)
                    else:
                        if v_too:
                            place(pi + 1, g1)
                        if qk_too:
                            squares(pi + 2, Q)
                        turned_out(n, u - 1)
                        exponent(n, u)
                        if qk_too:
                            rnorm(pi + 2, K)
                        if ahead and g + 3 == GROUPS:
                            tokens_for_qk(n + 1, b + 1)
                        heads_out(n, u - 1)
                        if qk_too:
                            rnorm(pi + 2, Q)
                        if ahead and g + 2 == GROUPS:
                            tokens_for_v(n + 1)
                turned_out(n, UNITS - 1)
                heads_out(n, UNITS - 1)

            def first_squares(layer):
                squares(layer * B * GROUPS, K)
                squares(layer * B * GROUPS, Q)

            def first_rnorms(layer):
                rnorm(layer * B * GROUPS, K)
                rnorm(layer * B * GROUPS, Q, 5)

            def first_values(layer):
                p0 = layer * B * GROUPS
                values_out(p0, 0, 0)
                values_out(p0, 0, 1)
                place(p0, 0)
                squares(p0 + 1, K)
                squares(p0 + 1, Q)
                rnorm(p0 + 1, K)
                rnorm(p0 + 1, Q, 5)

            def gelu(layer, b):
                for j, (f0, fn) in enumerate(FT):
                    act.wait_ge(s["fg_mm"], after((layer * B + b) * 3 + j + 1))
                    if b >= 2:
                        act.wait_ge(s["hh_dve"], after((layer * B + b - 2) * 3 + j + 1))
                    act.activation(gg[0:fn, b % 2, j, :], bank[4 + (b * 3 + j) % 2][0:fn, :], ACT.Gelu,
                                   bias=lp[0:fn, L_B1G + j:L_B1G + j + 1]).then_inc(s["gelu_act"], 1)

            def whole_layer(layer, another):
                n0 = layer * B
                with act.Fori(0, B - 1) as b:
                    attention(layer * B + b, b, True)
                attention(layer * B + (B - 1), B - 1, False)
                act.wait_ge(s["y_mm"], after(n0 + B))
                for c in range(B):
                    act.wait_ge(s["resid_dve"], after(layer * B + c + 1))
                    act.activation(xf[0:64, c, :], xv[0:64, c, :], ACT.Copy)
                    act.activation(xf[64:128, c, 1:T], xv[64:128, c, 0:T - 1], ACT.Copy).then_inc(s["xf_act"], 1)
                layer_norm(PRE + layer)
                act.preload_act_table_set("gelu_and_others")
                gelu(layer, 0)
                gelu(layer, 1)
                if another:
                    act.wait_ge(s["fres_dve"], after(n0 + 1))
                    first_tokens(layer + 1)
                gelu(layer, 2)
                if another:
                    first_squares(layer + 1)
                    act.preload_act_table_set("natural_log_exp_and_others")
                    first_rnorms(layer + 1)
                    act.preload_act_table_set("gelu_and_others")
                gelu(layer, 3)
                if another:
                    act.preload_act_table_set("natural_log_exp_and_others")
                    act.wait_ge(s["hh_dve"], after(layer * B * 3 + 12))
                    first_values(layer + 1)

            first_squares(0)
            first_rnorms(0)
            first_values(0)
            with act.Fori(0, DEPTH - 1) as layer:
                whole_layer(layer, True)
            whole_layer(DEPTH - 1, False)

            act.preload_act_table_set("natural_log_exp_and_others")
            for r in (0, 64):
                rows = ident_s[r:r + 64, r:r + 64].rearrange("p (h i) -> p i h", h=NH)[:, :, :, None]
                ins = act.activation(sel[r:r + 64], rows.to_broadcast([64, DK, NH, DV]), ACT.Copy)
            ins.then_inc(z["sel_made"], 1)
            layer_norm(PRE + DEPTH)
            act.preload_act_table_set("sigmoid_and_others")
            for b in range(B):
                act.wait_ge(z["gg_mm"], b + 1)
                act.activation(gs[:, b, :], bank[b][:, :], ACT.Sigmoid).then_inc(z["gg_act"], 1)
            act.preload_act_table_set("natural_log_exp_and_others")
            for b in range(B):
                act.wait_ge(z["kp_mm"], b + 1)
                act.activation(k_parts[b], bank[4][:, :], ACT.Copy).then_inc(z["kp_hi"], 1)
                act.wait_ge(z["z_copy"], b + 1)
                if b:
                    act.wait_ge(z["gk_dve"], b)
                act.activation(az[:, 0, :], zb, ACT.Abs).then_inc(z["abs_act"], 1)
                act.wait_ge(z["abs_act"], b + 1)
                act.activation(az[:, 1, :], az[:, 0, :], ACT.Exp, scale=-1.0).then_inc(z["gexp_act"], 1)
                act.wait_ge(z["gexp_act"], b + 1)
                act.activation(az[:, 0, :], az[:, 1, :], ACT.Ln, bias=one).then_inc(z["gln_act"], 1)
                act.wait_ge(z["qp_mm"], b + 1)
                act.activation(q_parts[b], bank[5][:, :], ACT.Copy, scale=Q_SCALE).then_inc(z["qp_hi"], 1)
                act.wait_ge(z["gv_mm"], b + 1)
                act.activation(vt[:, b, :], bank[b][:, :], ACT.Copy).then_inc(z["gv_copy"], 1)
                act.wait_ge(z["gk_dve"], b + 1)
                act.activation(egk[:, b, :], egk[:, b, :], ACT.Exp, scale=1.0 / GATE_NORM).then_inc(z["egk_act"], 1)
                act.wait_ge(z["egk_act"], b + 1)
                act.activation(g_parts[b], egk[:, b, :], ACT.Copy).then_inc(z["eg_hi"], 1)
            act.wait_ge(z["lg_mm"], 1)
            act.activation(lg, bank[6][:, 0:128].rearrange("p (m e) -> p m e", e=8), ACT.Copy).then_inc(z["lg_copy"], 1)
            for t in range(8):
                act.wait_ge(z["ew_turned"], t + 1)
                dst = w1t[:, 2 * t:2 * t + 2, :] if t < 4 else w2t[:, 2 * (t - 4):2 * (t - 4) + 2, :, :]
                src = bank[7 - t % 2][:, :]
                src = src.rearrange("p (e f) -> p e f", e=2) if t < 4 else src.rearrange("p (e h c) -> p e h c", e=2, h=2)
                act.activation(dst, src, ACT.Copy).then_inc(z["ew_copied"], 1)
            act.wait_ge(z["route"], 1)
            act.activation(gw12[:, 0, :], gw12[:, 0, :], ACT.Exp).then_inc(z["route"], 1)
            def squared(b):
                act.wait_ge(z["oadd"], DK * (b + 1))
                act.activation(xc[:, b, :], go[:, b, :], ACT.Square).then_inc(z["gsq_act"], 1)

            act.preload_act_table_set("gelu_and_others")
            for m in range(B * E):
                for h in range(2):
                    act.wait_ge(z["eh_mm"], 2 * m + h + 1)
                    if m >= 2:
                        act.wait_ge(z["ey_mm"], m - 1)
                    act.activation(ht[:, m % 2, h, :], bank[3 + 2 * (m % 2) + h][:, :], ACT.Gelu).then_inc(z["eh_act"], 1)
                if m >= E + 2 and (m - 2) % E == 0:
                    squared(m // E - 1)
            act.preload_act_table_set("natural_log_exp_and_others")
            squared(B - 1)
            for b in range(B):
                act.wait_ge(z["gms_mm"], b + 1)
                act.activation(lln[:, b % 2, :], bank[6 + b % 2][:, :], ACT.Ln, bias=eps, scale=1.0 / DV).then_inc(z["gl_act"], 1)
                act.wait_ge(z["gl_act"], b + 1)
                if b >= 2:
                    act.wait_ge(z["gn_dve"], b - 1)
                act.activation(lrs[:, b % 2, :], lln[:, b % 2, :], ACT.Exp, scale=-0.5).then_inc(z["gr_act"], 1)

        @block.vector
        def _(dve):
            for n in dve_s.values():
                dve.sem_inc(n, 1)
            dve.sem_inc(s["tab_dve"], 1)
            dve.sem_inc(s["mul_dve"], 1)
            count = [0]

            def link(ins):
                count[0] += 1
                ins.then_inc(z["dve_link"], 1)
                dve.wait_ge(z["dve_link"], count[0])

            def layer_norm(i, src, dst, gain=None, bias=None):
                for c in range(B):
                    dve.wait_ge(s["mean_mm"], after(i * B + c + 1))
                    dve.tensor_tensor(xc[:, c, :], src(c), bank[6][:, :], ALU.subtract).then_inc(s["ln_xc"], 1)
                    if c > 1:
                        normed(i, c - 2, dst, gain, bias)
                normed(i, B - 2, dst, gain, bias)
                normed(i, B - 1, dst, gain, bias)

            def normed(i, c, dst, gain, bias):
                dve.wait_ge(s["ln_rstd"], after(i * B + c + 1))
                if gain is None:
                    dve.tensor_tensor(dst(c), xc[:, c, :], lrs[:, c % 2, :], ALU.mult).then_inc(s["ln_out"], 1)

                    return
                dve.tensor_tensor(xc[:, c, :], xc[:, c, :], lrs[:, c % 2, :], ALU.mult).then_inc(s["ln_n"], 1)
                dve.wait_ge(s["ln_n"], after(i * B + c + 1))
                dve.tensor_scalar(dst(c), xc[:, c, :], gain, bias, ALU.mult, ALU.add).then_inc(s["ln_out"], 1)

            def col(k, rows=128):
                return par[0:rows, k:k + 1]

            dve.memset(mean_s[:, :], 1.0 / C)
            dve.memset(consts[:, 0:1], EPS)
            dve.memset(consts[:, 1:2], 1.0)
            dve.memset(consts[:, 2:3], 6e-20)
            dve.memset(consts[:, 3:4], 6.931471805599453)
            dve.memset(hb[:, :, 0:1], 0.0)
            dve.memset(h2b[:, :, 0:1], 0.0)
            for x in range(2):
                dve.memset(m_runs[x][:, 0:1], NEG_INF)
                dve.memset(s_runs[x][:, 0:1], 1.0)
                dve.memset(a_runs[x][:, 0:1], 0.0)
            dve.memset(wfull, 0.0).then_inc(z["zeroed"], 1)
            for w in (xs_hi, xs_lo, xv_hi, xv_lo):
                dve.memset(w[:, 0:WIN].bitcast(F32), 0.0)
                ins = dve.memset(w[64:128, WIN:WIN + 1].bitcast(F32), 0.0)
            ins.then_inc(z["padded"], 1)
            dve.wait_ge(z["padded"], 1)
            dve.wait_ge(z["zeroed"], 1)
            dve.wait_ge(z["x_copied"], B)
            dve.wait_ge(z["const_in"], 64)
            dve.tensor_copy(identb[:, :], ident_s[:, :])
            dve.tensor_copy(maskb[:, :], maskf)
            layer_norm(0, lambda c: accv[:, c, :], lambda c: xv[:, c, :], 1.0, 0.0)
            link(dve.tensor_scalar(wfull, wfull, col(P_W), None, ALU.add))
            dve.wait_ge(z["tm_in"], 96)
            link(dve.tensor_scalar(om[:, 0:5], par[:, P_MK:P_CR + 1], -1.0, 1.0, ALU.mult, ALU.add))
            for j, k in ((0, 0), (1, 1), (2, 2), (3, 4)):
                src = traw[:, j * C:(j + 1) * C]
                dve.tensor_scalar(tmix[:, 0, j * C:(j + 1) * C], src, col(P_MK + k), None, ALU.mult)
                ins = dve.tensor_scalar(tmix[:, 1, j * C:(j + 1) * C], src, om[:, k:k + 1], None, ALU.mult)
            ins.then_inc(z["mixed"], 1)
            dve.wait_ge(s["ln_out"], after(B))
            layer_norm(1, lambda c: xv[:, c, :], lambda c: hb[:, c, 1:T + 1], col(P_G1), col(P_B1))

            now, old = slice(1, T + 1), slice(0, T)

            def k_of(b):
                return bank[3 * (b % 2)][:, :]

            def v_of(b):
                return bank[3 * (b % 2) + 1][:, :]

            def done(b, ins):
                ins.then_inc(rwkv[b % 2], 1)

            def wait_step(b, k):
                dve.wait_ge(rwkv[b % 2], RW_STEPS * (b // 2) + k)

            def k_decayed(b):
                dve.wait_ge(z["kvr_mm"], b + 1)
                done(b, dve.tensor_scalar(kws[b % 2], k_of(b), col(P_W), None, ALU.add))

            def running_max(b):
                m = m_runs[b % 2]
                wait_step(b, 1)
                done(b, dve.tensor_tensor_scan(m[:, now], wfull, kws[b % 2], m[:, 0:1], ALU.add, ALU.max))

            def decay_args(b):
                m, args = m_runs[b % 2], argss[b % 2]
                wait_step(b, 2)
                dve.scalar_tensor_tensor(args[:, 0, :], m[:, old], col(P_W), m[:, now], ALU.add, ALU.subtract)
                dve.tensor_tensor(args[:, 1, :], kws[b % 2], m[:, now], ALU.subtract).then_inc(z["decay_arg"], 1)

            def running_sum(b):
                args = argss[b % 2]
                dve.wait_ge(z["decay_exp"], b + 1)
                dve.tensor_tensor_scan(s_runs[b % 2][:, now], args[:, 0, :], args[:, 1, :], 0.0, ALU.mult, ALU.add) \
                   .then_inc(z["sum_scan"], 1)

            def log_of_sum(b):
                dve.wait_ge(z["log_sum"], b + 1)
                done(b, dve.tensor_tensor(pps[b % 2], pps[b % 2], m_runs[b % 2], ALU.add))

            def carry_max(b):
                wait_step(b, 3)
                done(b, dve.tensor_tensor(kmxs[b % 2], k_of(b), pps[b % 2][:, old], ALU.max))

            def carry_args(b):
                args = argss[b % 2]
                wait_step(b, 4)
                dve.tensor_tensor(args[:, 0, :], pps[b % 2][:, old], kmxs[b % 2], ALU.subtract)
                dve.tensor_tensor(args[:, 1, :], k_of(b), kmxs[b % 2], ALU.subtract).then_inc(z["carry_arg"], 1)

            def carry_values(b):
                dve.wait_ge(z["carry_exp"], b + 1)
                done(b, dve.tensor_tensor(bvs[b % 2], v_of(b), argss[b % 2][:, 1, :], ALU.mult))

            def carry(b):
                wait_step(b, 5)
                done(b, dve.tensor_tensor_scan(a_runs[b % 2][:, now], argss[b % 2][:, 0, :], bvs[b % 2], 0.0,
                                               ALU.mult, ALU.add))

            def out_max(b):
                wait_step(b, 6)
                done(b, dve.scalar_tensor_tensor(kmxs[b % 2], k_of(b), col(P_U), pps[b % 2][:, old], ALU.add, ALU.max))

            def out_args(b):
                args = argss[b % 2]
                wait_step(b, 7)
                dve.tensor_tensor(args[:, 0, :], pps[b % 2][:, old], kmxs[b % 2], ALU.subtract)
                dve.scalar_tensor_tensor(args[:, 1, :], k_of(b), col(P_U), kmxs[b % 2], ALU.add, ALU.subtract) \
                   .then_inc(z["out_arg"], 1)

            def out_parts(b):
                args = argss[b % 2]
                dve.wait_ge(z["out_exp"], b + 1)
                dve.tensor_tensor(kws[b % 2], args[:, 0, :], a_runs[b % 2][:, old], ALU.mult)
                dve.tensor_tensor(bvs[b % 2], v_of(b), args[:, 1, :], ALU.mult)
                done(b, dve.tensor_tensor(kmxs[b % 2], args[:, 0, :], args[:, 1, :], ALU.add))

            def out_sum(b):
                wait_step(b, 8)
                done(b, dve.tensor_tensor(kws[b % 2], kws[b % 2], bvs[b % 2], ALU.add))

            def out_divisor(b):
                dve.wait_ge(z["gate_exp"], b + 1)
                wait_step(b, 9)
                done(b, dve.scalar_tensor_tensor(bvs[b % 2], rrs[b % 2], 1.0, kmxs[b % 2], ALU.add, ALU.mult))

            def out_reciprocal(b):
                wait_step(b, 10)
                done(b, dve.reciprocal(bvs[b % 2], bvs[b % 2]))

            def out_product(b):
                wait_step(b, 11)
                done(b, dve.tensor_tensor(kws[b % 2], kws[b % 2], bvs[b % 2], ALU.mult))

            def mixed_tokens(b):
                wait_step(b, 12)
                done(b, dve.tensor_tensor(rwx[:, b, :], kws[b % 2], xv[:, b, :], ALU.add))

            for b0 in range(0, B, 2):
                for stage in (k_decayed, running_max, decay_args, running_sum, log_of_sum, carry_max, carry_args,
                              carry_values, carry, out_max, out_args, out_parts, out_sum, out_divisor,
                              out_reciprocal, out_product, mixed_tokens):
                    for b in (b0, b0 + 1):
                        stage(b)
            layer_norm(2, lambda c: rwx[:, c, :], lambda c: h2b[:, c, 1:T + 1], col(P_G2), col(P_B2))

            def channel_input(b):
                dve.wait_ge(s["ln_out"], after(2 * B + b + 1))
                link(dve.tensor_scalar(ckx[:, b, :], h2b[:, b, 0:T], om[:, 3:4], None, ALU.mult))
                dve.scalar_tensor_tensor(ckx[:, b, :], h2b[:, b, 1:T + 1], col(P_CK), ckx[:, b, :], ALU.mult, ALU.add) \
                   .then_inc(z["ck_in"], 1)

            channel_input(0)
            channel_input(1)
            for b in range(B):
                bv = bvs[b % 2]
                for j in range(4):
                    dve.wait_ge(z["ck_mm"], 4 * b + j + 1)
                    if 4 * b + j >= 2:
                        dve.wait_ge(z["kk_act"], 4 * b + j - 1)
                    dve.tensor_scalar(argss[0][:, j % 2, :], bank[j][:, :], 0.0, None, ALU.max).then_inc(z["relu_dve"], 1)
                if b + 2 < B:
                    channel_input(b + 2)
                dve.wait_ge(z["cm_gate"], b + 1)
                dve.wait_ge(z["cv_mm"], b + 1)
                link(dve.tensor_tensor(bv, bank[5][:, :], rrs[b % 2], ALU.mult))
                link(dve.tensor_tensor(bv, bv, rwx[:, b, :], ALU.add))
                dve.tensor_tensor(accv[:, b, :], accv[:, b, :], bv, ALU.add).then_inc(z["cm_done"], 1)
            dve.wait_ge(z["cm_done"], B)

            dve.memset(qbd[:, 0], 0.0)
            dve.memset(kb[:, :, :, 0:WIN], 0.0)
            dve.wait_ge(z["rot_in"], 16)

            def shifted_lo_v(n):
                dve.wait_ge(s["xs_lo_pool"], after(2 * n + 2))
                dve.wait_ge(s["xv_hi_act"], after(n + 1))
                dve.tensor_copy(xv_lo[:, WIN:], xs_lo[:, WIN:].bitcast(F32)).then_inc(s["xv_lo_dve"], 1)

            def tables(pi, kind):
                at_ = 2 if kind == K else 0
                dve.wait_ge(s["rn_act"], after(pi * 2 + kind + 1))
                dve.wait_ge(s["mul_dve"], after(pi * 2 + kind + 1))
                dve.scalar_tensor_tensor(tab[:, 0, :], rnb[:, kind, :], RN_MAX, rot_s[:, at_, :], ALU.min, ALU.mult)
                dve.scalar_tensor_tensor(tab[:, 1, :], rnb[:, kind, :], RN_MAX, rot_s[:, at_ + 1, :], ALU.min, ALU.mult) \
                   .then_inc(s["tab_dve"], 1)

            def rotation(pi, kind):
                dve.wait_ge(s["tab_dve"], after(pi * 2 + kind + 2))
                dve.wait_ge(s["rotadd"], after(pi * 2 + kind))
                for o, a, t in ((0, 0, 0), (1, 1, 1), (2, 1, 0), (3, 0, 1)):
                    gain = (L_KA if kind == K else L_QA) + a
                    ins = dve.scalar_tensor_tensor(t4[:, o, :], bank[2 * kind + a][:, :], lp[:, gain:gain + 1],
                                                   tab[:, t, :], ALU.mult, ALU.mult)
                ins.then_inc(s["mul_dve"], 1)

            def place(pi, g):
                dve.wait_ge(s["rotadd"], after(pi * 2 + 2))
                for h in range(2, GH):
                    rows = slice(HALF * h, HALF * h + HALF)
                    ins = dve.tensor_copy(qbd[rows, g % 2, :, :, h, :], qst[rows].rearrange("p a (w t) -> p a w t", w=NW))
                ins.then_inc(s["placed_dve"], 1)

            def maximum(n, u):
                un = n * UNITS + u
                sc = bank[5][:, :].rearrange("p (w k) -> p w k", w=UW)
                dve.wait_ge(s["s_mm"], after(un + 1))
                dve.tensor_reduce(mx[:, u % 2, :], sc, AX, ALU.max).then_inc(s["max_dve"], 1)
                dve.wait_ge(s["max_dve"], after(un + 1))
                dve.tensor_tensor(probs[:, u % 2], sc, mx[:, u % 2, :, None].to_broadcast([128, UW, 2 * WIN]),
                                  ALU.subtract).then_inc(s["sub_dve"], 1)

            def sums(n, u):
                un = n * UNITS + u
                dve.wait_ge(s["exp_act"], after(un + 1))
                dve.tensor_reduce(sm[:, u % 2, :], probs[:, u % 2], AX, ALU.add).then_inc(s["sum_dve"], 1)
                dve.wait_ge(s["sum_dve"], after(un + 1))
                dve.reciprocal(rc[:, u % 2, :], sm[:, u % 2, :]).then_inc(s["rec_dve"], 1)

            def heads_out(n, u):
                dve.wait_ge(s["pv_mm"], after((n * UNITS + u) * 2 + 1))
                for h in range(2):
                    ins = dve.tensor_copy(head_windows(u, h, 0), own_part(7, h))
                ins.then_inc(s["o0_out"], 1)

            def attention(n, b, first, ahead):
                for u in range(UNITS):
                    g = u // 2
                    pi = n * GROUPS + g
                    v_too = g + 1 < GROUPS or ahead
                    qk_too = g + 2 < GROUPS or ahead
                    if u % 2 == 0:
                        if v_too and (u or first):
                            tables(pi + 1, Q)
                        maximum(n, u)
                        if v_too and (u or first):
                            rotation(pi + 1, Q)
                        sums(n, u)
                    else:
                        if v_too:
                            place(pi + 1, (g + 1) % GROUPS)
                        maximum(n, u)
                        sums(n, u)
                        if qk_too:
                            tables(pi + 2, K)
                            rotation(pi + 2, K)
                    if u:
                        heads_out(n, u - 1)
                    if ahead and u == 5:
                        shifted_lo_v(n + 1)
                if ahead:
                    tables(pi + 2, Q)
                    rotation(pi + 2, Q)
                heads_out(n, UNITS - 1)
                dve.wait_ge(s["y_mm"], after(n + 1))
                dve.tensor_tensor(xv[:, b, :], xv[:, b, :], bank[4][:, :], ALU.add).then_inc(s["resid_dve"], 1)

            def result(layer, b):
                n = layer * B + b
                dve.wait_ge(s["fy_mm"], after(n + 1))
                dve.scalar_tensor_tensor(xv[:, b, :], bank[7][:, :], lp[:, L_B2:L_B2 + 1], xv[:, b, :],
                                         ALU.add, ALU.add).then_inc(s["fres_dve"], 1)

            def gated(layer, b, j):
                f0, fn = FT[j]
                f = (layer * B + b) * 3 + j
                dve.wait_ge(s["gelu_act"], after(f + 1))
                dve.wait_ge(s["fa_mm"], after(f + 1))
                if b >= 2:
                    dve.wait_ge(s["fy_mm"], after(layer * B + b - 1))
                dve.scalar_tensor_tensor(hh[0:fn, b % 2, j, :], bank[6][0:fn, :],
                                         lp[0:fn, L_B1A + j:L_B1A + j + 1], gg[0:fn, b % 2, j, :],
                                         ALU.add, ALU.mult).then_inc(s["hh_dve"], 1)

            def whole_layer(layer, another):
                attention(layer * B, 0, True, True)
                with dve.Fori(1, B - 1) as b:
                    attention(layer * B + b, b, False, True)
                attention(layer * B + (B - 1), B - 1, False, False)
                dve.wait_ge(ff_in, layer * 64 + 64)
                dve.memset(xf[64:128, :, 0:1], 0.0).then_inc(s["xf0_dve"], 1)
                dve.wait_ge(s["xf0_dve"], after(layer + 1))
                layer_norm(PRE + layer, lambda c: xf[:, c, :], lambda c: xh[:, c, :],
                           lp[:, L_G:L_G + 1], lp[:, L_B:L_B + 1])
                p1 = (layer + 1) * B * GROUPS
                for b in range(B):
                    for j in range(3):
                        gated(layer, b, j)
                        if another and b == 3 and j == 0:
                            tables(p1, Q)
                        if another and b == 3 and j == 1:
                            rotation(p1, Q)
                    if b in (1, 2):
                        result(layer, b - 1)
                    if b == 2:
                        result(layer, b)
                        if another:
                            dve.wait_ge(wo_in, layer * 32 + 64)
                            shifted_lo_v((layer + 1) * B)
                            tables(p1, K)
                            rotation(p1, K)
                result(layer, 3)
                if another:
                    dve.memset(vb[0:WIN, :, 1, 0, :], 0.0)
                    place(p1, 0)
                    tables(p1 + 1, K)
                    rotation(p1 + 1, K)

            dve.wait_ge(wo_in, 32)
            shifted_lo_v(0)
            for kind in (K, Q):
                tables(0, kind)
                rotation(0, kind)
            dve.memset(vb[0:WIN, :, 1, 0, :], 0.0)
            place(0, 0)
            dve.memset(qbd[:, 1], 0.0)
            dve.memset(pts, 0.0)
            tables(1, K)
            rotation(1, K)
            with dve.Fori(0, DEPTH - 1) as layer:
                whole_layer(layer, True)
            whole_layer(DEPTH - 1, False)

            dve.wait_ge(s["fres_dve"], after(DEPTH * B))
            for b in range(B):
                dve.tensor_tensor(accv[:, b, :], accv[:, b, :], xv[:, b, :], ALU.add).then_inc(z["fin_sum"], 1)
            dve.wait_ge(z["fin_sum"], B)
            layer_norm(PRE + DEPTH, lambda c: accv[:, c, :], lambda c: xn2[:, c, :], 1.0, 0.0)
            for b in range(B):
                dve.wait_ge(z["gg_act"], b + 1)
                dve.scalar_tensor_tensor(gs[:, b, :], bank[b][:, :], col(P_GW), gs[:, b, :], ALU.mult, ALU.mult) \
                   .then_inc(z["gg_dve"], 1)
            def low_rank(b):
                dve.wait_ge(z["g1_mm"], b + 1)
                if b:
                    dve.wait_ge(z["z_mm"], b)
                dve.tensor_copy(g1s[0:LR, :], bank[6][0:LR, :]).then_inc(z["g1_copy"], 1)

            low_rank(0)
            for b in range(B):
                dve.wait_ge(z["kp_hi"], b + 1)
                dve.tensor_tensor(k_parts[b][64:128], bank[4][64:128, :], k_parts[b][64:128].bitcast(F32),
                                  ALU.subtract).then_inc(z["kp_lo"], 1)
                dve.wait_ge(z["z_mm"], b + 1)
                if b:
                    dve.wait_ge(z["abs_act"], b)
                dve.tensor_scalar(zb, bank[7][:, :], col(P_BGK), None, ALU.add).then_inc(z["z_copy"], 1)
                if b + 1 < B:
                    low_rank(b + 1)
                dve.wait_ge(z["z_copy"], b + 1)
                dve.wait_ge(z["gln_act"], b + 1)
                dve.scalar_tensor_tensor(egk[:, b, :], zb, 0.0, az[:, 0, :], ALU.min, ALU.subtract) \
                   .then_inc(z["gk_dve"], 1)
                dve.wait_ge(z["qp_hi"], b + 1)
                dve.scalar_tensor_tensor(q_parts[b][64:128], bank[5][64:128, :], Q_SCALE, q_parts[b][64:128].bitcast(F32),
                                         ALU.mult, ALU.subtract).then_inc(z["qp_lo"], 1)
                dve.wait_ge(z["eg_hi"], b + 1)
                dve.tensor_tensor(g_parts[b][64:128], egk[64:128, b, :], g_parts[b][64:128].bitcast(F32),
                                  ALU.subtract).then_inc(z["eg_lo"], 1)
            dve.wait_ge(z["lg_copy"], 1)
            for m in range(TILES):
                ins = dve.max(top8[:, m, :], lg[:, m, :])
            link(ins)
            for m in range(TILES):
                ins = dve.max_index(topi[:, 8 * m:8 * m + 8], top8[:, m, :], lg[:, m, :])
            link(ins)
            dve.tensor_copy(topf, topi[:, :].rearrange("p (m e) -> p m e", e=8))
            dve.tensor_tensor(gw12[:, 0, :], top8[:, :, 1], top8[:, :, 0], ALU.subtract).then_inc(z["route"], 1)
            dve.wait_ge(z["route"], 2)
            link(dve.tensor_scalar(gw12[:, 1, :], gw12[:, 0, :], 1.0, None, ALU.add))
            link(dve.reciprocal(gw12[:, 1, :], gw12[:, 1, :]))
            link(dve.tensor_tensor(gw12[:, 2, :], gw12[:, 0, :], gw12[:, 1, :], ALU.mult))
            dve.wait_ge(z["iota_pool"], 8)

            def of_expert(x):
                return x[:, :, None].to_broadcast([128, TILES, 8])

            each = iot[:, None, :].to_broadcast([128, TILES, 8])
            dve.tensor_tensor(gate, each, topf[:, :, 0:1].to_broadcast([128, TILES, 8]), ALU.is_equal)
            link(dve.tensor_tensor(gpart, each, topf[:, :, 1:2].to_broadcast([128, TILES, 8]), ALU.is_equal))
            dve.tensor_tensor(gate, gate, of_expert(gw12[:, 1, :]), ALU.mult)
            link(dve.tensor_tensor(gpart, gpart, of_expert(gw12[:, 2, :]), ALU.mult))
            link(dve.tensor_tensor(gate, gate, gpart, ALU.add))

            def kv(t):
                dve.wait_ge(z["rk_mm"], t + 1)
                if t >= 2:
                    dve.wait_ge(z["scan_dve"], t - 1)
                if t == 0:
                    dve.wait_ge(z["gv_copy"], B)
                dve.tensor_tensor(kvb[:, t % 2, :], bank[0][:, :], vt[:, t // DK, :], ALU.mult).then_inc(z["kv_dve"], 1)

            def scan(t):
                dve.wait_ge(z["rg_mm"], t + 1)
                dve.wait_ge(z["kv_dve"], t + 1)
                if t >= 2:
                    dve.wait_ge(z["qs_dve"], t - 1)
                dve.tensor_tensor_scan(sst[:, t % 2, :], bank[1][:, :], kvb[:, t % 2, :], 0.0, ALU.mult, ALU.add) \
                   .then_inc(z["scan_dve"], 1)

            def qs(t):
                dve.wait_ge(z["rq_mm"], t + 1)
                dve.wait_ge(z["scan_dve"], t + 1)
                if t >= 2:
                    dve.wait_ge(z["oadd"], t - 1)
                dve.tensor_tensor(tmp[:, t % 2, :], bank[2][:, :], sst[:, t % 2, :], ALU.mult).then_inc(z["qs_dve"], 1)

            def expert_sum(m):
                q, e = m // E, m % E
                dve.wait_ge(z["ey_mm"], m + 1)
                if e:
                    dve.wait_ge(z["ey_dve"], m)
                for j in range(4):
                    tile = 4 * q + j
                    part = bank[7][:, 128 * j:128 * j + 128]
                    if e:
                        ins = dve.scalar_tensor_tensor(otok[:, tile, :], part, gate[:, tile, e:e + 1], otok[:, tile, :],
                                                       ALU.mult, ALU.add)
                    else:
                        ins = dve.tensor_scalar(otok[:, tile, :], part, gate[:, tile, e:e + 1], None, ALU.mult)
                ins.then_inc(z["ey_dve"], 1)

            for t in range(B * DK + 2):
                if t < B * DK:
                    kv(t)
                if 1 <= t <= B * DK:
                    scan(t - 1)
                if t >= 2:
                    qs(t - 2)
                if t >= 4 and t % 2 == 0:
                    expert_sum(t // 2 - 2)
            expert_sum(B * E - 1)
            def gated_norm(b):
                dve.wait_ge(z["gr_act"], b + 1)
                link(dve.tensor_tensor(go[:, b, :], go[:, b, :], lrs[:, b % 2, :], ALU.mult))
                dve.tensor_tensor(go[:, b, :], go[:, b, :], gs[:, b, :], ALU.mult).then_inc(z["gn_dve"], 1)

            def add_gla(b):
                dve.wait_ge(z["go_mm"], b + 1)
                dve.tensor_tensor(accv[:, b, :], accv[:, b, :], bank[4 + b % 2][:, :], ALU.add).then_inc(z["x1_dve"], 1)

            for b in range(B):
                gated_norm(b)
                if b:
                    add_gla(b - 1)
            add_gla(B - 1)
            dve.wait_ge(z["ey_dve"], B * E)
            for b in range(B):
                dve.wait_ge(z["tok_mm"], b + 1)
                dve.tensor_tensor(otok[:, 4 * b:4 * b + 4, :], otok[:, 4 * b:4 * b + 4, :],
                                  bank[b][:, :].rearrange("p (m c) -> p m c", c=C), ALU.add).then_inc(z["out_dve"], 1)

        @block.gpsimd
        def _(pool):
            for n in pool_s.values():
                pool.sem_inc(n, 1)

            def shifted_lo(n, b):
                pool.wait_ge(s["xs_hi_act"], after(n + 1))
                pool.tensor_tensor(xs_lo[0:64, WIN:], xv[0:64, b, :], xs_hi[0:64, WIN:].bitcast(F32), ALU.subtract) \
                    .then_inc(s["xs_lo_pool"], 1)
                pool.wait_ge(s["xs_lo_pool"], after(2 * n + 1))
                pool.tensor_tensor(xs_lo[64:128, WIN + 1:], xv[64:128, b, 0:T - 1], xs_hi[64:128, WIN + 1:].bitcast(F32),
                                   ALU.subtract).then_inc(s["xs_lo_pool"], 1)
                pool.wait_ge(s["xs_lo_pool"], after(2 * n + 2))

            def square_sum(pi, kind):
                pool.wait_ge(s["sq_act"], after(pi * 2 + kind + 1))
                pool.tensor_tensor(sqs[:, kind, :], sqb[:, kind, 0, :], sqb[:, kind, 1, :], ALU.add).then_inc(s["sqadd"], 1)

            def rotate(pi, g, kind):
                pool.wait_ge(s["mul_dve"], after(pi * 2 + kind + 2))
                if kind == Q:
                    pool.wait_ge(s["placed_act"], after(pi))
                    pool.wait_ge(s["placed_dve"], after(pi))
                dst = qst if kind == Q else kb[:, g % 2, :, WIN:]
                pool.tensor_tensor(dst[:, 0, :], t4[:, 0, :], t4[:, 1, :], ALU.subtract)
                pool.tensor_tensor(dst[:, 1, :], t4[:, 2, :], t4[:, 3, :], ALU.add).then_inc(s["rotadd"], 1)

            def normalise(n, u):
                pool.wait_ge(s["rec_dve"], after(n * UNITS + u + 1))
                pool.tensor_tensor(probs[:, u % 2], probs[:, u % 2],
                                   rc[:, u % 2, :, None].to_broadcast([128, UW, 2 * WIN]), ALU.mult) \
                    .then_inc(s["norm_pool"], 1)

            def attention(n, b, ahead):
                for u in range(UNITS):
                    g = u // 2
                    pi = n * GROUPS + g
                    v_too = g + 1 < GROUPS or ahead
                    qk_too = g + 2 < GROUPS or ahead
                    if u % 2 == 0:
                        if v_too:
                            rotate(pi + 1, (g + 1) % GROUPS, Q)
                        normalise(n, u)
                        if qk_too:
                            square_sum(pi + 2, K)
                    else:
                        if qk_too:
                            square_sum(pi + 2, Q)
                        normalise(n, u)
                        if ahead and g + 3 == GROUPS:
                            shifted_lo(n + 1, b + 1)
                        if qk_too:
                            rotate(pi + 2, g % 2, K)

            def split_weights(layer):
                pool.wait_ge(wqkv_in, layer * 16 + 16)
                pool.wait_ge(s["v_mm"], after(layer * B * GROUPS * 2))

                def halves(w, p, a):
                    return w[:, p * INNER:(p + 1) * INNER].rearrange("p (g a h d) -> p g a h d", g=GROUPS, a=2, h=GH)[:, :, a]

                def whole(w, p, a):
                    return w[:, p * INNER:(p + 1) * INNER].rearrange("p (g h a d) -> p g h a d", g=GROUPS, a=2, h=GH)[:, :, :, a]

                for p in range(2):
                    for a in range(2):
                        pool.tensor_tensor(halves(wq_hi[:, :], p, a), whole(wraw, p, a),
                                           consts[:, 1:2, None, None].to_broadcast([128, GROUPS, GH, HALF]), ALU.mult)
                pool.tensor_tensor(wq_hi[:, 2 * INNER:], wraw[:, 2 * INNER:], consts[:, 1:2].to_broadcast([128, INNER]), ALU.mult) \
                    .then_inc(s["split_hi"], 1)
                pool.wait_ge(s["split_hi"], after(layer + 1))
                for p in range(2):
                    for a in range(2):
                        pool.tensor_tensor(halves(wq_lo[:, :], p, a), whole(wraw, p, a),
                                           halves(wq_hi[:, :].bitcast(F32), p, a), ALU.subtract)
                pool.tensor_tensor(wq_lo[:, 2 * INNER:], wraw[:, 2 * INNER:], wq_hi[:, 2 * INNER:].bitcast(F32),
                                   ALU.subtract).then_inc(s["split"], 1)

            def first_group(layer):
                p0 = layer * B * GROUPS
                shifted_lo(layer * B, 0)
                square_sum(p0, K)
                square_sum(p0, Q)
                rotate(p0, 0, K)
                rotate(p0, 0, Q)
                square_sum(p0 + 1, K)
                square_sum(p0 + 1, Q)
                rotate(p0 + 1, 1, K)

            def whole_layer(layer, another):
                with pool.Fori(0, B - 1) as b:
                    attention(layer * B + b, b, True)
                attention(layer * B + (B - 1), B - 1, False)
                if another:
                    split_weights(layer + 1)
                    first_group(layer + 1)

            pool.wait_ge(z["padded"], 1)
            split_weights(0)
            first_group(0)
            with pool.Fori(0, DEPTH - 1) as layer:
                whole_layer(layer, True)
            whole_layer(DEPTH - 1, False)

            pool.wait_ge(s["fres_dve"], after(DEPTH * B))
            for e in range(E):
                pool.memset(iot[:, e:e + 1], float(e)).then_inc(z["iota_pool"], 1)
            for t in range(B * DK):
                b = t // DK
                pool.wait_ge(z["qs_dve"], t + 1)
                if t % DK == 0:
                    pool.tensor_copy(go[:, b, :], tmp[:, t % 2, :]).then_inc(z["oadd"], 1)
                else:
                    pool.wait_ge(z["oadd"], t)
                    pool.tensor_tensor(go[:, b, :], go[:, b, :], tmp[:, t % 2, :], ALU.add).then_inc(z["oadd"], 1)


def rotary():
    import numpy as np
    f = np.float32
    half = np.arange(0, DH, 2, dtype=f)
    inv_freq = (1.0 / f(10000.0) ** (half / f(DH))).astype(f)
    t = np.arange(T, dtype=f)
    freqs = (t[:, None] * inv_freq[None, :]).astype(f)
    base = ((half + f(0.4 * DH)) / f(1.4 * DH)).astype(f)
    power = ((t - f(T // 2)) / f(WIN // 2)).astype(f)
    scale = (base[None, :] ** power[:, None]).astype(f)
    cos, sin = np.cos(freqs), np.sin(freqs)
    tabs = np.stack([cos * scale, sin * scale, cos * (1 / scale), sin * (1 / scale)]).astype(f)
    return np.ascontiguousarray(np.tile(tabs.transpose(2, 0, 1), (GH, 1, 1)))


def masks():
    import numpy as np
    q = np.arange(128)[:, None] % WIN
    k = np.arange(2 * WIN)[None, :]
    seen = np.where(k < WIN, q <= k, q >= k - WIN)
    m = np.where(seen, 0.0, -1e30)
    unit = np.tile(m, (1, UW))
    first = unit.copy()
    first[:, 0:WIN] = -1e30
    return np.concatenate([first, unit], axis=1).astype(np.float32)


def kernel(**inputs):
    import numpy as np
    import concourse.bacc as bacc
    from concourse.bass_utils import run_bass_kernel_spmd as run

    a = {k: np.ascontiguousarray(v) for k, v in inputs.items()}

    def column(v):
        v = v.reshape(-1)
        return np.concatenate([v, np.zeros(128 - v.size, v.dtype)])

    p0 = "L0_attn_"
    params = np.stack([column(v) for v in (
        a[p0 + "time_decay"], a[p0 + "time_first"], a[p0 + "ln1_g"], a[p0 + "ln1_b"], a[p0 + "ln2_g"], a[p0 + "ln2_b"],
        a[p0 + "mix_k"], a[p0 + "mix_v"], a[p0 + "mix_r"], a[p0 + "cmix_k"], a[p0 + "cmix_r"],
        np.tile(a["L1_attn_gw"], NH), np.tile(a["L1_attn_bgk2"], 2))], axis=1)
    f0 = "L0_ffn_"
    lparams = []
    for i in range(DEPTH):
        q, k, b1 = a[f0 + "q_scale"][i], a[f0 + "k_scale"][i], a[f0 + "b1"][i]
        cols = [np.tile(q[:HALF], GH), np.tile(q[HALF:], GH), np.tile(k[:HALF], GH), np.tile(k[HALF:], GH),
                a[f0 + "ln_g"][i], a[f0 + "ln_b"][i]]
        cols += [column(b1[s:s + n]) for s, n in FT] + [column(b1[FF + s:FF + s + n]) for s, n in FT]
        cols.append(a[f0 + "b2"][i])
        lparams.append(np.stack(cols, axis=1))
    arrays = {
        "x": a["L0_attn_x"], "params": params, "lparams": np.stack(lparams),
        "w_tk": a[p0 + "w_tk"], "w_tv": a[p0 + "w_tv"], "w_tr": a[p0 + "w_tr"], "w_ck": a[p0 + "w_ck"],
        "w_cv": a[p0 + "w_cv"], "w_cr": a[p0 + "w_cr"],
        "wqkv": a[f0 + "Wqkv"], "wo": a[f0 + "Wo"], "w1": a[f0 + "W1"], "w2": a[f0 + "W2"],
        "gwq": a["L1_attn_Wq"], "gwk": a["L1_attn_Wk"], "gwv": a["L1_attn_Wv"], "gwg1": a["L1_attn_Wgk1"],
        "gwg2": a["L1_attn_Wgk2"], "gwg": a["L1_attn_Wg"], "gwo": a["L1_attn_Wo"],
        "router_t": a["L1_ffn_router_w"].T, "ew1": a["L1_ffn_w1"], "ew2": a["L1_ffn_w2"],
        "rot": rotary(), "blocks": np.kron(np.eye(4), np.ones((32, 32))).astype(np.float32),
        "ident": np.eye(128, dtype=np.float32), "mask": masks(),
    }
    nc = bacc.Bacc("TRN2", target_bir_lowering=False, num_devices=1)
    data, args = {}, []
    for name, v in arrays.items():
        v = np.ascontiguousarray(v)
        data[f"in_{name}"] = v
        args.append(nc.dram_tensor(f"in_{name}", v.shape, mybir.dt.from_np(v.dtype), kind="ExternalInput").ap())
    out = nc.dram_tensor("out_0", (B, T, C), F32, kind="ExternalOutput").ap()
    program(nc, *args, out)
    r = run(nc, [data], core_ids=[0])
    return r.results[0]["out_0"]
```
